# Optimizing a Trainium2 kernel written in Bass

```python
import numpy as np
import jax
import jax.numpy as jnp

def _softmax(x, axis=-1):
    return jax.nn.softmax(x, axis=axis)

def _gelu(x):
    return jax.nn.gelu(x, approximate=True)

def _silu(x):
    return jax.nn.silu(x)

def _sigmoid(x):
    return jax.nn.sigmoid(x)

def _layernorm(x, axis=-1, eps=1e-05):
    m = jnp.mean(x, axis=axis, keepdims=True)
    v = jnp.var(x, axis=axis, keepdims=True)
    return (x - m) / jnp.sqrt(v + eps)

def _scatter_add(tgt, idx, src, axis=0):
    return tgt.at[idx].add(src)

def _segment_sum(src, seg, n):
    return jax.ops.segment_sum(src, seg, n)
kernel_name = 'mk_perceiver_d1_seqx_r8_8530ec'

def setup_inputs(seed: int=0):
    np.random.seed(seed)
    _w = jnp.asarray

    def _rec_inputs():
        import jax
        import jax.numpy as jnp
        _rk = jax.random.key(seed)
        x = -0.0005207 + 1.001 * jax.random.normal(jax.random.fold_in(_rk, 1), (1, 128, 512), jnp.float32)
        _lenS = 128 - jax.random.randint(jax.random.fold_in(_rk, 7), (1,), 0, max(1, 128 // 4) + 1, jnp.int32)
        _lenS2 = 2048 - jax.random.randint(jax.random.fold_in(_rk, 8), (1,), 0, max(1, 2048 // 4) + 1, jnp.int32)
        _ctx_4096P = jax.random.normal(jax.random.fold_in(_rk, 11), (1, 16, 512), jnp.float32)
        _ctx_4096c = jax.random.dirichlet(jax.random.fold_in(_rk, 511), 0.3 * jnp.ones((16,), jnp.float32), (1, 2048))
        _ctx_4096t = jnp.einsum('bsk,bkd->bsd', _ctx_4096c, _ctx_4096P)
        _ctx_4096t = _ctx_4096t * jax.lax.rsqrt(jnp.mean(jnp.square(_ctx_4096t)) + 1e-12) * 0.953939
        ctx_4096 = -0.00010331 + 0.999899 * (_ctx_4096t + 0.3 * jax.random.normal(jax.random.fold_in(_rk, 611), (1, 2048, 512), jnp.float32))
        return (x, ctx_4096)
    x, ctx_4096 = _rec_inputs()

    def _L0_xattn_setup():
        import jax, jax.numpy as jnp
        import numpy as np
        import math
        HIDDEN = 512
        N_HEADS = 32
        HEAD_DIM = 128
        N_KV_HEADS = 4
        N_GROUPS = N_HEADS // N_KV_HEADS
        key = jax.random.key(seed)
        ks = jax.random.split(key, 6)
        B, NL, S = (8, 64, 512)
        latents = jax.random.normal(ks[0], (B, NL, HIDDEN), dtype=jnp.float32)
        context = jax.random.normal(ks[1], (B, S, HIDDEN), dtype=jnp.float32)
        scale = 1.0 / math.sqrt(HIDDEN)
        Wq = jax.random.normal(ks[2], (HIDDEN, N_HEADS * HEAD_DIM), dtype=jnp.float32) * scale
        Wk = jax.random.normal(ks[3], (HIDDEN, N_KV_HEADS * HEAD_DIM), dtype=jnp.float32) * scale
        Wv = jax.random.normal(ks[4], (HIDDEN, N_KV_HEADS * HEAD_DIM), dtype=jnp.float32) * scale
        Wo = jax.random.normal(ks[5], (N_HEADS * HEAD_DIM, HIDDEN), dtype=jnp.float32) * scale
        return {'latents': latents, 'context': context, 'Wq': Wq, 'Wk': Wk, 'Wv': Wv, 'Wo': Wo}
    _L0_xattn_all = _L0_xattn_setup()
    _L0_xattn_in = {k: v for k, v in _L0_xattn_all.items() if k in ('Wq', 'Wk', 'Wv', 'Wo')}
    del _L0_xattn_all

    def _L0_attn_setup():
        import jax, jax.numpy as jnp
        import numpy as np
        H = 128
        P = 64
        G = 8
        N = 128
        CS = 128
        K = 4
        DIM = 512
        INTER = H * P
        CONV_DIM = INTER + 2 * G * N
        EPS = 1e-05

        def segment_sum(x):
            T = x.shape[-1]
            x = jnp.repeat(x[..., None], T, axis=-1)
            x = jnp.where(jnp.tril(jnp.ones((T, T), dtype=bool), -1), x, 0.0)
            s = jnp.cumsum(x, axis=-2)
            return jnp.where(jnp.tril(jnp.ones((T, T), dtype=bool), 0), s, -jnp.inf)
        key = jax.random.key(seed)
        ks = jax.random.split(key, 8)
        Bz, L = (1, 256)
        return {'hidden_states': jax.random.normal(ks[0], (Bz, L, DIM), jnp.float32), 'in_proj_w': jax.random.normal(ks[1], (INTER + CONV_DIM + H, DIM), jnp.float32) * 0.02, 'conv_w': jax.random.normal(ks[2], (CONV_DIM, 1, K), jnp.float32) * 0.2, 'conv_b': jnp.zeros((CONV_DIM,), jnp.float32), 'dt_bias': jnp.log(jnp.exp(jnp.linspace(0.001, 0.1, H)) - 1.0).astype(jnp.float32), 'A_log': jnp.log(jax.random.uniform(ks[3], (H,), jnp.float32, 1.0, 16.0)), 'D': jnp.ones((H,), jnp.float32), 'norm_w': jnp.ones((INTER,), jnp.float32), 'out_proj_w': jax.random.normal(ks[4], (DIM, INTER), jnp.float32) * 0.02}
    _L0_attn_all = _L0_attn_setup()
    _L0_attn_in = {k: v for k, v in _L0_attn_all.items() if k in ('in_proj_w', 'conv_w', 'conv_b', 'dt_bias', 'A_log', 'D', 'norm_w', 'out_proj_w')}
    del _L0_attn_all

    def _L0_ffn_setup():
        import jax, jax.numpy as jnp
        import numpy as np
        DIM = 512
        INTER = 1792
        SPARSITY = 32
        RANK = 16
        key = jax.random.key(seed)
        ks = jax.random.split(key, 5)
        B, T = (32, 1)
        x = jax.random.normal(ks[0], (B, T, DIM), dtype=jnp.float32)
        c1_w = jax.random.normal(ks[1], (RANK, DIM), dtype=jnp.float32) * (1.0 / np.sqrt(DIM))
        c2_w = jax.random.normal(ks[2], (INTER, RANK), dtype=jnp.float32) * (1.0 / np.sqrt(RANK))
        w1 = jax.random.normal(ks[3], (INTER, DIM), dtype=jnp.float32) * (1.0 / np.sqrt(DIM))
        w2t = jax.random.normal(ks[4], (INTER, DIM), dtype=jnp.float32) * (1.0 / np.sqrt(INTER))
        return {'x': x, 'c1_w': c1_w, 'c2_w': c2_w, 'w1': w1, 'w2t': w2t}
    _L0_ffn_all = _L0_ffn_setup()
    _L0_ffn_in = {k: v for k, v in _L0_ffn_all.items() if k in ('c1_w', 'c2_w', 'w1', 'w2t')}
    del _L0_ffn_all
    return {'x': x, 'ctx_4096': ctx_4096, 'L0_xattn_Wq': _L0_xattn_in['Wq'], 'L0_xattn_Wk': _L0_xattn_in['Wk'], 'L0_xattn_Wv': _L0_xattn_in['Wv'], 'L0_xattn_Wo': _L0_xattn_in['Wo'], 'L0_attn_in_proj_w': _L0_attn_in['in_proj_w'], 'L0_attn_conv_w': _L0_attn_in['conv_w'], 'L0_attn_conv_b': _L0_attn_in['conv_b'], 'L0_attn_dt_bias': _L0_attn_in['dt_bias'], 'L0_attn_A_log': _L0_attn_in['A_log'], 'L0_attn_D': _L0_attn_in['D'], 'L0_attn_norm_w': _L0_attn_in['norm_w'], 'L0_attn_out_proj_w': _L0_attn_in['out_proj_w'], 'L0_ffn_c1_w': _L0_ffn_in['c1_w'], 'L0_ffn_c2_w': _L0_ffn_in['c2_w'], 'L0_ffn_w1': _L0_ffn_in['w1'], 'L0_ffn_w2t': _L0_ffn_in['w2t']}

def reference(x, ctx_4096, L0_xattn_Wq, L0_xattn_Wk, L0_xattn_Wv, L0_xattn_Wo, L0_attn_in_proj_w, L0_attn_conv_w, L0_attn_conv_b, L0_attn_dt_bias, L0_attn_A_log, L0_attn_D, L0_attn_norm_w, L0_attn_out_proj_w, L0_ffn_c1_w, L0_ffn_c2_w, L0_ffn_w1, L0_ffn_w2t):
    import jax
    import jax.numpy as jnp

    def _L0_xattn_ref(latents, context, Wq, Wk, Wv, Wo):
        import jax, jax.numpy as jnp
        import numpy as np
        import math
        HIDDEN = 512
        N_HEADS = 32
        HEAD_DIM = 128
        N_KV_HEADS = 4
        N_GROUPS = N_HEADS // N_KV_HEADS
        b, q_len, _ = latents.shape
        kv_len = q_len + context.shape[1]
        hidden_states = jnp.concatenate([context, latents], axis=1)
        q = (latents @ Wq).reshape(b, q_len, N_KV_HEADS, N_GROUPS, HEAD_DIM)
        k = (hidden_states @ Wk).reshape(b, kv_len, N_KV_HEADS, HEAD_DIM)
        v = (hidden_states @ Wv).reshape(b, kv_len, N_KV_HEADS, HEAD_DIM)
        scale = 1.0 / math.sqrt(HEAD_DIM)
        scores = jnp.einsum('bqhgd,bkhd->bhgqk', q, k) * scale
        attn = jax.nn.softmax(scores.astype(jnp.float32), axis=-1).astype(q.dtype)
        out = jnp.einsum('bhgqk,bkhd->bqhgd', attn, v)
        out = out.reshape(b, q_len, N_HEADS * HEAD_DIM)
        return out @ Wo

    def _L0_attn_ref(hidden_states, in_proj_w, conv_w, conv_b, dt_bias, A_log, D, norm_w, out_proj_w):
        import jax, jax.numpy as jnp
        import numpy as np
        H = 128
        P = 64
        G = 8
        N = 128
        CS = 128
        K = 4
        DIM = 512
        INTER = H * P
        CONV_DIM = INTER + 2 * G * N
        EPS = 1e-05

        def segment_sum(x):
            T = x.shape[-1]
            x = jnp.repeat(x[..., None], T, axis=-1)
            x = jnp.where(jnp.tril(jnp.ones((T, T), dtype=bool), -1), x, 0.0)
            s = jnp.cumsum(x, axis=-2)
            return jnp.where(jnp.tril(jnp.ones((T, T), dtype=bool), 0), s, -jnp.inf)
        Bz, L, _ = hidden_states.shape
        proj = hidden_states @ in_proj_w.T
        gate = proj[..., :INTER]
        hBC = proj[..., INTER:INTER + CONV_DIM]
        dt = proj[..., INTER + CONV_DIM:]
        xc = jnp.transpose(hBC, (0, 2, 1))
        xc = jax.lax.conv_general_dilated(xc, conv_w, (1,), [(K - 1, 0)], dimension_numbers=('NCH', 'OIH', 'NCH'), feature_group_count=CONV_DIM) + conv_b[None, :, None]
        hBC = jax.nn.silu(jnp.transpose(xc, (0, 2, 1)))
        x = hBC[..., :INTER].reshape(Bz, L, H, P)
        Bm = hBC[..., INTER:INTER + G * N].reshape(Bz, L, G, N)
        Cm = hBC[..., INTER + G * N:].reshape(Bz, L, G, N)
        Bm = jnp.repeat(Bm, H // G, axis=2)
        Cm = jnp.repeat(Cm, H // G, axis=2)
        dt = jax.nn.softplus(dt + dt_bias)
        A = -jnp.exp(A_log)
        D_residual = D[None, None, :, None] * x
        A_dt = A[None, None, :] * dt
        x_dt = x * dt[..., None]
        Cn = L // CS
        Ac = jnp.transpose(A_dt.reshape(Bz, Cn, CS, H), (0, 3, 1, 2))
        xch = x_dt.reshape(Bz, Cn, CS, H, P)
        Bch = Bm.reshape(Bz, Cn, CS, H, N)
        Cch = Cm.reshape(Bz, Cn, CS, H, N)
        A_cumsum = jnp.cumsum(Ac, axis=-1)
        Lmat = jnp.exp(segment_sum(Ac))
        Gm = jnp.einsum('bclhn,bcshn->bclsh', Cch, Bch)
        M = Gm * jnp.transpose(Lmat, (0, 2, 3, 4, 1))
        Y_diag = jnp.einsum('bclsh,bcshp->bclhp', M, xch)
        decay_states = jnp.exp(A_cumsum[..., -1:] - A_cumsum)
        B_decay = Bch * jnp.transpose(decay_states, (0, 2, 3, 1))[..., None]
        states = jnp.einsum('bclhn,bclhp->bchpn', B_decay, xch)
        states_cat = jnp.concatenate([jnp.zeros_like(states[:, :1]), states], axis=1)
        A_last = jnp.pad(A_cumsum[..., -1], ((0, 0), (0, 0), (1, 0)))
        decay_chunk = jnp.exp(segment_sum(A_last))
        new_states = jnp.einsum('bhij,bjhpn->bihpn', decay_chunk, states_cat)
        states = new_states[:, :-1]
        state_decay = jnp.transpose(jnp.exp(A_cumsum), (0, 2, 3, 1))
        Y_off = jnp.einsum('bclhn,bchpn->bclhp', Cch, states) * state_decay[..., None]
        y = (Y_diag + Y_off).reshape(Bz, L, H, P) + D_residual
        y = y.reshape(Bz, L, INTER)
        var = jnp.mean(jnp.square(y), axis=-1, keepdims=True)
        y = y * jax.lax.rsqrt(var + EPS) * norm_w
        y = y * jax.nn.silu(gate)
        return y @ out_proj_w.T

    def _L0_ffn_ref(x, c1_w, c2_w, w1, w2t):
        import jax, jax.numpy as jnp
        import numpy as np
        DIM = 512
        INTER = 1792
        SPARSITY = 32
        RANK = 16
        B, T, M = x.shape
        xf = x.reshape(B * T, M)
        inter = xf @ c1_w.T @ c2_w.T
        n_blocks = INTER // SPARSITY
        blk = inter.reshape(B * T, n_blocks, SPARSITY)
        idx = jnp.argmax(blk, axis=-1) + jnp.arange(0, INTER, SPARSITY)
        w1_g = w1[idx]
        w2_g = w2t[idx]
        h = jax.nn.relu(jnp.einsum('bkm,bm->bk', w1_g, xf))
        out = jnp.einsum('bk,bkm->bm', h, w2_g)
        return out.reshape(B, T, M)
    x = x + _L0_xattn_ref(_layernorm(x, axis=-1), ctx_4096, L0_xattn_Wq, L0_xattn_Wk, L0_xattn_Wv, L0_xattn_Wo)
    x = x + _L0_attn_ref(_layernorm(x, axis=-1), L0_attn_in_proj_w, L0_attn_conv_w, L0_attn_conv_b, L0_attn_dt_bias, L0_attn_A_log, L0_attn_D, L0_attn_norm_w, L0_attn_out_proj_w)
    x = x + _L0_ffn_ref(_layernorm(x, axis=-1), L0_ffn_c1_w, L0_ffn_c2_w, L0_ffn_w1, L0_ffn_w2t)
    return x

_drawn_inputs = setup_inputs


def setup_inputs(seed=0):
    import zlib

    import numpy as np

    out = dict(_drawn_inputs(seed))
    spreads = {'L0_attn_conv_b': (0.0, 0.1), 'L0_attn_D': (1.0, 0.2), 'L0_attn_norm_w': (1.0, 0.2)}
    factors = {}
    for name, (base, spread) in spreads.items():
        noise = np.random.default_rng([zlib.crc32(name.encode()), seed]).standard_normal(out[name].shape)
        drawn = base * np.exp(spread * noise) if base else spread * noise
        out[name] = jnp.asarray(drawn.astype(out[name].dtype))
    for name, factor in factors.items():
        out[name] = (out[name] * factor).astype(out[name].dtype)
    return out
```

```python
from contextlib import ExitStack

import concourse.bass as bass
from concourse import mybir

F32 = mybir.dt.float32
F32R = mybir.dt.float32r
I32 = mybir.dt.int32
ALU = mybir.AluOpType
ACT = mybir.ActivationFunctionType
AX_X = mybir.AxisListType.X

P = 128
T = 128
DM = 512
NC = DM // P
BANK = 512
EPS = 1e-5

S_CTX = 2048
KV_LEN = S_CTX + T
NKT = KV_LEN // P
KVH = 4
HPK = 8
PAIRS = HPK // 2
NCHUNK = 5
UNITS = 9
SCALE = 128.0 ** -0.5

GROUPS = 8
HPG = 16
TPG = 8
NH = GROUPS * HPG
INTER = NH * 64
FF = 1792
BLK = 32
NBLK = FF // BLK
NFT = FF // P

RING = 4
SLOT = 2048
FFN0 = 52


def chunk_cols(c):
    return c * BANK, min((c + 1) * BANK, KV_LEN)


def build(nc, x, ctx_t, wq, wk, wv, wo, w_in, w_dt, w_out, conv_w, conv_b, dt_bias, a_log, d_skip,
          norm_w, c1, c2, w1, w2, w2_tail, out):
    with ExitStack() as ctx:
        def sem(name):
            return ctx.enter_context(nc.semaphore(name))

        def sbuf(stack, name, shape, dt=F32):
            return stack.enter_context(nc.sbuf_tensor(name, shape, dt))

        ring = [sbuf(ctx, f"ring{s}", [P, SLOT]) for s in range(RING)]
        res = sbuf(ctx, "res", [P, DM])
        normed = sbuf(ctx, "normed", [P, DM])
        norm_t = sbuf(ctx, "norm_t", [P, NC, T])
        ident = sbuf(ctx, "ident", [P, P])
        stats = sbuf(ctx, "stats", [P, 6])
        mean_var = sbuf(ctx, "mean_var", [P, 2])
        rstd = sbuf(ctx, "rstd", [P, 3])
        zeros1 = sbuf(ctx, "zeros1", [P, 1])

        k_all = sbuf(ctx, "k_all", [P, KVH, KV_LEN])
        with ExitStack() as st:
            v_all = sbuf(st, "v_all", [P, NKT, KVH * P])
            with ExitStack() as st1:
                wkv_hi = sbuf(st1, "wkv_hi", [P, 2, NC, DM], F32R)
                wkv_lo = sbuf(st1, "wkv_lo", [P, 2, NC, DM], F32R)
                ctx_hi = [sbuf(st1, f"ctx_hi{b}", [P, NC, BANK], F32R) for b in range(2)]
                ctx_lo = [sbuf(st1, f"ctx_lo{b}", [P, NC, BANK], F32R) for b in range(2)]
                lat_hi = sbuf(st1, "lat_hi", [P, NC, T], F32R)
                lat_lo = sbuf(st1, "lat_lo", [P, NC, T], F32R)
            with ExitStack() as st2:
                k_hi = sbuf(st2, "k_hi", [P, KV_LEN], F32R)
                k_lo = sbuf(st2, "k_lo", [P, KV_LEN], F32R)
                v_hi = sbuf(st2, "v_hi", [P, NKT, P], F32R)
                v_lo = sbuf(st2, "v_lo", [P, NKT, P], F32R)
                prob = [sbuf(st2, f"prob{b}", [P, 2, KV_LEN]) for b in range(2)]
                pt_hi = [sbuf(st2, f"pt_hi{b}", [P, 2, 2 * P], F32R) for b in range(3)]
                pt_lo = [sbuf(st2, f"pt_lo{b}", [P, 2, 2 * P], F32R) for b in range(3)]
                q_hi = [sbuf(st2, f"q_hi{b}", [P, 2 * P], F32R) for b in range(4)]
                q_lo = [sbuf(st2, f"q_lo{b}", [P, 2 * P], F32R) for b in range(4)]
                ones = sbuf(st2, "ones", [P, P])
                chunk_max = sbuf(st2, "chunk_max", [P, 2, 2, NCHUNK])
                neg_max = sbuf(st2, "neg_max", [P, 2, 2])
                row_sum = sbuf(st2, "row_sum", [P, 2, 2])
                row_inv = sbuf(st2, "row_inv", [P, 2, 2])
                diag = [sbuf(st2, f"diag{b}", [P, 2, P]) for b in range(2)]
                inv_bc = [sbuf(st2, f"inv_bc{b}", [P, 2 * P]) for b in range(2)]
        with ExitStack() as st3:
            w_dt_sb = sbuf(st3, "w_dt_sb", [P, NC, NH])
            cw = sbuf(st3, "cw", [P, 80, 4])
            cb = sbuf(st3, "cb", [P, 80])
            dskip = sbuf(st3, "dskip", [P, 64])
            nw = sbuf(st3, "nw", [P, 64])
            dtb = sbuf(st3, "dtb", [P, NH])
            alog = sbuf(st3, "alog", [P, NH])
            sp = [sbuf(st3, f"sp{i}", [P, NH]) for i in range(6)]
            dt = sbuf(st3, "dt", [P, NH])
            a_f = sbuf(st3, "a_f", [P, NH])
            a_hi = sbuf(st3, "a_hi", [P, NH], F32R)
            a_lo = sbuf(st3, "a_lo", [P, NH], F32R)
            upper = sbuf(st3, "upper", [P, P])
            upper_r = sbuf(st3, "upper_r", [P, P], F32R)
            causal = sbuf(st3, "causal", [P, P])
            raw = [sbuf(st3, f"raw{b}", [P, 4, T]) for b in range(2)]
            acc = [sbuf(st3, f"acc{b}", [P, 4, T]) for b in range(2)]
            bc = sbuf(st3, "bc", [P, 16, T])
            gm = sbuf(st3, "gm", [P, GROUPS, T])
            xc = [sbuf(st3, f"xc{b}", [P, TPG, T]) for b in range(2)]
            sg = [sbuf(st3, f"sg{b}", [P, TPG, T]) for b in range(2)]
            at_hi = sbuf(st3, "at_hi", [P, HPG, T], F32R)
            at_lo = sbuf(st3, "at_lo", [P, HPG, T], F32R)
            decay = [sbuf(st3, f"decay{b}", [P, HPG, T]) for b in range(2)]
            xdt = sbuf(st3, "xdt", [P, HPG, 64])
            yv = sbuf(st3, "yv", [P, TPG, T])
            ysq = sbuf(st3, "ysq", [P, TPG, T])
            sq_sum = sbuf(st3, "sq_sum", [P, TPG, T])
            sq_tok = sbuf(st3, "sq_tok", [P, T])
            ug = sbuf(st3, "ug", [P, TPG, T])
            ones_m = sbuf(st3, "ones_m", [P, 1])
            o_acc = sbuf(st3, "o_acc", [P, DM])
            c1_sb = sbuf(st3, "c1_sb", [P, NC, 16])
            c2_sb = sbuf(st3, "c2_sb", [16, FF])
            r1_sb = sbuf(st3, "r1_sb", [16, T])
            rank_i = sbuf(st3, "rank_i", [P, BLK], I32)
            rank = sbuf(st3, "rank", [P, BLK])
            bmax = sbuf(st3, "bmax", [P, NBLK])
            kmax = sbuf(st3, "kmax", [P, NBLK])
            final = sbuf(st3, "final", [P, DM])
            key = decay[0][:, 0:FF // T, :].rearrange("p a b -> p (a b)").rearrange("p (n j) -> p n j", j=BLK)
            hsel = decay[1][:, 0:FF // T, :].rearrange("p a b -> p (a b)")
            hsel_t = bc

        k_flat = k_all[:, :, :].rearrange("p k n -> p (k n)")
        ps = ctx.enter_context(nc.psum_tensor("ps", [P, 8, BANK], F32))

        landed = [sem(f"landed{s}") for s in range(RING)]
        freed = [sem(f"freed{s}") for s in range(RING)]
        x_in = sem("x_in")
        const_in = sem("const_in")
        ident_ok = sem("ident_ok")
        pool_const = sem("pool_const")
        ln = sem("ln")
        w_hi, w_lo, c_hi, c_lo = sem("w_hi"), sem("w_lo"), sem("c_hi"), sem("c_lo")
        kv_ps, k_ev, v_ev = sem("kv_ps"), sem("k_ev"), sem("v_ev")
        kh_ok, kl_ok, vh_ok, vl_ok = sem("kh_ok"), sem("kl_ok"), sem("vh_ok"), sem("vl_ok")
        q_ps, qh_ok, ql_ok = sem("q_ps"), sem("qh_ok"), sem("ql_ok")
        s_ps, s_ev, nm_ok, exp_ok = sem("s_ps"), sem("s_ev"), sem("nm_ok"), sem("exp_ok")
        t_ps, pth_ok, ptl_ok, pv_ps = sem("t_ps"), sem("pth_ok"), sem("ptl_ok"), sem("pv_ps")
        inv_ok, diag_ok, bc_ok, o_ok = sem("inv_ok"), sem("diag_ok"), sem("bc_ok"), sem("o_ok")
        wo_ps, res_ok = sem("wo_ps"), sem("res_ok")
        dt_ps, dts, a_ok = sem("dt_ps"), sem("dts"), sem("a_ok")
        proj_ps, proj_ev, taps, conv_ok, silu_ok = (sem("proj_ps"), sem("proj_ev"), sem("taps"),
                                                    sem("conv_ok"), sem("silu_ok"))
        gm_ps, gm_ok, at_ok, seg_ps, dec_ok, m_ok = (sem("gm_ps"), sem("gm_ok"), sem("at_ok"),
                                                     sem("seg_ps"), sem("dec_ok"), sem("m_ok"))
        xt_ps, xdt_ok, y_ps, y_ok, ysq_ok, sq_ok = (sem("xt_ps"), sem("xdt_ok"), sem("y_ps"),
                                                    sem("y_ok"), sem("ysq_ok"), sem("sq_ok"))
        ug_ok, op_ps, oacc_ok, var_s = sem("ug_ok"), sem("op_ps"), sem("oacc_ok"), sem("var_s")
        f_pe, f_dve, f_act, f_mask = sem("f_pe"), sem("f_dve"), sem("f_act"), sem("f_mask")
        stored = sem("stored")

        BEFORE = (4, 4, 7, 7)

        def stream(m):
            return m % RING, BEFORE[m % RING] + m // RING

        block = ctx.enter_context(nc.Block())

        @block.sync
        def _(sp):
            def load(slot, src, prior):
                if not (isinstance(prior, int) and prior == 0):
                    sp.wait_ge(freed[slot], prior)
                cols = src.shape[-1]
                sp.dma_start(ring[slot][:, 0:cols], src).then_inc(landed[slot], 16)

            load(0, wk, 0)
            load(2, ctx_t[0], 0)
            load(1, wv, 0)
            sp.dma_start(res[:], x).then_inc(x_in, 16)
            load(3, ctx_t[1], 0)
            load(0, ctx_t[2], 1)
            load(1, ctx_t[3], 1)
            load(2, wq[0], 1)
            load(3, wq[1], 1)
            load(0, wo[0], 2)
            load(1, wo[1], 2)
            for kv in range(1, KVH):
                load(2, wq[2 * kv], 1 + kv)
                load(3, wq[2 * kv + 1], 1 + kv)
            load(2, wo[2], 5)
            load(3, wo[3], 5)
            sp.wait_ge(o_ok, 4 * PAIRS + 1)
            sp.dma_start(w_dt_sb[:], w_dt).then_inc(const_in, 16)
            sp.dma_start(dtb[:], dt_bias.unsqueeze(0).to_broadcast([P, NH])).then_inc(const_in, 16)
            sp.dma_start(alog[:], a_log.unsqueeze(0).to_broadcast([P, NH])).then_inc(const_in, 16)
            sp.dma_start(cw[:], conv_w).then_inc(const_in, 16)
            sp.dma_start(cb[:], conv_b).then_inc(const_in, 16)
            sp.dma_start(nw[:], norm_w).then_inc(const_in, 16)
            for half in range(2):
                sp.dma_start(dskip[64 * half:64 * half + 64, :],
                             d_skip[half:half + 1, :].to_broadcast([64, 64])).then_inc(const_in, 16)
            sp.dma_start(c1_sb[:], c1).then_inc(const_in, 16)
            sp.dma_start(c2_sb[:], c2).then_inc(const_in, 16)
            load(0, wo[4], 3)
            load(1, wo[5], 3)
            load(2, wo[6], 6)
            load(3, wo[7], 6)
            for m in range(4):
                load(stream(m)[0], w_in[32 + m], stream(m)[1])
            for j in range(2):
                load(stream(4 + j)[0], w_in[16 + j], stream(4 + j)[1])
            for j in range(2):
                load(stream(6 + j)[0], w_in[j], stream(6 + j)[1])

            w_in_rows = w_in.rearrange("n p f -> (n p) f")
            w_out_rows = w_out.rearrange("n p f -> (n p) f")

            def step_loads(g, b, turn, last):
                j = 0
                if not last:
                    for first in (16 + 2 * (g + 1), 2 * (g + 1)):
                        for i in range(2):
                            m = 8 + 6 * b + j
                            load(m % RING, w_in_rows[bass.ds((first + i) * P, P), :],
                                 turn * 3 + (BEFORE[m % RING] + m // RING))
                            j += 1
                for i in range(2):
                    m = 8 + 6 * b + j
                    load(m % RING, w_out_rows[bass.ds((2 * g + i) * P, P), :],
                         turn * 3 + (BEFORE[m % RING] + m // RING))
                    j += 1

            with sp.Fori(0, 3) as turn:
                for b in range(2):
                    step_loads(turn * 2 + b, b, turn, False)
            step_loads(6, 0, 3, False)
            step_loads(7, 1, 3, True)
            for c in range(4):
                s, before = stream(FFN0 + c)
                load(s, w1[c], before)
            for c in range(4):
                s, before = stream(FFN0 + 4 + c)
                load(s, w2[c] if c < 3 else w2_tail[0], before)
            sp.wait_ge(f_dve, 6)
            sp.dma_start(out, final[:]).then_inc(stored, 16)
            sp.wait_ge(stored, 16)

        @block.gpsimd
        def _(pool):
            pool.memset(ident[:], 0.0).then_inc(ident_ok, 1)
            pool.wait_ge(ident_ok, 1)
            pool.affine_select(out=ident[:], in_=ident[:], compare_op=ALU.not_equal, fill=1.0, base=0,
                               pattern=[[-1, P]], channel_multiplier=1).then_inc(ident_ok, 1)
            pool.wait_ge(ident_ok, 2)
            pool.wait_ge(kv_ps, 34)
            pool.memset(ones[:], 1.0).then_inc(pool_const, 1)

            for n in range(KVH * PAIRS):
                pool.wait_ge(inv_ok, n + 1)
                for h in range(2):
                    i = pool.tensor_scalar(diag[n % 2][:, h, :], ident[:], row_inv[:, n % 2, h:h + 1], 1.0,
                                           ALU.mult, ALU.mult)
                i.then_inc(diag_ok, 1)

            pool.wait_ge(o_ok, 4 * PAIRS + 1)
            pool.memset(upper[:], 1.0).then_inc(pool_const, 1)
            pool.memset(causal[:], 1.0).then_inc(pool_const, 1)
            pool.memset(ones_m[:], 1.0).then_inc(pool_const, 1)
            pool.iota(rank_i[:], pattern=[[-1, BLK]], base=BLK, channel_multiplier=0).then_inc(pool_const, 1)
            pool.memset(sq_sum[:], 0.0).then_inc(sq_ok, 1)
            pool.wait_ge(pool_const, 5)
            pool.affine_select(out=upper[:], in_=upper[:], compare_op=ALU.is_gt, fill=0.0, base=0,
                               pattern=[[-1, P]], channel_multiplier=1).then_inc(pool_const, 1)
            pool.affine_select(out=causal[:], in_=causal[:], compare_op=ALU.is_ge, fill=0.0, base=0,
                               pattern=[[1, P]], channel_multiplier=-1).then_inc(pool_const, 1)

            def steps_a(g):
                for dst, src in ((at_hi, a_hi), (at_lo, a_lo)):
                    i = pool.affine_select(
                        out=dst[:], in_=src[:, g * HPG:g * HPG + HPG].bitcast(F32).unsqueeze(2).to_broadcast([P, HPG, T]),
                        compare_op=ALU.is_ge, fill=0.0, base=0, pattern=[[0, HPG], [1, T]],
                        channel_multiplier=-1)
                i.then_inc(at_ok, 1)

            def add_squares(g):
                pool.wait_ge(ysq_ok, g + 1)
                pool.wait_ge(sq_ok, g + 1)
                pool.tensor_tensor(sq_sum[:], sq_sum[:], ysq[:], ALU.add).then_inc(sq_ok, 1)

            pool.wait_ge(a_ok, 2)
            steps_a(0)
            for g in range(GROUPS - 1):
                pool.wait_ge(seg_ps, 2 * g + 2)
                steps_a(g + 1)
                add_squares(g)
            add_squares(GROUPS - 1)

        @block.scalar
        def _(act):
            copy = lambda dst, src: nc.scalar.activation(dst, src, ACT.Copy)

            def norm_sqrt(k):
                act.wait_ge(ln, 8 * k + 3)
                nc.scalar.activation(rstd[:, 1:2], rstd[:, 0:1], ACT.Sqrt).then_inc(ln, 1)

            def norm_evac(k, bank):
                act.wait_ge(ln, 8 * k + 7)
                copy(norm_t[:], ps[:, bank, :].rearrange("p (c t) -> p c t", c=NC)).then_inc(ln, 1)

            def split_w(i):
                act.wait_ge(landed[i], 16)
                copy(wkv_hi[:, i], ring[i][:].rearrange("p (c n) -> p c n", c=NC)).then_inc(w_hi, 1)

            def split_ctx(j):
                s, k = (2, 3, 0, 1)[j], (1, 1, 2, 2)[j]
                act.wait_ge(landed[s], 16 * k)
                if j >= 2:
                    act.wait_ge(kv_ps, 8 * (j - 1))
                copy(ctx_hi[j % 2][:], ring[s][:].rearrange("p (c n) -> p c n", c=NC)).then_inc(c_hi, 1)

            def v_out(j):
                for t in range(4):
                    act.wait_ge(kv_ps, 8 * j + 5 + t)
                    copy(v_all[:, 4 * j + t, :], ps[:, 4 + t, :]).then_inc(v_ev, 1)

            split_w(0)
            split_ctx(0)
            split_w(1)
            split_ctx(1)
            norm_sqrt(0)
            v_out(0)
            split_ctx(2)
            norm_evac(0, 2)
            act.wait_ge(ln, 8)
            copy(lat_hi[:], norm_t[:]).then_inc(c_hi, 1)
            v_out(1)
            split_ctx(3)
            v_out(2)
            v_out(3)
            act.wait_ge(kv_ps, 34)
            copy(v_all[:, 16, :], ps[:, 1, :]).then_inc(v_ev, 1)

            def k_split(kv):
                copy(k_hi[:], k_flat[:, bass.ds(kv * KV_LEN, KV_LEN)]).then_inc(kh_ok, 1)

            def v_split(kv, half):
                a, b = ((0, 8), (8, NKT))[half]
                copy(v_hi[:, a:b, :], v_all[:, a:b, bass.ds(kv * P, P)]).then_inc(vh_ok, 1)

            def q_split(m, slot, bank):
                act.wait_ge(q_ps, m + 1)
                copy(q_hi[slot][:], ps[:, bank, 0:2 * P]).then_inc(qh_ok, 1)

            def soft_exp(m, b, h):
                act.wait_ge(nm_ok, 2 * m + h + 1)
                nc.scalar.activation(prob[b][:, h, :], prob[b][:, h, :], ACT.Exp, bias=neg_max[:, b, h:h + 1],
                                     accum_out=row_sum[:, b, h:h + 1]).then_inc(exp_ok, 1)

            def pt_split(unit, u, bank):
                w = 2 if u < 8 else 1
                act.wait_ge(t_ps, unit + 1)
                copy(pt_hi[u % 3][:, 0:w, :],
                     ps[:, bank, 0:w * 256].rearrange("p (w n) -> p w n", w=w)).then_inc(pth_ok, 1)

            def attn_step(kv, p, last):
                n = kv * PAIRS + p
                b = p % 2
                turn = p == PAIRS - 1
                for u in range(UNITS):
                    if turn and not last and u == 0:
                        act.wait_ge(s_ps, 10 * n + 10)
                        k_split(kv + 1)
                    tgt = u + 2
                    if tgt < UNITS:
                        act.wait_ge(pv_ps, 10 * n + u + 1)
                        pt_split(9 * n + tgt, tgt, 4 + (9 * p + tgt) % 2)
                    elif not turn:
                        act.wait_ge(pv_ps, 10 * n + u + 1)
                        pt_split(9 * (n + 1) + tgt - UNITS, tgt - UNITS, 4 + (9 * p + tgt) % 2)
                    if not turn:
                        if u == 2:
                            soft_exp(n + 1, 1 - b, 0)
                        if u == 4:
                            soft_exp(n + 1, 1 - b, 1)
                        if u == 5 and not (last and p >= 2):
                            q_split(n + 2, (p + 2) % 4, 6 + (1 - b))
                    elif not last:
                        if u == 5:
                            act.wait_ge(pv_ps, 10 * n + 9)
                            v_split(kv + 1, 0)
                        if u == 6:
                            soft_exp(n + 1, 1 - b, 0)
                        if u == 8:
                            soft_exp(n + 1, 1 - b, 1)
                act.wait_ge(pv_ps, 10 * n + 10)
                copy(inv_bc[b][:], ps[:, 6 + b, 256:512]).then_inc(bc_ok, 1)
                if turn and not last:
                    v_split(kv + 1, 1)
                    q_split(n + 2, (p + 2) % 4, 6 + (1 - b))
                    for i in range(2):
                        act.wait_ge(pv_ps, 10 * n + 8 + i)
                        pt_split(9 * (n + 1) + i, i, 4 + (9 * (p + 1) + i) % 2)

            act.wait_ge(k_ev, 17)
            act.wait_ge(kv_ps, 34)
            k_split(0)
            act.wait_ge(v_ev, 17)
            v_split(0, 0)
            v_split(0, 1)
            q_split(0, 0, 7)
            q_split(1, 1, 6)
            soft_exp(0, 0, 0)
            soft_exp(0, 0, 1)
            pt_split(0, 0, 4)
            pt_split(1, 1, 5)
            with act.Fori(0, KVH - 1) as kv:
                for p in range(PAIRS):
                    attn_step(kv, p, False)
            for p in range(PAIRS):
                attn_step(KVH - 1, p, True)

            norm_sqrt(1)
            norm_evac(1, 7)
            act.wait_ge(dts, 2)
            nc.scalar.activation(sp[2][:], sp[1][:], ACT.Exp, scale=-1.0).then_inc(dts, 1)
            act.wait_ge(const_in, 160)
            nc.scalar.activation(sp[5][:], alog[:], ACT.Exp).then_inc(a_ok, 1)

            def raw_out(q, k, bank):
                act.wait_ge(proj_ps, q + 1)
                if not (isinstance(k, int) and k < 2):
                    act.wait_ge(taps, k - 1)
                copy(raw[bank][:], ps[:, bank, :].rearrange("p (c t) -> p c t", c=4)).then_inc(proj_ev, 1)

            def conv_silu(k, slot, dst):
                act.wait_ge(taps, k + 1)
                nc.scalar.activation(dst, acc[slot][:], ACT.Silu).then_inc(silu_ok, 1)

            def gate_out(q, bank, dst):
                act.wait_ge(proj_ps, q + 1)
                nc.scalar.activation(dst, ps[:, bank, :].rearrange("p (c t) -> p c t", c=4),
                                     ACT.Silu).then_inc(proj_ev, 1)

            def decay_exp(g, b, half):
                act.wait_ge(seg_ps, 2 * g + half + 1)
                nc.scalar.activation(decay[b][:, 8 * half:8 * half + 8, :],
                                     ps[:, 2:4, :].rearrange("p a (h t) -> p (a h) t", t=T),
                                     ACT.Exp).then_inc(dec_ok, 1)

            def squares(g):
                act.wait_ge(y_ok, g + 1)
                act.wait_ge(sq_ok, g + 1)
                nc.scalar.activation(ysq[:], yv[:], ACT.Square).then_inc(ysq_ok, 1)

            for k in range(4):
                raw_out(k, k, k % 2)
                if k:
                    conv_silu(k - 1, (k - 1) % 2, bc[:, 4 * (k - 1):4 * k, :])
            raw_out(4, 4, 0)
            conv_silu(3, 1, bc[:, 12:16, :])
            raw_out(5, 5, 1)
            conv_silu(4, 0, xc[0][:, 0:4, :])
            conv_silu(5, 1, xc[0][:, 4:8, :])
            decay_exp(0, 0, 0)
            gate_out(6, 0, sg[0][:, 0:4, :])
            gate_out(7, 1, sg[0][:, 4:8, :])
            decay_exp(0, 0, 1)

            def mamba_step(g, b):
                q, k, o = 4 * g + 8, 2 * g + 6, 1 - b
                decay_exp(g + 1, o, 0)
                raw_out(q, k, 0)
                decay_exp(g + 1, o, 1)
                squares(g)
                raw_out(q + 1, k + 1, 1)
                conv_silu(k, 0, xc[o][:, 0:4, :])
                gate_out(q + 2, 0, sg[o][:, 0:4, :])
                gate_out(q + 3, 1, sg[o][:, 4:8, :])
                conv_silu(k + 1, 1, xc[o][:, 4:8, :])

            with act.Fori(0, 3) as turn:
                for b in range(2):
                    mamba_step(turn * 2 + b, b)
            mamba_step(6, 0)
            squares(7)
            act.wait_ge(var_s, 3)
            nc.scalar.activation(rstd[:, 1:2], rstd[:, 0:1], ACT.Sqrt).then_inc(var_s, 1)

            norm_sqrt(2)
            norm_evac(2, 7)
            act.wait_ge(f_pe, 1)
            copy(r1_sb[:], ps[0:16, 6, 0:T]).then_inc(f_act, 1)
            for i in range(4):
                w = min(4, NFT - 4 * i)
                act.wait_ge(f_pe, 4 + i)
                copy(hsel_t[:, 4 * i:4 * i + w, :],
                     ps[:, i, 0:w * T].rearrange("p (c t) -> p c t", t=T)).then_inc(f_act, 1)

        @block.vector
        def _(dve):
            sub = lambda dst, a, hi: nc.vector.tensor_tensor(dst, a, hi, ALU.subtract)

            def norm(k):
                nc.vector.bn_stats(stats[:], res[:]).then_inc(ln, 1)
                dve.wait_ge(ln, 8 * k + 1)
                nc.vector.bn_aggr(mean_var[:], stats[:]).then_inc(ln, 1)
                dve.wait_ge(ln, 8 * k + 2)
                nc.vector.tensor_scalar(rstd[:, 0:1], mean_var[:, 1:2], EPS, None, ALU.add).then_inc(ln, 1)
                dve.wait_ge(ln, 8 * k + 4)
                nc.vector.reciprocal(rstd[:, 2:3], rstd[:, 1:2]).then_inc(ln, 1)
                dve.wait_ge(ln, 8 * k + 5)
                nc.vector.tensor_scalar(normed[:], res[:], mean_var[:, 0:1], rstd[:, 2:3],
                                        ALU.subtract, ALU.mult).then_inc(ln, 1)

            def split_w(i):
                dve.wait_ge(w_hi, i + 1)
                sub(wkv_lo[:, i], ring[i][:].rearrange("p (c n) -> p c n", c=NC),
                    wkv_hi[:, i].bitcast(F32)).then_inc(w_lo, 1)
                dve.wait_ge(w_lo, i + 1)
                dve.sem_inc(freed[i], 1)

            def split_ctx(j):
                s = (2, 3, 0, 1)[j]
                dve.wait_ge(c_hi, j + 1 + (j == 3))
                if j >= 2:
                    dve.wait_ge(kv_ps, 8 * (j - 1))
                sub(ctx_lo[j % 2][:], ring[s][:].rearrange("p (c n) -> p c n", c=NC),
                    ctx_hi[j % 2][:].bitcast(F32)).then_inc(c_lo, 1)
                dve.wait_ge(c_lo, j + 1 + (j == 3))
                dve.sem_inc(freed[s], 1)

            def k_out(j):
                for kv in range(KVH):
                    dve.wait_ge(kv_ps, 8 * j + 1 + kv)
                    nc.vector.tensor_copy(k_all[:, kv, BANK * j:BANK * j + BANK], ps[:, kv, :]).then_inc(k_ev, 1)

            nc.vector.memset(zeros1[:], 0.0).then_inc(o_ok, 1)
            split_w(0)
            split_ctx(0)
            split_w(1)
            split_ctx(1)
            dve.wait_ge(x_in, 16)
            norm(0)
            k_out(0)
            split_ctx(2)
            k_out(1)
            dve.wait_ge(c_hi, 4)
            sub(lat_lo[:], norm_t[:], lat_hi[:].bitcast(F32)).then_inc(c_lo, 1)
            split_ctx(3)
            k_out(2)
            k_out(3)
            dve.wait_ge(kv_ps, 33)
            nc.vector.tensor_copy(k_all[:, :, S_CTX:KV_LEN],
                                  ps[:, 0, :].rearrange("p (k t) -> p k t", k=KVH)).then_inc(k_ev, 1)

            def k_split(kv):
                dve.wait_ge(kh_ok, kv + 1)
                sub(k_lo[:], k_flat[:, bass.ds(kv * KV_LEN, KV_LEN)], k_hi[:].bitcast(F32)).then_inc(kl_ok, 1)

            def v_split(kv, half):
                a, b = ((0, 8), (8, NKT))[half]
                dve.wait_ge(vh_ok, 2 * kv + half + 1)
                sub(v_lo[:, a:b, :], v_all[:, a:b, bass.ds(kv * P, P)],
                    v_hi[:, a:b, :].bitcast(F32)).then_inc(vl_ok, 1)

            def q_split(m, slot, bank):
                dve.wait_ge(qh_ok, m + 1)
                sub(q_lo[slot][:], ps[:, bank, 0:2 * P], q_hi[slot][:].bitcast(F32)).then_inc(ql_ok, 1)

            def scores_out(m, b, c):
                h, i = c // NCHUNK, c % NCHUNK
                lo, hi = chunk_cols(i)
                dve.wait_ge(s_ps, 10 * m + c + 1)
                nc.vector.tensor_scalar(prob[b][:, h, lo:hi], ps[:, (2 * (b % 2) + c) % 4, 0:hi - lo], SCALE, None,
                                        ALU.mult, ALU.max, accum_out=chunk_max[:, b, h, i:i + 1]).then_inc(s_ev, 1)
                if i == NCHUNK - 1:
                    dve.wait_ge(s_ev, 10 * m + c + 1)
                    nc.vector.tensor_reduce(neg_max[:, b, h:h + 1], chunk_max[:, b, h, :], AX_X, ALU.max,
                                            negate=True).then_inc(nm_ok, 1)

            def invert(m, b):
                dve.wait_ge(exp_ok, 2 * m + 2)
                nc.vector.reciprocal(row_inv[:, b, :], row_sum[:, b, :]).then_inc(inv_ok, 1)

            def pt_split(unit, u, bank):
                w = 2 if u < 8 else 1
                dve.wait_ge(pth_ok, unit + 1)
                sub(pt_lo[u % 3][:, 0:w, :], ps[:, bank, 0:w * 256].rearrange("p (w n) -> p w n", w=w),
                    pt_hi[u % 3][:, 0:w, :].bitcast(F32)).then_inc(ptl_ok, 1)

            def attn_step(kv, p, last):
                n = kv * PAIRS + p
                b = p % 2
                turn = p == PAIRS - 1
                for u in range(UNITS):
                    if turn and not last and u == 0:
                        k_split(kv + 1)
                    tgt = u + 2
                    if tgt < UNITS:
                        pt_split(9 * n + tgt, tgt, 4 + (9 * p + tgt) % 2)
                    elif not turn:
                        if u == 7:
                            invert(n + 1, 1 - b)
                        pt_split(9 * (n + 1) + tgt - UNITS, tgt - UNITS, 4 + (9 * p + tgt) % 2)
                    if not turn:
                        if u < 5:
                            scores_out(n + 1, 1 - b, 2 * u)
                            scores_out(n + 1, 1 - b, 2 * u + 1)
                        if u == 5 and not (last and p >= 2):
                            q_split(n + 2, (p + 2) % 4, 6 + (1 - b))
                    elif not last and u >= 4:
                        scores_out(n + 1, 1 - b, 2 * u - 8)
                        scores_out(n + 1, 1 - b, 2 * u - 7)
                        if u == 5:
                            v_split(kv + 1, 0)
                dve.wait_ge(bc_ok, n + 1)
                nc.vector.tensor_tensor(k_flat[:, bass.ds(kv * KV_LEN + 256 * p, 256)],
                                        ps[:, 6 + b, 0:256], inv_bc[b][:], ALU.mult).then_inc(o_ok, 1)
                if turn and not last:
                    v_split(kv + 1, 1)
                    q_split(n + 2, (p + 2) % 4, 6 + (1 - b))
                    invert(n + 1, 1 - b)
                    for i in range(2):
                        pt_split(9 * (n + 1) + i, i, 4 + (9 * (p + 1) + i) % 2)

            k_split(0)
            v_split(0, 0)
            v_split(0, 1)
            q_split(0, 0, 7)
            q_split(1, 1, 6)
            for c in range(10):
                scores_out(0, 0, c)
            invert(0, 0)
            pt_split(0, 0, 4)
            pt_split(1, 1, 5)
            with dve.Fori(0, KVH - 1) as kv:
                for p in range(PAIRS):
                    attn_step(kv, p, False)
            for p in range(PAIRS):
                attn_step(KVH - 1, p, True)

            dve.wait_ge(wo_ps, 1)
            nc.vector.tensor_tensor(res[:], res[:], ps[:, 0, :], ALU.add).then_inc(res_ok, 1)
            dve.wait_ge(res_ok, 1)
            norm(1)
            dve.wait_ge(pool_const, 7)
            nc.vector.tensor_copy(upper_r[:], upper[:]).then_inc(pool_const, 1)
            nc.vector.tensor_copy(rank[:], rank_i[:]).then_inc(pool_const, 1)
            nc.vector.memset(o_acc[:], 0.0).then_inc(oacc_ok, 1)

            dve.wait_ge(dt_ps, 1)
            dve.wait_ge(const_in, 160)
            z, zabs, u_, s_, s2, ea = sp
            nc.vector.tensor_tensor(z[:], ps[:, 6, 0:NH], dtb[:], ALU.add).then_inc(dts, 1)
            dve.wait_ge(dts, 1)
            nc.vector.scalar_tensor_tensor(zabs[:], z[:], -1.0, z[:], ALU.mult, ALU.max).then_inc(dts, 1)
            dve.wait_ge(dts, 3)
            nc.vector.tensor_scalar(zabs[:], u_[:], 2.0, None, ALU.add).then_inc(dts, 1)
            dve.wait_ge(dts, 4)
            nc.vector.reciprocal(s2[:], zabs[:]).then_inc(dts, 1)
            dve.wait_ge(dts, 5)
            nc.vector.tensor_tensor(s_[:], u_[:], s2[:], ALU.mult).then_inc(dts, 1)
            dve.wait_ge(dts, 6)
            nc.vector.tensor_tensor(s2[:], s_[:], s_[:], ALU.mult).then_inc(dts, 1)
            dve.wait_ge(dts, 7)
            nc.vector.tensor_scalar(zabs[:], s2[:], 1.0 / 17, None, ALU.mult).then_inc(dts, 1)
            k = 8
            for odd in (15, 13, 11, 9, 7, 5, 3):
                dve.wait_ge(dts, k)
                nc.vector.scalar_tensor_tensor(zabs[:], zabs[:], 1.0 / odd, s2[:], ALU.add,
                                               ALU.mult).then_inc(dts, 1)
                k += 1
            dve.wait_ge(dts, k)
            nc.vector.scalar_tensor_tensor(zabs[:], zabs[:], 1.0, s_[:], ALU.add, ALU.mult).then_inc(dts, 1)
            dve.wait_ge(dts, k + 1)
            nc.vector.tensor_scalar(z[:], z[:], 0.0, None, ALU.max).then_inc(dts, 1)
            dve.wait_ge(dts, k + 2)
            nc.vector.scalar_tensor_tensor(dt[:], zabs[:], 2.0, z[:], ALU.mult, ALU.add).then_inc(dts, 1)
            dve.wait_ge(dts, k + 3)
            dve.wait_ge(a_ok, 1)
            nc.vector.scalar_tensor_tensor(a_f[:], ea[:], -1.0, dt[:], ALU.mult, ALU.mult).then_inc(dts, 1)
            dve.wait_ge(dts, k + 4)
            nc.vector.tensor_copy(a_hi[:], a_f[:]).then_inc(dts, 1)
            dve.wait_ge(dts, k + 5)
            sub(a_lo[:], a_f[:], a_hi[:].bitcast(F32)).then_inc(a_ok, 1)

            def conv(k, slot, tile):
                r, a = raw[slot], acc[slot]
                for i in range(4):
                    ins = nc.vector.tensor_scalar(a[:, i, :], r[:, i, :], cw[:, bass.ds(tile + i, 1), 3:4].rearrange("p a b -> p (a b)"),
                                                  cb[:, bass.ds(tile + i, 1)], ALU.mult, ALU.add)
                    ins.then_inc(conv_ok, 1)
                for back in range(1, 4):
                    for i in range(4):
                        dve.wait_ge(conv_ok, 16 * k + 4 * (back - 1) + i + 1)
                        ins = nc.vector.scalar_tensor_tensor(
                            a[:, i, back:], r[:, i, 0:T - back],
                            cw[:, bass.ds(tile + i, 1), 3 - back:4 - back].rearrange("p a b -> p (a b)"),
                            a[:, i, back:], ALU.mult, ALU.add)
                        ins.then_inc(conv_ok, 1)
                dve.wait_ge(conv_ok, 16 * k + 16)
                dve.sem_inc(taps, 1)

            def taps_of(q, k, slot, tile):
                dve.wait_ge(proj_ev, q + 1)
                if not (isinstance(k, int) and k < 2):
                    dve.wait_ge(silu_ok, k - 1)
                conv(k, slot, tile)

            def mask_decay(g, b, half):
                dve.wait_ge(dec_ok, 2 * g + half + 1)
                d = decay[b][:, 8 * half:8 * half + 8, :]
                nc.vector.tensor_tensor(d, d, gm[:, bass.ds(g, 1), :].to_broadcast([P, 8, T]),
                                        ALU.mult).then_inc(m_ok, 1)

            def x_times_dt(g):
                dve.wait_ge(xt_ps, g + 1)
                nc.vector.tensor_tensor(xdt[:], ps[:, 4:6, :].rearrange("p a (h c) -> p (a h) c", c=64),
                                        dt[:, bass.ds(g * HPG, HPG)].unsqueeze(2).to_broadcast([P, HPG, 64]),
                                        ALU.mult).then_inc(xdt_ok, 1)

            def skip_add(g, b):
                dve.wait_ge(y_ps, g + 1)
                for t in range(TPG):
                    ins = nc.vector.scalar_tensor_tensor(
                        yv[:, t, :], xc[b][:, t, :], dskip[:, bass.ds(g * TPG + t, 1)],
                        ps[:, 4 + t // 4, (t % 4) * T:(t % 4 + 1) * T], ALU.mult, ALU.add)
                ins.then_inc(y_ok, 1)
                dve.wait_ge(y_ok, g + 1)
                for t in range(TPG):
                    ins = nc.vector.scalar_tensor_tensor(
                        ug[:, t, :], yv[:, t, :], nw[:, bass.ds(g * TPG + t, 1)], sg[b][:, t, :],
                        ALU.mult, ALU.mult)
                ins.then_inc(ug_ok, 1)

            def add_out(g):
                dve.wait_ge(op_ps, g + 1)
                dve.wait_ge(oacc_ok, g + 1)
                nc.vector.tensor_tensor(o_acc[:], o_acc[:], ps[:, 6, :], ALU.add).then_inc(oacc_ok, 1)

            for k in range(4):
                taps_of(k, k, k % 2, 64 + 4 * k)
            taps_of(4, 4, 0, 0)
            taps_of(5, 5, 1, 4)
            dve.wait_ge(gm_ps, 1)
            nc.vector.tensor_tensor(gm[:], ps[:, 4:6, :].rearrange("p a (g t) -> p (a g) t", t=T),
                                    causal[:].unsqueeze(1).to_broadcast([P, GROUPS, T]),
                                    ALU.mult).then_inc(gm_ok, 1)
            dve.wait_ge(gm_ok, 1)
            mask_decay(0, 0, 0)
            mask_decay(0, 0, 1)

            def mamba_step(g, b):
                q, k, o = 4 * g + 8, 2 * g + 6, 1 - b
                x_times_dt(g)
                mask_decay(g + 1, o, 0)
                taps_of(q, k, 0, 8 * g + 8)
                mask_decay(g + 1, o, 1)
                skip_add(g, b)
                taps_of(q + 1, k + 1, 1, 8 * g + 12)
                add_out(g)

            with dve.Fori(0, 3) as turn:
                for b in range(2):
                    mamba_step(turn * 2 + b, b)
            mamba_step(6, 0)
            x_times_dt(7)
            skip_add(7, 1)
            dve.wait_ge(sq_ok, GROUPS + 1)
            nc.vector.tensor_reduce(sq_tok[:], sq_sum[:].rearrange("p c t -> p t c"), AX_X,
                                    ALU.add).then_inc(var_s, 1)
            dve.wait_ge(var_s, 2)
            nc.vector.tensor_scalar(rstd[:, 0:1], ps[:, 7, 0:1], 1.0 / INTER, EPS, ALU.mult,
                                    ALU.add).then_inc(var_s, 1)
            add_out(7)
            dve.wait_ge(var_s, 4)
            nc.vector.reciprocal(rstd[:, 2:3], rstd[:, 1:2]).then_inc(var_s, 1)
            dve.wait_ge(var_s, 5)
            dve.wait_ge(oacc_ok, GROUPS + 1)
            nc.vector.scalar_tensor_tensor(res[:], o_acc[:], rstd[:, 2:3], res[:], ALU.mult,
                                           ALU.add).then_inc(res_ok, 1)
            dve.wait_ge(res_ok, 2)

            norm(2)
            inter = ps[:, 0:4, :].rearrange("p a n -> p (a n)")[:, 0:FF]
            blocks = inter.rearrange("p (n j) -> p n j", j=BLK)
            dve.wait_ge(f_pe, 2)
            nc.vector.tensor_reduce(bmax[:], blocks, AX_X, ALU.max).then_inc(f_mask, 1)
            dve.wait_ge(f_mask, 1)
            nc.vector.tensor_tensor(key, blocks, bmax[:].unsqueeze(2).to_broadcast([P, NBLK, BLK]),
                                    ALU.is_equal).then_inc(f_mask, 1)
            dve.wait_ge(f_mask, 2)
            nc.vector.tensor_tensor(key, key, rank[:].unsqueeze(1).to_broadcast([P, NBLK, BLK]),
                                    ALU.mult).then_inc(f_mask, 1)
            dve.wait_ge(f_mask, 3)
            nc.vector.tensor_reduce(kmax[:], key, AX_X, ALU.max).then_inc(f_mask, 1)
            dve.wait_ge(f_mask, 4)
            nc.vector.tensor_tensor(key, key, kmax[:].unsqueeze(2).to_broadcast([P, NBLK, BLK]),
                                    ALU.is_equal).then_inc(f_mask, 1)
            dve.wait_ge(f_mask, 5)
            dve.wait_ge(f_pe, 3)
            key_flat = decay[0][:, 0:FF // T, :].rearrange("p a b -> p (a b)")
            for i in range(4):
                lo, hi = i * BANK, min(i * BANK + BANK, FF)
                nc.vector.scalar_tensor_tensor(hsel[:, lo:hi], ps[:, 4 + i, 0:hi - lo], 0.0, key_flat[:, lo:hi],
                                               ALU.max, ALU.mult).then_inc(f_dve, 1)
            dve.wait_ge(f_pe, 8)
            nc.vector.tensor_tensor(final[:], res[:], ps[:, 4, :], ALU.add).then_inc(f_dve, 2)

        @block.tensor
        def _(pe):
            mm = nc.tensor.matmul

            def norm_transpose(k, bank):
                pe.wait_ge(ln, 8 * k + 6)
                for c in range(NC):
                    ins = nc.tensor.transpose(ps[:, bank, c * P:c * P + P], normed[:, c * P:c * P + P], ident[:])
                ins.then_inc(ln, 1)

            def split_product(dst, a_hi_, a_lo_, b_hi_, b_lo_, first, last):
                mm(dst, a_hi_, b_hi_, start=first, stop=False)
                mm(dst, a_lo_, b_hi_, start=False, stop=False)
                return mm(dst, a_hi_, b_lo_, start=False, stop=last)

            def project(j):
                ch, cl = ctx_hi[j % 2], ctx_lo[j % 2]
                pe.wait_ge(c_lo, j + 1 + (j == 3))
                pe.wait_ge(w_lo, 1)
                for kv in range(KVH):
                    if j:
                        pe.wait_ge(k_ev, 4 * (j - 1) + kv + 1)
                    if j == 2 and kv == 2:
                        pe.wait_ge(ln, 8)
                    for c in range(NC):
                        ins = split_product(ps[:, kv, :], wkv_hi[:, 0, c, kv * P:kv * P + P],
                                            wkv_lo[:, 0, c, kv * P:kv * P + P], ch[:, c, :], cl[:, c, :],
                                            c == 0, c == NC - 1)
                    ins.then_inc(kv_ps, 1)
                pe.wait_ge(w_lo, 2)
                for t in range(4):
                    if j:
                        pe.wait_ge(v_ev, 4 * (j - 1) + t + 1)
                    for c in range(NC):
                        ins = split_product(ps[:, 4 + t, :], ch[:, c, t * P:t * P + P], cl[:, c, t * P:t * P + P],
                                            wkv_hi[:, 1, c, :], wkv_lo[:, 1, c, :], c == 0, c == NC - 1)
                    ins.then_inc(kv_ps, 1)

            project(0)
            project(1)
            pe.wait_ge(ident_ok, 2)
            pe.wait_ge(k_ev, 7)
            norm_transpose(0, 2)
            project(2)
            project(3)
            pe.wait_ge(c_lo, 4)
            pe.wait_ge(k_ev, 13)
            for kv in range(KVH):
                for c in range(NC):
                    ins = split_product(ps[:, 0, kv * P:kv * P + P], wkv_hi[:, 0, c, kv * P:kv * P + P],
                                        wkv_lo[:, 0, c, kv * P:kv * P + P], lat_hi[:, c, :], lat_lo[:, c, :],
                                        c == 0, c == NC - 1)
            ins.then_inc(kv_ps, 1)
            pe.wait_ge(k_ev, 14)
            for c in range(NC):
                ins = split_product(ps[:, 1, :], lat_hi[:, c, :], lat_lo[:, c, :], wkv_hi[:, 1, c, :],
                                    wkv_lo[:, 1, c, :], c == 0, c == NC - 1)
            ins.then_inc(kv_ps, 1)

            def queries(m, kv, p, bank):
                s = 2 + p // 2
                if p % 2 == 0:
                    pe.wait_ge(landed[s], kv * 16 + 32)
                w = ring[s][:].rearrange("p (c n) -> p c n", c=NC)
                for h in range(2):
                    col = ((p % 2) * 2 + h) * P
                    for c in range(NC):
                        ins = mm(ps[:, bank, h * P:h * P + P], w[:, c, col:col + P], norm_t[:, c, :],
                                 start=(c == 0), stop=(c == NC - 1))
                ins.then_inc(q_ps, 1)
                if p % 2 == 1:
                    pe.wait_ge(q_ps, m + 1)
                    pe.sem_inc(freed[s], 1)

            def scores(m, b, qslot, c, wait_bank=True):
                h, i = c // NCHUNK, c % NCHUNK
                lo, hi = chunk_cols(i)
                if wait_bank:
                    pe.wait_ge(s_ev, 10 * m + c - 3)
                split_product(ps[:, (2 * b + c) % 4, 0:hi - lo], q_hi[qslot][:, h * P:h * P + P],
                              q_lo[qslot][:, h * P:h * P + P], k_hi[:, lo:hi], k_lo[:, lo:hi],
                              True, True).then_inc(s_ps, 1)

            def transposes(unit, b, u, bank):
                for w in range(2 if u < 8 else 1):
                    for h in range(2):
                        kt = 2 * u + w
                        at = w * 256 + h * P
                        ins = nc.tensor.transpose(ps[:, bank, at:at + P], prob[b][:, h, kt * P:kt * P + P], ident[:])
                ins.then_inc(t_ps, 1)

            def values(unit, b, u):
                pe.wait_ge(ptl_ok, unit + 1)
                for w in range(2 if u < 8 else 1):
                    kt = 2 * u + w
                    ins = split_product(ps[:, 6 + b, 0:256], v_hi[:, kt, :], v_lo[:, kt, :],
                                        pt_hi[u % 3][:, w, :], pt_lo[u % 3][:, w, :], kt == 0, kt == NKT - 1)
                ins.then_inc(pv_ps, 1)

            def attn_step(kv, p, last):
                n = kv * PAIRS + p
                b = p % 2
                turn = p == PAIRS - 1
                pe.wait_ge(diag_ok, n + 1)
                if last and turn:
                    pe.wait_ge(o_ok, n)
                else:
                    pe.wait_ge(ql_ok, n + 2)
                mm(ps[:, 6 + b, 256:512], ones[:], diag[b][:].rearrange("p h n -> p (h n)"), start=True,
                   stop=True).then_inc(pv_ps, 1)
                if p == 0:
                    pe.wait_ge(vl_ok, 2 * kv + 2)
                for u in range(UNITS):
                    tgt = u + 2
                    if tgt < UNITS:
                        pe.wait_ge(ptl_ok, 9 * n + u + 1)
                        transposes(9 * n + tgt, b, tgt, 4 + (9 * p + tgt) % 2)
                    elif not turn:
                        pe.wait_ge(ptl_ok, 9 * n + u + 1)
                        if u == 7:
                            pe.wait_ge(exp_ok, 2 * n + 4)
                        transposes(9 * (n + 1) + tgt - UNITS, 1 - b, tgt - UNITS, 4 + (9 * p + tgt) % 2)
                    values(9 * n + u, b, u)
                    if not turn:
                        if u < 5:
                            if u == 0:
                                pe.wait_ge(ql_ok, n + 2)
                            scores(n + 1, 1 - b, (p + 1) % 4, 2 * u)
                            scores(n + 1, 1 - b, (p + 1) % 4, 2 * u + 1)
                        if u == 5 and not (last and p >= 2):
                            pe.wait_ge(o_ok, n + 1)
                            queries(n + 2, kv + (p >= 2), (p + 2) % 4, 6 + (1 - b))
                    elif not last and u >= 4:
                        if u == 4:
                            pe.wait_ge(kl_ok, kv + 2)
                            pe.wait_ge(ql_ok, n + 2)
                        scores(n + 1, 1 - b, 0, 2 * u - 8)
                        scores(n + 1, 1 - b, 0, 2 * u - 7)
                if turn and not last:
                    pe.wait_ge(o_ok, n + 1)
                    queries(n + 2, kv + 1, 1, 6 + (1 - b))
                    pe.wait_ge(exp_ok, 2 * n + 4)
                    for i in range(2):
                        pe.wait_ge(ptl_ok, 9 * (n + 1) + i - 1)
                        transposes(9 * (n + 1) + i, 1 - b, i, 4 + (9 * (p + 1) + i) % 2)

            pe.wait_ge(v_ev, 16)
            pe.wait_ge(ln, 8)
            queries(0, 0, 0, 7)
            queries(1, 0, 1, 6)
            pe.wait_ge(k_ev, 17)
            pe.wait_ge(v_ev, 17)
            pe.wait_ge(kl_ok, 1)
            pe.wait_ge(ql_ok, 1)
            for c in range(10):
                scores(0, 0, 0, c, wait_bank=c >= 4)
            pe.wait_ge(pool_const, 1)
            pe.wait_ge(exp_ok, 2)
            transposes(0, 0, 0, 4)
            transposes(1, 0, 1, 5)
            with pe.Fori(0, KVH - 1) as kv:
                for p in range(PAIRS):
                    attn_step(kv, p, False)
            for p in range(PAIRS):
                attn_step(KVH - 1, p, True)

            for c in range(8):
                s, k = ((0, 3), (1, 3), (2, 6), (3, 6), (0, 4), (1, 4), (2, 7), (3, 7))[c]
                pe.wait_ge(landed[s], 16 * k)
                pe.wait_ge(o_ok, 2 * c + 3)
                w = ring[s][:].rearrange("p (h n) -> p h n", h=4)
                for h in range(4):
                    at = (4 * (c % 2) + h) * P
                    ins = mm(ps[:, 0, :], k_all[:, c // 2, at:at + P], w[:, h, :],
                             start=(c == 0 and h == 0), stop=(c == 7 and h == 3))
                ins.then_inc(freed[s], 1)
            pe.wait_ge(freed[3], 7)
            pe.sem_inc(wo_ps, 1)
            norm_transpose(1, 7)

            pe.wait_ge(ln, 16)
            pe.wait_ge(const_in, 160)
            for c in range(NC):
                ins = mm(ps[:, 6, 0:NH], norm_t[:, c, :], w_dt_sb[:, c, :], start=(c == 0), stop=(c == NC - 1))
            ins.then_inc(dt_ps, 1)

            def in_proj(slot, loads, q, bank):
                pe.wait_ge(landed[slot], loads * 16)
                if not (isinstance(q, int) and q < 2):
                    pe.wait_ge(proj_ev, q - 1)
                w = ring[slot][:].rearrange("p (t c n) -> p t c n", t=4, c=NC)
                for t in range(4):
                    for c in range(NC):
                        ins = mm(ps[:, bank, t * T:t * T + T], w[:, t, c, :], norm_t[:, c, :],
                                 start=(c == 0), stop=(c == NC - 1))
                ins.then_inc(proj_ps, 1)
                pe.wait_ge(proj_ps, q + 1)
                pe.sem_inc(freed[slot], 1)

            def segments(g, b, half):
                if not (isinstance(g, int) and g == 0 and half == 0):
                    pe.wait_ge(dec_ok, 2 * g + half)
                pe.wait_ge(at_ok, g + 1)
                for i in range(2):
                    h = 8 * half + 4 * i
                    mm(ps[:, 2 + i, :], upper_r[:], at_hi[:, h:h + 4, :].rearrange("p h t -> p (h t)"), start=True, stop=False)
                    ins = mm(ps[:, 2 + i, :], upper_r[:], at_lo[:, h:h + 4, :].rearrange("p h t -> p (h t)"), start=False, stop=True)
                ins.then_inc(seg_ps, 1)

            def x_transposes(g, b):
                pe.wait_ge(silu_ok, 2 * g + 6)
                if not (isinstance(g, int) and g == 0):
                    pe.wait_ge(y_ok, g)
                for t in range(TPG):
                    ins = nc.tensor.transpose(ps[:, 4 + t // 4, (t % 4) * T:(t % 4 + 1) * T], xc[b][:, t, :], ident[:])
                ins.then_inc(xt_ps, 1)

            def y_product(g, b):
                pe.wait_ge(xdt_ok, g + 1)
                pe.wait_ge(m_ok, 2 * g + 2)
                for h in range(HPG):
                    t = h // 2
                    ins = mm(ps[(h % 2) * 64:(h % 2) * 64 + 64, 4 + t // 4, (t % 4) * T:(t % 4 + 1) * T],
                             xdt[:, h, :], decay[b][:, h, :], start=True, stop=True)
                ins.then_inc(y_ps, 1)

            def out_proj(g, chunks):
                pe.wait_ge(ug_ok, g + 1)
                if not (isinstance(g, int) and g == 0):
                    pe.wait_ge(oacc_ok, g + 1)
                for i, (slot, loads) in enumerate(chunks):
                    pe.wait_ge(landed[slot], loads * 16)
                    w = ring[slot][:].rearrange("p (t n) -> p t n", t=4)
                    for t in range(4):
                        ins = mm(ps[:, 6, :], ug[:, 4 * i + t, :], w[:, t, :], start=(i == 0 and t == 0),
                                 stop=(i == 1 and t == 3))
                    ins.then_inc(freed[slot], 1)
                pe.wait_ge(freed[chunks[1][0]], chunks[1][1])
                pe.sem_inc(op_ps, 1)

            for m in range(4):
                in_proj(stream(m)[0], stream(m)[1] + 1, m, m % 2)
            for m in range(4, 6):
                in_proj(stream(m)[0], stream(m)[1] + 1, m, m % 2)
            pe.wait_ge(silu_ok, 4)
            for g in range(GROUPS):
                ins = mm(ps[:, 4 + g // 4, (g % 4) * T:(g % 4 + 1) * T], bc[:, g, :], bc[:, 8 + g, :],
                         start=True, stop=True)
            ins.then_inc(gm_ps, 1)
            pe.wait_ge(pool_const, 8)
            segments(0, 0, 0)
            for m in range(6, 8):
                in_proj(stream(m)[0], stream(m)[1] + 1, m, m % 2)
            segments(0, 0, 1)
            pe.wait_ge(gm_ok, 1)

            def mamba_step(g, b, turn, last):
                q = 4 * g + 8
                chunks = [((8 + 6 * b + j) % RING,
                           turn * 3 + (BEFORE[(8 + 6 * b + j) % RING] + (8 + 6 * b + j) // RING + 1))
                          for j in range(6)]
                x_transposes(g, b)
                if last:
                    y_product(g, b)
                    out_proj(g, chunks[0:2])
                    return
                segments(g + 1, 1 - b, 0)
                in_proj(*chunks[0], q, 0)
                segments(g + 1, 1 - b, 1)
                y_product(g, b)
                in_proj(*chunks[1], q + 1, 1)
                in_proj(*chunks[2], q + 2, 0)
                in_proj(*chunks[3], q + 3, 1)
                out_proj(g, chunks[4:6])

            with pe.Fori(0, 3) as turn:
                for b in range(2):
                    mamba_step(turn * 2 + b, b, turn, False)
            mamba_step(6, 0, 3, False)
            mamba_step(7, 1, 3, True)
            pe.wait_ge(var_s, 1)
            pe.wait_ge(pool_const, 7)
            mm(ps[:, 7, 0:1], sq_tok[:], ones_m[:], start=True, stop=True).then_inc(var_s, 1)

            norm_transpose(2, 7)
            pe.wait_ge(ln, 24)
            for c in range(NC):
                ins = mm(ps[0:16, 6, 0:T], c1_sb[:, c, :], norm_t[:, c, :], start=(c == 0), stop=(c == NC - 1))
            ins.then_inc(f_pe, 1)
            pe.wait_ge(f_act, 1)
            for i in range(4):
                lo, hi = i * BANK, min(i * BANK + BANK, FF)
                ins = mm(ps[:, i, 0:hi - lo], r1_sb[:], c2_sb[:, lo:hi], start=True, stop=True)
            ins.then_inc(f_pe, 1)
            for c in range(NC):
                s, before = stream(FFN0 + c)
                pe.wait_ge(landed[s], 16 * (before + 1))
                for i in range(4):
                    lo, hi = i * BANK, min(i * BANK + BANK, FF)
                    ins = mm(ps[:, 4 + i, 0:hi - lo], norm_t[:, c, :], ring[s][:, lo:hi], start=(c == 0),
                             stop=(c == NC - 1))
                ins.then_inc(freed[s], 1)
            pe.wait_ge(freed[stream(FFN0 + 3)[0]], stream(FFN0 + 3)[1] + 1)
            pe.sem_inc(f_pe, 1)
            for i in range(4):
                pe.wait_ge(f_dve, i + 1)
                for t in range(4 * i, min(4 * i + 4, NFT)):
                    ins = nc.tensor.transpose(ps[:, i, (t % 4) * T:(t % 4 + 1) * T], hsel[:, t * T:t * T + T], ident[:])
                ins.then_inc(f_pe, 1)
            for i in range(4):
                s, before = stream(FFN0 + 4 + i)
                pe.wait_ge(landed[s], 16 * (before + 1))
                pe.wait_ge(f_act, 2 + i)
                for t in range(4 * i, min(4 * i + 4, NFT)):
                    ins = mm(ps[:, 4, :], hsel_t[:, t, :], ring[s][:, (t % 4) * DM:(t % 4 + 1) * DM],
                             start=(t == 0), stop=(t == NFT - 1))
            ins.then_inc(f_pe, 1)


_NAMES = ["x", "ctx_t", "wq", "wk", "wv", "wo", "w_in", "w_dt", "w_out", "conv_w", "conv_b", "dt_bias",
          "a_log", "d_skip", "norm_w", "c1", "c2", "w1", "w2", "w2_tail"]


def kernel(**inputs):
    import numpy as np
    import concourse.bacc as bacc
    from concourse.bass_utils import run_bass_kernel_spmd

    a = {k: np.asarray(v) for k, v in inputs.items()}

    def tiles(w, n):
        k, cols = w.shape
        return w.reshape(k // 128, 128, cols // n, n).transpose(2, 1, 0, 3).reshape(cols // n, 128, -1)

    def rows(w, r):
        k, cols = w.shape
        return w.reshape(k // (128 * r), r, 128, cols).transpose(0, 2, 1, 3).reshape(-1, 128, r * cols)

    w_in = a["L0_attn_in_proj_w"]
    w_main = w_in[:18432].reshape(36, 4, 128, 4, 128).transpose(0, 4, 1, 3, 2).reshape(36, 128, 2048)
    w2 = a["L0_ffn_w2t"]
    laid = {
        "x": a["x"][0],
        "ctx_t": tiles(a["ctx_4096"][0].T, 512),
        "wq": tiles(a["L0_xattn_Wq"], 512),
        "wk": tiles(a["L0_xattn_Wk"], 512)[0],
        "wv": tiles(a["L0_xattn_Wv"], 512)[0],
        "wo": rows(a["L0_xattn_Wo"], 4),
        "w_in": w_main,
        "w_dt": tiles(w_in[18432:].T, 128).reshape(128, 4, 128),
        "w_out": rows(a["L0_attn_out_proj_w"].T, 4),
        "conv_w": a["L0_attn_conv_w"].reshape(80, 128, 4).transpose(1, 0, 2),
        "conv_b": a["L0_attn_conv_b"].reshape(80, 128).T,
        "dt_bias": a["L0_attn_dt_bias"],
        "a_log": a["L0_attn_A_log"],
        "d_skip": a["L0_attn_D"].reshape(64, 2).T,
        "norm_w": a["L0_attn_norm_w"].reshape(64, 128).T,
        "c1": tiles(a["L0_ffn_c1_w"].T, 16).reshape(128, 4, 16),
        "c2": a["L0_ffn_c2_w"].T,
        "w1": a["L0_ffn_w1"].T.reshape(4, 128, 1792),
        "w2": rows(w2[:1536], 4),
        "w2_tail": rows(w2[1536:], 2),
    }
    nc = bacc.Bacc("TRN2", target_bir_lowering=False, num_devices=1)
    arrays, args = {}, []
    for name in _NAMES:
        v = np.ascontiguousarray(laid[name])
        arrays[f"{name}_dram"] = v
        args.append(nc.dram_tensor(f"{name}_dram", v.shape, mybir.dt.from_np(v.dtype), kind="ExternalInput").ap())
    out = nc.dram_tensor("out_dram", (T, DM), F32, kind="ExternalOutput").ap()
    build(nc, *args, out)
    r = run_bass_kernel_spmd(nc, [arrays], core_ids=[0])
    return r.results[0]["out_dram"].reshape(1, T, DM)
```

```python
from contextlib import ExitStack

import concourse.bass as bass
from concourse import mybir

F32 = mybir.dt.float32
F32R = mybir.dt.float32r
I32 = mybir.dt.int32
ALU = mybir.AluOpType
ACT = mybir.ActivationFunctionType
AX_X = mybir.AxisListType.X

P = 128
T = 128
DM = 512
NC = DM // P
BANK = 512
EPS = 1e-5

S_CTX = 2048
KV_LEN = S_CTX + T
NKT = KV_LEN // P
KVH = 4
HPK = 8
PAIRS = HPK // 2
NCHUNK = 5
UNITS = 9
PIECES = ((0, 512), (512, 1024), (1024, 1536), (1536, 2176))
NPC = len(PIECES)
EXP_AT = ((), (), ((0, 0),), ((0, 1), (0, 2)), ((0, 3),), ((1, 0), (1, 1)), ((1, 2),), ((1, 3),), ())
K_AT = {2: {5: (0,), 6: (1,), 7: (2,), 8: (3,)}, 3: {0: (4,)}}
V_AT = {4: 0, 7: 1}
W_UNIT = 2
OUT_UNITS = (5, 6)
ADD_UNITS = (6, 7)
Q_UNIT = 2
V_PARTS = ((0, 6), (6, 12), (12, 17))
SCALE = 128.0 ** -0.5

GROUPS = 8
HPG = 16
TPG = 8
NH = GROUPS * HPG
INTER = NH * 64
FF = 1792
BLK = 32
NBLK = FF // BLK
NFT = FF // P

RING = 4
SLOT = 2048
FFN0 = 52


def chunk_cols(c):
    return c * BANK, min((c + 1) * BANK, KV_LEN)


def build(nc, x, ctx_t, wq, wk, wv, wo, w_in, w_dt, w_out, conv_w, conv_b, dt_bias, a_log, d_skip,
          norm_w, c1, c2, w1, w2, w2_tail, out):
    with ExitStack() as ctx:
        def sem(name):
            return ctx.enter_context(nc.semaphore(name))

        def sbuf(stack, name, shape, dt=F32):
            return stack.enter_context(nc.sbuf_tensor(name, shape, dt))

        ring = [sbuf(ctx, f"ring{s}", [P, SLOT]) for s in range(RING)]
        res = sbuf(ctx, "res", [P, DM])
        normed = sbuf(ctx, "normed", [P, DM])
        norm_t = sbuf(ctx, "norm_t", [P, NC, T])
        ident = sbuf(ctx, "ident", [P, P])
        stats = sbuf(ctx, "stats", [P, 6])
        mean_var = sbuf(ctx, "mean_var", [P, 2])
        rstd = sbuf(ctx, "rstd", [P, 3])
        row_inv = sbuf(ctx, "row_inv", [P, 2, 2])
        o_hi = sbuf(ctx, "o_hi", [P, 2 * P], F32R)
        o_lo = sbuf(ctx, "o_lo", [P, 2 * P], F32R)
        wo_hi = sbuf(ctx, "wo_hi", [P, 2, DM], F32R)
        wo_lo = sbuf(ctx, "wo_lo", [P, 2, DM], F32R)

        with ExitStack() as st:
            k_all = sbuf(st, "k_all", [P, KVH, KV_LEN])
            v_all = sbuf(st, "v_all", [P, NKT, KVH * P])
            k_hi = sbuf(st, "k_hi", [P, KV_LEN], F32R)
            k_lo = sbuf(st, "k_lo", [P, KV_LEN], F32R)
            with ExitStack() as st1:
                wkv_hi = sbuf(st1, "wkv_hi", [P, 2, NC, DM], F32R)
                wkv_lo = sbuf(st1, "wkv_lo", [P, 2, NC, DM], F32R)
                ctx_hi = [sbuf(st1, f"ctx_hi{b}", [P, NC, BANK], F32R) for b in range(2)]
                ctx_lo = [sbuf(st1, f"ctx_lo{b}", [P, NC, BANK], F32R) for b in range(2)]
                lat_hi = sbuf(st1, "lat_hi", [P, NC, T], F32R)
                lat_lo = sbuf(st1, "lat_lo", [P, NC, T], F32R)
            with ExitStack() as st2:
                v_hi = sbuf(st2, "v_hi", [P, NKT, P], F32R)
                v_lo = sbuf(st2, "v_lo", [P, NKT, P], F32R)
                prob = [sbuf(st2, f"prob{b}", [P, 2, KV_LEN]) for b in range(2)]
                pt_hi = [sbuf(st2, f"pt_hi{b}", [P, 2, 2 * P], F32R) for b in range(3)]
                pt_lo = [sbuf(st2, f"pt_lo{b}", [P, 2, 2 * P], F32R) for b in range(3)]
                q_hi = [sbuf(st2, f"q_hi{b}", [P, 2 * P], F32R) for b in range(2)]
                q_lo = [sbuf(st2, f"q_lo{b}", [P, 2 * P], F32R) for b in range(2)]
                chunk_max = sbuf(st2, "chunk_max", [P, 2, 2, NCHUNK])
                neg_max = sbuf(st2, "neg_max", [P, 2, 2])
                part_sum = sbuf(st2, "part_sum", [P, 2, 2, NPC])
                row_sum = sbuf(st2, "row_sum", [P, 2, 2])
        with ExitStack() as st3:
            w_dt_sb = sbuf(st3, "w_dt_sb", [P, NC, NH])
            cw = sbuf(st3, "cw", [P, 80, 4])
            cb = sbuf(st3, "cb", [P, 80])
            dskip = sbuf(st3, "dskip", [P, 64])
            nw = sbuf(st3, "nw", [P, 64])
            dtb = sbuf(st3, "dtb", [P, NH])
            alog = sbuf(st3, "alog", [P, NH])
            upper = sbuf(st3, "upper", [P, P])
            causal = sbuf(st3, "causal", [P, P])
            ones_m = sbuf(st3, "ones_m", [P, 1])
            c1_sb = sbuf(st3, "c1_sb", [P, NC, 16])
            c2_sb = sbuf(st3, "c2_sb", [16, FF])
            rank_i = sbuf(st3, "rank_i", [P, BLK], I32)
            sq_sum = sbuf(st3, "sq_sum", [P, TPG, T])
            softplus = [sbuf(st3, f"softplus{i}", [P, NH]) for i in range(6)]
            dt = sbuf(st3, "dt", [P, NH])
            a_f = sbuf(st3, "a_f", [P, NH])
            a_hi = sbuf(st3, "a_hi", [P, NH], F32R)
            a_lo = sbuf(st3, "a_lo", [P, NH], F32R)
            upper_r = sbuf(st3, "upper_r", [P, P], F32R)
            o_acc = sbuf(st3, "o_acc", [P, DM])
            raw = [sbuf(st3, f"raw{b}", [P, 4, T]) for b in range(2)]
            acc = [sbuf(st3, f"acc{b}", [P, 4, T]) for b in range(2)]
            bc = sbuf(st3, "bc", [P, 16, T])
            gm = sbuf(st3, "gm", [P, GROUPS, T])
            xc = [sbuf(st3, f"xc{b}", [P, TPG, T]) for b in range(2)]
            sg = [sbuf(st3, f"sg{b}", [P, TPG, T]) for b in range(2)]
            at_hi = sbuf(st3, "at_hi", [P, HPG, T], F32R)
            at_lo = sbuf(st3, "at_lo", [P, HPG, T], F32R)
            decay = [sbuf(st3, f"decay{b}", [P, HPG, T]) for b in range(2)]
            xdt = sbuf(st3, "xdt", [P, HPG, 64])
            yv = sbuf(st3, "yv", [P, TPG, T])
            ysq = sbuf(st3, "ysq", [P, TPG, T])
            sq_tok = sbuf(st3, "sq_tok", [P, T])
            ug = sbuf(st3, "ug", [P, TPG, T])
            r1_sb = sbuf(st3, "r1_sb", [16, T])
            rank = sbuf(st3, "rank", [P, BLK])
            bmax = sbuf(st3, "bmax", [P, NBLK])
            kmax = sbuf(st3, "kmax", [P, NBLK])
            final = sbuf(st3, "final", [P, DM])
            key = decay[0][:, 0:FF // T, :].rearrange("p a b -> p (a b)").rearrange("p (n j) -> p n j", j=BLK)
            hsel = decay[1][:, 0:FF // T, :].rearrange("p a b -> p (a b)")
            hsel_t = bc

        k_flat = k_all[:, :, :].rearrange("p k n -> p (k n)")
        ps = ctx.enter_context(nc.psum_tensor("ps", [P, 8, BANK], F32))

        landed = [sem(f"landed{s}") for s in range(RING)]
        freed = [sem(f"freed{s}") for s in range(RING)]
        x_in = sem("x_in")
        const_in = sem("const_in")
        ident_ok = sem("ident_ok")
        pool_const = sem("pool_const")
        ln = sem("ln")
        first_in = [sem(f"first_in{c}") for c in range(NC - 1)]
        first_hi, first_lo = sem("first_hi"), sem("first_lo")
        w_hi, w_lo, c_hi, c_lo = sem("w_hi"), sem("w_lo"), sem("c_hi"), sem("c_lo")
        kv_ps, k_ev, v_ev = sem("kv_ps"), sem("k_ev"), sem("v_ev")
        kh_ok, kl_ok, vh_ok, vl_ok = sem("kh_ok"), sem("kl_ok"), sem("vh_ok"), sem("vl_ok")
        q_ps, qh_ok, ql_ok = sem("q_ps"), sem("qh_ok"), sem("ql_ok")
        s_ps, s_ev, nm_ok, exp_ok = sem("s_ps"), sem("s_ev"), sem("nm_ok"), sem("exp_ok")
        t_ps, pth_ok, ptl_ok, pv_ps = sem("t_ps"), sem("pth_ok"), sem("ptl_ok"), sem("pv_ps")
        sum_ok, inv_ok, oh_ok, ol_ok = sem("sum_ok"), sem("inv_ok"), sem("oh_ok"), sem("ol_ok")
        woh_ok, wol_ok, wo_ps, wo_ev = sem("woh_ok"), sem("wol_ok"), sem("wo_ps"), sem("wo_ev")
        res_ok = sem("res_ok")
        dt_ps, dts, a_ok = sem("dt_ps"), sem("dts"), sem("a_ok")
        proj_ev, taps, conv_ok, silu_ok = sem("proj_ev"), sem("taps"), sem("conv_ok"), sem("silu_ok")
        gm_ps, gm_ok, at_ok, seg_ps, dec_ok, m_ok = (sem("gm_ps"), sem("gm_ok"), sem("at_ok"),
                                                     sem("seg_ps"), sem("dec_ok"), sem("m_ok"))
        xt_ps, xdt_ok, y_ps, y_ok, ysq_ok, sq_ok = (sem("xt_ps"), sem("xdt_ok"), sem("y_ps"),
                                                    sem("y_ok"), sem("ysq_ok"), sem("sq_ok"))
        ug_ok, oacc_ok, var_s = sem("ug_ok"), sem("oacc_ok"), sem("var_s")
        f_pe, f_dve, f_act, f_mask = sem("f_pe"), sem("f_dve"), sem("f_act"), sem("f_mask")
        stored = sem("stored")

        BEFORE = (6, 6, 5, 5)

        def stream(m):
            slot = (m + 2) % RING
            return slot, BEFORE[slot] + m // RING

        def step_chunk(turn, b, j):
            slot, before = stream(8 + 6 * b + j)
            return slot, turn * 3 + before

        block = ctx.enter_context(nc.Block())

        @block.sync
        def _(sp):
            def load(slot, src, prior):
                if not (isinstance(prior, int) and prior == 0):
                    sp.wait_ge(freed[slot], prior)
                cols = src.shape[-1]
                sp.dma_start(ring[slot][:, 0:cols], src).then_inc(landed[slot], 16)

            for c in range(NC):
                for slot, src in ((0, wk), (2, ctx_t[0])):
                    piece = slice(c * DM, (c + 1) * DM)
                    done = first_in[c] if c < NC - 1 else landed[slot]
                    sp.dma_start(ring[slot][:, piece], src[:, piece]).then_inc(done, 16)
            load(1, wv, 0)
            sp.dma_start(res[:], x).then_inc(x_in, 16)
            load(3, ctx_t[1], 0)
            load(0, ctx_t[2], 1)
            load(1, ctx_t[3], 1)
            load(2, wq[0], 1)
            load(3, wq[1], 1)
            load(0, wo[0], 2)
            load(1, wo[1], 2)
            for kv in range(1, KVH):
                load(2, wq[2 * kv], 1 + kv)
                load(3, wq[2 * kv + 1], 1 + kv)
                load(0, wo[2 * kv], 2 + kv)
                load(1, wo[2 * kv + 1], 2 + kv)
            sp.wait_ge(kl_ok, KVH * NCHUNK)
            sp.dma_start(w_dt_sb[:], w_dt).then_inc(const_in, 16)
            sp.dma_start(dtb[:], dt_bias.unsqueeze(0).to_broadcast([P, NH])).then_inc(const_in, 16)
            sp.dma_start(alog[:], a_log.unsqueeze(0).to_broadcast([P, NH])).then_inc(const_in, 16)
            sp.dma_start(cw[:], conv_w).then_inc(const_in, 16)
            sp.dma_start(cb[:], conv_b).then_inc(const_in, 16)
            sp.dma_start(nw[:], norm_w).then_inc(const_in, 16)
            for half in range(2):
                sp.dma_start(dskip[64 * half:64 * half + 64, :],
                             d_skip[half:half + 1, :].to_broadcast([64, 64])).then_inc(const_in, 16)
            sp.dma_start(c1_sb[:], c1).then_inc(const_in, 16)
            sp.dma_start(c2_sb[:], c2).then_inc(const_in, 16)
            for m in range(4):
                load(stream(m)[0], w_in[32 + m], stream(m)[1])
            for j in range(2):
                load(stream(4 + j)[0], w_in[16 + j], stream(4 + j)[1])
            for j in range(2):
                load(stream(6 + j)[0], w_in[j], stream(6 + j)[1])

            w_in_rows = w_in.rearrange("n p f -> (n p) f")
            w_out_rows = w_out.rearrange("n p f -> (n p) f")

            def step_loads(g, b, turn, last):
                sources = [] if last else [(w_in_rows, 16 + 2 * (g + 1) + i) for i in range(2)] + \
                                          [(w_in_rows, 2 * (g + 1) + i) for i in range(2)]
                sources += [(w_out_rows, 2 * g + i) for i in range(2)]
                for j, (rows, at) in enumerate(sources):
                    slot, before = step_chunk(turn, b, j)
                    load(slot, rows[bass.ds(at * P, P), :], before)

            with sp.Fori(0, 3) as turn:
                for b in range(2):
                    step_loads(turn * 2 + b, b, turn, False)
            step_loads(6, 0, 3, False)
            step_loads(7, 1, 3, True)
            for c in range(4):
                s, before = stream(FFN0 + c)
                load(s, w1[c], before)
            for c in range(4):
                s, before = stream(FFN0 + 4 + c)
                load(s, w2[c] if c < 3 else w2_tail[0], before)
            sp.wait_ge(f_dve, 6)
            sp.dma_start(out, final[:]).then_inc(stored, 16)
            sp.wait_ge(stored, 16)

        @block.gpsimd
        def _(pool):
            pool.memset(ident[:], 0.0).then_inc(ident_ok, 1)
            pool.wait_ge(ident_ok, 1)
            pool.affine_select(out=ident[:], in_=ident[:], compare_op=ALU.not_equal, fill=1.0, base=0,
                               pattern=[[-1, P]], channel_multiplier=1).then_inc(ident_ok, 1)
            pool.wait_ge(ident_ok, 2)
            sub = lambda dst, a, hi: pool.tensor_tensor(dst, a, hi, ALU.subtract)

            def k_split(kv, i):
                a, b = chunk_cols(i)
                pool.wait_ge(kh_ok, NCHUNK * kv + i + 1)
                sub(k_lo[:, a:b], k_all[:, kv, a:b], k_hi[:, a:b].bitcast(F32)).then_inc(kl_ok, 1)

            def v_split(kv, part):
                a, b = V_PARTS[part]
                pool.wait_ge(vh_ok, 3 * kv + part + 1)
                sub(v_lo[:, a:b, :], v_all[:, a:b, kv * P:kv * P + P],
                    v_hi[:, a:b, :].bitcast(F32)).then_inc(vl_ok, 1)

            def wo_split(m):
                slot, half = m % PAIRS // 2, m % 2
                pool.wait_ge(woh_ok, m + 1)
                sub(wo_lo[:], ring[slot][:, half * 2 * DM:(half + 1) * 2 * DM]
                    .rearrange("p (h n) -> p h n", h=2), wo_hi[:].bitcast(F32)).then_inc(wol_ok, 1)
                if half == 1:
                    pool.wait_ge(wol_ok, m + 1)
                    pool.sem_inc(freed[slot], 1)

            for part in range(3):
                v_split(0, part)
            for n in range(KVH * PAIRS):
                kv, p = n // PAIRS, n % PAIRS
                more = kv < KVH - 1
                if more and p == 3:
                    k_split(kv + 1, 4)
                if n:
                    wo_split(n - 1)
                if more and p == 2:
                    for i in range(4):
                        k_split(kv + 1, i)
                if more and p == 3:
                    for part in range(3):
                        v_split(kv + 1, part)

            pool.wait_ge(kl_ok, KVH * NCHUNK)
            pool.memset(upper[:], 1.0).then_inc(pool_const, 1)
            pool.memset(causal[:], 1.0).then_inc(pool_const, 1)
            pool.memset(ones_m[:], 1.0).then_inc(pool_const, 1)
            pool.iota(rank_i[:], pattern=[[-1, BLK]], base=BLK, channel_multiplier=0).then_inc(pool_const, 1)
            pool.memset(sq_sum[:], 0.0).then_inc(sq_ok, 1)
            pool.wait_ge(pool_const, 4)
            pool.affine_select(out=upper[:], in_=upper[:], compare_op=ALU.is_gt, fill=0.0, base=0,
                               pattern=[[-1, P]], channel_multiplier=1).then_inc(pool_const, 1)
            pool.affine_select(out=causal[:], in_=causal[:], compare_op=ALU.is_ge, fill=0.0, base=0,
                               pattern=[[1, P]], channel_multiplier=-1).then_inc(pool_const, 1)

            def steps_a(g):
                for dst, src in ((at_hi, a_hi), (at_lo, a_lo)):
                    i = pool.affine_select(
                        out=dst[:], in_=src[:, g * HPG:g * HPG + HPG].bitcast(F32).unsqueeze(2).to_broadcast([P, HPG, T]),
                        compare_op=ALU.is_ge, fill=0.0, base=0, pattern=[[0, HPG], [1, T]],
                        channel_multiplier=-1)
                i.then_inc(at_ok, 1)

            def add_squares(g):
                pool.wait_ge(ysq_ok, g + 1)
                pool.wait_ge(sq_ok, g + 1)
                pool.tensor_tensor(sq_sum[:], sq_sum[:], ysq[:], ALU.add).then_inc(sq_ok, 1)

            wo_split(KVH * PAIRS - 1)
            pool.wait_ge(a_ok, 2)
            steps_a(0)
            for g in range(GROUPS - 1):
                pool.wait_ge(seg_ps, 2 * g + 2)
                steps_a(g + 1)
                add_squares(g)
            add_squares(GROUPS - 1)

        @block.scalar
        def _(act):
            copy = lambda dst, src: nc.scalar.activation(dst, src, ACT.Copy)

            def norm_sqrt(k):
                act.wait_ge(ln, 8 * k + 3)
                nc.scalar.activation(rstd[:, 1:2], rstd[:, 0:1], ACT.Sqrt).then_inc(ln, 1)

            def norm_evac(k, bank):
                act.wait_ge(ln, 8 * k + 7)
                copy(norm_t[:], ps[:, bank, :].rearrange("p (c t) -> p c t", c=NC)).then_inc(ln, 1)

            def split_first(c):
                if c < NC - 1:
                    act.wait_ge(first_in[c], 32)
                else:
                    act.wait_ge(landed[0], 16)
                copy(wkv_hi[:, 0, c, :], ring[0][:, c * DM:(c + 1) * DM]).then_inc(first_hi, 1)
                if c == NC - 1:
                    act.wait_ge(landed[2], 16)
                copy(ctx_hi[0][:, c, :], ring[2][:, c * DM:(c + 1) * DM]).then_inc(first_hi, 1)

            def split_wv():
                act.wait_ge(landed[1], 16)
                copy(wkv_hi[:, 1], ring[1][:].rearrange("p (c n) -> p c n", c=NC)).then_inc(w_hi, 1)

            def split_ctx(j):
                s, k = (2, 3, 0, 1)[j], (1, 1, 2, 2)[j]
                act.wait_ge(landed[s], 16 * k)
                if j >= 2:
                    act.wait_ge(kv_ps, 8 * (j - 1))
                copy(ctx_hi[j % 2][:], ring[s][:].rearrange("p (c n) -> p c n", c=NC)).then_inc(c_hi, 1)

            def v_out(j):
                for t in range(4):
                    act.wait_ge(kv_ps, 8 * j + 5 + t)
                    copy(v_all[:, 4 * j + t, :], ps[:, 4 + t, :]).then_inc(v_ev, 1)

            def k_split(kv, i):
                a, b = chunk_cols(i)
                copy(k_hi[:, a:b], k_flat[:, bass.ds(kv * KV_LEN + a, b - a)]).then_inc(kh_ok, 1)

            for c in range(NC):
                split_first(c)
            split_wv()
            split_ctx(1)
            norm_sqrt(0)
            v_out(0)
            split_ctx(2)
            act.wait_ge(k_ev, 5)
            k_split(0, 0)
            k_split(0, 1)
            norm_evac(0, 2)
            act.wait_ge(ln, 8)
            copy(lat_hi[:], norm_t[:]).then_inc(c_hi, 1)
            v_out(1)
            split_ctx(3)
            v_out(2)
            act.wait_ge(k_ev, 13)
            k_split(0, 2)
            k_split(0, 3)
            v_out(3)
            act.wait_ge(kv_ps, 34)
            copy(v_all[:, 16, :], ps[:, 1, :]).then_inc(v_ev, 1)

            def v_split(kv, part):
                a, b = V_PARTS[part]
                copy(v_hi[:, a:b, :], v_all[:, a:b, bass.ds(kv * P, P)]).then_inc(vh_ok, 1)

            def q_split(m, slot, bank):
                act.wait_ge(q_ps, m + 1)
                copy(q_hi[slot][:], ps[:, bank, 0:2 * P]).then_inc(qh_ok, 1)

            def soft_exp(m, b, h, i):
                if i == 0:
                    act.wait_ge(nm_ok, 2 * m + h + 1)
                lo, hi = PIECES[i]
                nc.scalar.activation(prob[b][:, h, lo:hi], prob[b][:, h, lo:hi], ACT.Exp,
                                     bias=neg_max[:, b, h:h + 1],
                                     accum_out=part_sum[:, b, h, i:i + 1]).then_inc(exp_ok, 1)

            def pt_split(unit, u, bank):
                w = 2 if u < 8 else 1
                act.wait_ge(t_ps, unit + 1)
                copy(pt_hi[u % 3][:, 0:w, :],
                     ps[:, bank, 0:w * 256].rearrange("p (w n) -> p w n", w=w)).then_inc(pth_ok, 1)

            def o_split(b):
                copy(o_hi[:], ps[:, 6 + b, 0:2 * P]).then_inc(oh_ok, 1)

            def wo_split(kv, p):
                act.wait_ge(landed[p // 2], 16 * kv + 48)
                copy(wo_hi[:], ring[p // 2][:, (p % 2) * 2 * DM:(p % 2 + 1) * 2 * DM]
                     .rearrange("p (h n) -> p h n", h=2)).then_inc(woh_ok, 1)

            def attn_step(kv, p, first, last):
                n = kv * PAIRS + p
                b = p % 2
                turn = p == PAIRS - 1
                for u in range(UNITS):
                    tgt = u + 2
                    if tgt < UNITS or not (last and turn):
                        act.wait_ge(pv_ps, 9 * n + u + 1)
                        pt_split(9 * n + tgt, tgt % UNITS, 4 + (9 * p + tgt) % 2)
                    if u == 0 and not first:
                        o_split(1 - b)
                    if u == W_UNIT and not first:
                        wo_split(kv - (p == 0), (p - 1) % PAIRS)
                    if not (last and turn):
                        for h, i in EXP_AT[u]:
                            soft_exp(n + 1, 1 - b, h, i)
                    if u == Q_UNIT + 1 and not (last and p >= 2):
                        q_split(n + 2, b, 6 + (1 - b))
                    if not last:
                        for i in K_AT.get(p, {}).get(u, ()):
                            k_split(kv + 1, i)
                        if turn and u in V_AT:
                            v_split(kv + 1, V_AT[u])
                if turn and not last:
                    act.wait_ge(pv_ps, 9 * n + 10)
                    v_split(kv + 1, 2)

            act.wait_ge(k_ev, 17)
            act.wait_ge(kv_ps, 34)
            q_split(0, 0, 7)
            k_split(0, NCHUNK - 1)
            q_split(1, 1, 6)
            act.wait_ge(v_ev, 17)
            v_split(0, 0)
            for h in range(2):
                for i in range(NPC):
                    soft_exp(0, 0, h, i)
            v_split(0, 1)
            v_split(0, 2)
            pt_split(0, 0, 4)
            pt_split(1, 1, 5)
            attn_step(0, 0, True, False)
            with act.Fori(0, KVH - 1) as kv:
                for p in range(1, PAIRS):
                    attn_step(kv, p, False, False)
                attn_step(kv + 1, 0, False, False)
            for p in range(1, PAIRS):
                attn_step(KVH - 1, p, False, True)
            act.wait_ge(pv_ps, 9 * KVH * PAIRS + 1)
            o_split(1)
            wo_split(KVH - 1, PAIRS - 1)

            norm_sqrt(1)
            norm_evac(1, 7)
            act.wait_ge(dts, 2)
            nc.scalar.activation(softplus[2][:], softplus[1][:], ACT.Exp, scale=-1.0).then_inc(dts, 1)
            act.wait_ge(const_in, 160)
            nc.scalar.activation(softplus[5][:], alog[:], ACT.Exp).then_inc(a_ok, 1)

            def raw_out(chunk, k, bank):
                act.wait_ge(freed[chunk[0]], chunk[1] + 1)
                if not (isinstance(k, int) and k < 2):
                    act.wait_ge(taps, k - 1)
                copy(raw[bank][:], ps[:, bank, :].rearrange("p (c t) -> p c t", c=4)).then_inc(proj_ev, 1)

            def conv_silu(k, slot, dst):
                act.wait_ge(taps, k + 1)
                nc.scalar.activation(dst, acc[slot][:], ACT.Silu).then_inc(silu_ok, 1)

            def gate_out(chunk, bank, dst):
                act.wait_ge(freed[chunk[0]], chunk[1] + 1)
                nc.scalar.activation(dst, ps[:, bank, :].rearrange("p (c t) -> p c t", c=4),
                                     ACT.Silu).then_inc(proj_ev, 1)

            def decay_exp(g, b, half):
                act.wait_ge(seg_ps, 2 * g + half + 1)
                nc.scalar.activation(decay[b][:, 8 * half:8 * half + 8, :],
                                     ps[:, 2:4, :].rearrange("p a (h t) -> p (a h) t", t=T),
                                     ACT.Exp).then_inc(dec_ok, 1)

            def squares(g):
                act.wait_ge(y_ok, g + 1)
                act.wait_ge(sq_ok, g + 1)
                nc.scalar.activation(ysq[:], yv[:], ACT.Square).then_inc(ysq_ok, 1)

            for k in range(4):
                raw_out(stream(k), k, k % 2)
                if k:
                    conv_silu(k - 1, (k - 1) % 2, bc[:, 4 * (k - 1):4 * k, :])
            raw_out(stream(4), 4, 0)
            conv_silu(3, 1, bc[:, 12:16, :])
            raw_out(stream(5), 5, 1)
            conv_silu(4, 0, xc[0][:, 0:4, :])
            conv_silu(5, 1, xc[0][:, 4:8, :])
            decay_exp(0, 0, 0)
            gate_out(stream(6), 0, sg[0][:, 0:4, :])
            gate_out(stream(7), 1, sg[0][:, 4:8, :])
            decay_exp(0, 0, 1)

            def mamba_step(g, b, turn):
                k, o = 2 * g + 6, 1 - b
                decay_exp(g + 1, o, 0)
                raw_out(step_chunk(turn, b, 0), k, 0)
                decay_exp(g + 1, o, 1)
                squares(g)
                raw_out(step_chunk(turn, b, 1), k + 1, 1)
                conv_silu(k, 0, xc[o][:, 0:4, :])
                gate_out(step_chunk(turn, b, 2), 0, sg[o][:, 0:4, :])
                gate_out(step_chunk(turn, b, 3), 1, sg[o][:, 4:8, :])
                conv_silu(k + 1, 1, xc[o][:, 4:8, :])

            with act.Fori(0, 3) as turn:
                for b in range(2):
                    mamba_step(turn * 2 + b, b, turn)
            mamba_step(6, 0, 3)
            squares(7)
            act.wait_ge(var_s, 3)
            nc.scalar.activation(rstd[:, 1:2], rstd[:, 0:1], ACT.Sqrt).then_inc(var_s, 1)

            norm_sqrt(2)
            norm_evac(2, 7)
            act.wait_ge(f_pe, 1)
            copy(r1_sb[:], ps[0:16, 6, 0:T]).then_inc(f_act, 1)
            for i in range(4):
                w = min(4, NFT - 4 * i)
                act.wait_ge(f_pe, 3 + i)
                copy(hsel_t[:, 4 * i:4 * i + w, :],
                     ps[:, i, 0:w * T].rearrange("p (c t) -> p c t", t=T)).then_inc(f_act, 1)

        @block.vector
        def _(dve):
            sub = lambda dst, a, hi: nc.vector.tensor_tensor(dst, a, hi, ALU.subtract)

            def norm(k):
                nc.vector.bn_stats(stats[:], res[:]).then_inc(ln, 1)
                dve.wait_ge(ln, 8 * k + 1)
                nc.vector.bn_aggr(mean_var[:], stats[:]).then_inc(ln, 1)
                dve.wait_ge(ln, 8 * k + 2)
                nc.vector.tensor_scalar(rstd[:, 0:1], mean_var[:, 1:2], EPS, None, ALU.add).then_inc(ln, 1)
                dve.wait_ge(ln, 8 * k + 4)
                nc.vector.reciprocal(rstd[:, 2:3], rstd[:, 1:2]).then_inc(ln, 1)
                dve.wait_ge(ln, 8 * k + 5)
                nc.vector.tensor_scalar(normed[:], res[:], mean_var[:, 0:1], rstd[:, 2:3],
                                        ALU.subtract, ALU.mult).then_inc(ln, 1)

            def split_first(c):
                dve.wait_ge(first_hi, 2 * c + 1)
                sub(wkv_lo[:, 0, c, :], ring[0][:, c * DM:(c + 1) * DM],
                    wkv_hi[:, 0, c, :].bitcast(F32)).then_inc(first_lo, 1)
                dve.wait_ge(first_hi, 2 * c + 2)
                sub(ctx_lo[0][:, c, :], ring[2][:, c * DM:(c + 1) * DM],
                    ctx_hi[0][:, c, :].bitcast(F32)).then_inc(first_lo, 1)

            def split_wv():
                dve.wait_ge(w_hi, 1)
                sub(wkv_lo[:, 1], ring[1][:].rearrange("p (c n) -> p c n", c=NC),
                    wkv_hi[:, 1].bitcast(F32)).then_inc(w_lo, 1)
                dve.wait_ge(w_lo, 1)
                dve.sem_inc(freed[1], 1)

            def k_split(i):
                a, b = chunk_cols(i)
                dve.wait_ge(kh_ok, i + 1)
                sub(k_lo[:, a:b], k_flat[:, a:b], k_hi[:, a:b].bitcast(F32)).then_inc(kl_ok, 1)

            def split_ctx(j):
                s = (2, 3, 0, 1)[j]
                dve.wait_ge(c_hi, j + (j == 3))
                if j >= 2:
                    dve.wait_ge(kv_ps, 8 * (j - 1))
                sub(ctx_lo[j % 2][:], ring[s][:].rearrange("p (c n) -> p c n", c=NC),
                    ctx_hi[j % 2][:].bitcast(F32)).then_inc(c_lo, 1)
                dve.wait_ge(c_lo, j + (j == 3))
                dve.sem_inc(freed[s], 1)

            def k_out(j):
                for kv in range(KVH):
                    dve.wait_ge(kv_ps, 8 * j + 1 + kv)
                    nc.vector.tensor_copy(k_all[:, kv, BANK * j:BANK * j + BANK], ps[:, kv, :]).then_inc(k_ev, 1)

            dve.sem_inc(wo_ev, 2)
            for c in range(NC):
                split_first(c)
            dve.wait_ge(first_lo, 2 * NC)
            dve.sem_inc(freed[0], 1)
            dve.sem_inc(freed[2], 1)
            split_wv()
            split_ctx(1)
            dve.wait_ge(x_in, 16)
            norm(0)
            k_out(0)
            split_ctx(2)
            k_out(1)
            k_split(0)
            k_split(1)
            dve.wait_ge(c_hi, 3)
            sub(lat_lo[:], norm_t[:], lat_hi[:].bitcast(F32)).then_inc(c_lo, 1)
            split_ctx(3)
            k_out(2)
            k_out(3)
            k_split(2)
            k_split(3)
            dve.wait_ge(kv_ps, 33)
            nc.vector.tensor_copy(k_all[:, :, S_CTX:KV_LEN],
                                  ps[:, 0, :].rearrange("p (k t) -> p k t", k=KVH)).then_inc(k_ev, 1)

            def q_split(m, slot, bank):
                dve.wait_ge(qh_ok, m + 1)
                sub(q_lo[slot][:], ps[:, bank, 0:2 * P], q_hi[slot][:].bitcast(F32)).then_inc(ql_ok, 1)

            def scores_out(m, b, c):
                h, i = c // NCHUNK, c % NCHUNK
                lo, hi = chunk_cols(i)
                dve.wait_ge(s_ps, 10 * m + c + 1)
                nc.vector.tensor_scalar(prob[b][:, h, lo:hi], ps[:, c % 4, 0:hi - lo], SCALE, None,
                                        ALU.mult, ALU.max, accum_out=chunk_max[:, b, h, i:i + 1]).then_inc(s_ev, 1)
                if i == NCHUNK - 1:
                    dve.wait_ge(s_ev, 10 * m + c + 1)
                    nc.vector.tensor_reduce(neg_max[:, b, h:h + 1], chunk_max[:, b, h, :], AX_X, ALU.max,
                                            negate=True).then_inc(nm_ok, 1)

            def invert(m, b):
                dve.wait_ge(exp_ok, 2 * NPC * (m + 1))
                nc.vector.tensor_reduce(row_sum[:, b, :], part_sum[:, b, :, :], AX_X, ALU.add).then_inc(sum_ok, 1)
                dve.wait_ge(sum_ok, m + 1)
                nc.vector.reciprocal(row_inv[:, b, :], row_sum[:, b, :]).then_inc(inv_ok, 1)

            def pt_split(unit, u, bank):
                w = 2 if u < 8 else 1
                dve.wait_ge(pth_ok, unit + 1)
                sub(pt_lo[u % 3][:, 0:w, :], ps[:, bank, 0:w * 256].rearrange("p (w n) -> p w n", w=w),
                    pt_hi[u % 3][:, 0:w, :].bitcast(F32)).then_inc(ptl_ok, 1)

            def o_split(m, b):
                dve.wait_ge(oh_ok, m + 1)
                sub(o_lo[:], ps[:, 6 + b, 0:2 * P], o_hi[:].bitcast(F32)).then_inc(ol_ok, 1)

            def add_heads(m, b, h):
                dve.wait_ge(inv_ok, m + 1)
                dve.wait_ge(wo_ev, 2 * m + h + 2)
                dve.wait_ge(wo_ps, 2 * m + h + 1)
                nc.vector.scalar_tensor_tensor(res[:], ps[:, 2 + h, :], row_inv[:, b, h:h + 1], res[:],
                                               ALU.mult, ALU.add).then_inc(wo_ev, 1)

            def attn_step(kv, p, first, last):
                n = kv * PAIRS + p
                b = p % 2
                turn = p == PAIRS - 1
                for u in range(UNITS):
                    tgt = u + 2
                    if tgt < UNITS or not (last and turn):
                        pt_split(9 * n + tgt, tgt % UNITS, 4 + (9 * p + tgt) % 2)
                    if u == 0 and not first:
                        o_split(n - 1, 1 - b)
                    if u in ADD_UNITS and not first:
                        add_heads(n - 1, 1 - b, u - ADD_UNITS[0])
                    if u == Q_UNIT + 1 and not (last and p >= 2):
                        q_split(n + 2, b, 6 + (1 - b))
                    if u < 5 and not (last and turn):
                        scores_out(n + 1, 1 - b, 2 * u)
                        scores_out(n + 1, 1 - b, 2 * u + 1)
                if not (last and turn):
                    invert(n + 1, 1 - b)

            q_split(0, 0, 7)
            scores_out(0, 0, 0)
            k_split(NCHUNK - 1)
            q_split(1, 1, 6)
            for c in range(1, 10):
                scores_out(0, 0, c)
            invert(0, 0)
            pt_split(0, 0, 4)
            pt_split(1, 1, 5)
            attn_step(0, 0, True, False)
            with dve.Fori(0, KVH - 1) as kv:
                for p in range(1, PAIRS):
                    attn_step(kv, p, False, False)
                attn_step(kv + 1, 0, False, False)
            for p in range(1, PAIRS):
                attn_step(KVH - 1, p, False, True)
            o_split(KVH * PAIRS - 1, 1)
            add_heads(KVH * PAIRS - 1, 1, 0)
            add_heads(KVH * PAIRS - 1, 1, 1)

            dve.wait_ge(wo_ev, 2 * KVH * PAIRS + 2)
            norm(1)
            dve.wait_ge(pool_const, 6)
            nc.vector.tensor_copy(upper_r[:], upper[:]).then_inc(pool_const, 1)
            nc.vector.tensor_copy(rank[:], rank_i[:]).then_inc(pool_const, 1)
            nc.vector.memset(o_acc[:], 0.0).then_inc(oacc_ok, 1)

            dve.wait_ge(dt_ps, 1)
            dve.wait_ge(const_in, 160)
            z, zabs, exp_z, ratio, s2, exp_a = softplus
            nc.vector.tensor_tensor(z[:], ps[:, 6, 0:NH], dtb[:], ALU.add).then_inc(dts, 1)
            dve.wait_ge(dts, 1)
            nc.vector.scalar_tensor_tensor(zabs[:], z[:], -1.0, z[:], ALU.mult, ALU.max).then_inc(dts, 1)
            dve.wait_ge(dts, 3)
            nc.vector.tensor_scalar(zabs[:], exp_z[:], 2.0, None, ALU.add).then_inc(dts, 1)
            dve.wait_ge(dts, 4)
            nc.vector.reciprocal(s2[:], zabs[:]).then_inc(dts, 1)
            dve.wait_ge(dts, 5)
            nc.vector.tensor_tensor(ratio[:], exp_z[:], s2[:], ALU.mult).then_inc(dts, 1)
            dve.wait_ge(dts, 6)
            nc.vector.tensor_tensor(s2[:], ratio[:], ratio[:], ALU.mult).then_inc(dts, 1)
            dve.wait_ge(dts, 7)
            nc.vector.tensor_scalar(zabs[:], s2[:], 1.0 / 17, None, ALU.mult).then_inc(dts, 1)
            k = 8
            for odd in (15, 13, 11, 9, 7, 5, 3):
                dve.wait_ge(dts, k)
                nc.vector.scalar_tensor_tensor(zabs[:], zabs[:], 1.0 / odd, s2[:], ALU.add,
                                               ALU.mult).then_inc(dts, 1)
                k += 1
            dve.wait_ge(dts, k)
            nc.vector.scalar_tensor_tensor(zabs[:], zabs[:], 1.0, ratio[:], ALU.add, ALU.mult).then_inc(dts, 1)
            dve.wait_ge(dts, k + 1)
            nc.vector.tensor_scalar(z[:], z[:], 0.0, None, ALU.max).then_inc(dts, 1)
            dve.wait_ge(dts, k + 2)
            nc.vector.scalar_tensor_tensor(dt[:], zabs[:], 2.0, z[:], ALU.mult, ALU.add).then_inc(dts, 1)
            dve.wait_ge(dts, k + 3)
            dve.wait_ge(a_ok, 1)
            nc.vector.scalar_tensor_tensor(a_f[:], exp_a[:], -1.0, dt[:], ALU.mult, ALU.mult).then_inc(dts, 1)
            dve.wait_ge(dts, k + 4)
            nc.vector.tensor_copy(a_hi[:], a_f[:]).then_inc(dts, 1)
            dve.wait_ge(dts, k + 5)
            sub(a_lo[:], a_f[:], a_hi[:].bitcast(F32)).then_inc(a_ok, 1)

            def conv(k, slot, tile):
                r, a = raw[slot], acc[slot]
                for i in range(4):
                    ins = nc.vector.tensor_scalar(a[:, i, :], r[:, i, :], cw[:, bass.ds(tile + i, 1), 3:4].rearrange("p a b -> p (a b)"),
                                                  cb[:, bass.ds(tile + i, 1)], ALU.mult, ALU.add)
                    ins.then_inc(conv_ok, 1)
                for back in range(1, 4):
                    for i in range(4):
                        dve.wait_ge(conv_ok, 16 * k + 4 * (back - 1) + i + 1)
                        ins = nc.vector.scalar_tensor_tensor(
                            a[:, i, back:], r[:, i, 0:T - back],
                            cw[:, bass.ds(tile + i, 1), 3 - back:4 - back].rearrange("p a b -> p (a b)"),
                            a[:, i, back:], ALU.mult, ALU.add)
                        ins.then_inc(conv_ok, 1)
                dve.wait_ge(conv_ok, 16 * k + 16)
                dve.sem_inc(taps, 1)

            def taps_of(q, k, slot, tile):
                dve.wait_ge(proj_ev, q + 1)
                if not (isinstance(k, int) and k < 2):
                    dve.wait_ge(silu_ok, k - 1)
                conv(k, slot, tile)

            def mask_decay(g, b, half):
                dve.wait_ge(dec_ok, 2 * g + half + 1)
                d = decay[b][:, 8 * half:8 * half + 8, :]
                nc.vector.tensor_tensor(d, d, gm[:, bass.ds(g, 1), :].to_broadcast([P, 8, T]),
                                        ALU.mult).then_inc(m_ok, 1)

            def x_times_dt(g):
                dve.wait_ge(xt_ps, g + 1)
                nc.vector.tensor_tensor(xdt[:], ps[:, 4:6, :].rearrange("p a (h c) -> p (a h) c", c=64),
                                        dt[:, bass.ds(g * HPG, HPG)].unsqueeze(2).to_broadcast([P, HPG, 64]),
                                        ALU.mult).then_inc(xdt_ok, 1)

            def skip_add(g, b):
                dve.wait_ge(y_ps, g + 1)
                for t in range(TPG):
                    ins = nc.vector.scalar_tensor_tensor(
                        yv[:, t, :], xc[b][:, t, :], dskip[:, bass.ds(g * TPG + t, 1)],
                        ps[:, 4 + t // 4, (t % 4) * T:(t % 4 + 1) * T], ALU.mult, ALU.add)
                ins.then_inc(y_ok, 1)
                dve.wait_ge(y_ok, g + 1)
                for t in range(TPG):
                    ins = nc.vector.scalar_tensor_tensor(
                        ug[:, t, :], yv[:, t, :], nw[:, bass.ds(g * TPG + t, 1)], sg[b][:, t, :],
                        ALU.mult, ALU.mult)
                ins.then_inc(ug_ok, 1)

            def add_out(g, chunk):
                dve.wait_ge(freed[chunk[0]], chunk[1] + 1)
                dve.wait_ge(oacc_ok, g + 1)
                nc.vector.tensor_tensor(o_acc[:], o_acc[:], ps[:, 6, :], ALU.add).then_inc(oacc_ok, 1)

            for k in range(4):
                taps_of(k, k, k % 2, 64 + 4 * k)
            taps_of(4, 4, 0, 0)
            taps_of(5, 5, 1, 4)
            dve.wait_ge(gm_ps, 1)
            nc.vector.tensor_tensor(gm[:], ps[:, 4:6, :].rearrange("p a (g t) -> p (a g) t", t=T),
                                    causal[:].unsqueeze(1).to_broadcast([P, GROUPS, T]),
                                    ALU.mult).then_inc(gm_ok, 1)
            dve.wait_ge(gm_ok, 1)
            mask_decay(0, 0, 0)
            mask_decay(0, 0, 1)

            def mamba_step(g, b, turn):
                q, k, o = 4 * g + 8, 2 * g + 6, 1 - b
                x_times_dt(g)
                mask_decay(g + 1, o, 0)
                taps_of(q, k, 0, 8 * g + 8)
                mask_decay(g + 1, o, 1)
                skip_add(g, b)
                taps_of(q + 1, k + 1, 1, 8 * g + 12)
                add_out(g, step_chunk(turn, b, 5))

            with dve.Fori(0, 3) as turn:
                for b in range(2):
                    mamba_step(turn * 2 + b, b, turn)
            mamba_step(6, 0, 3)
            x_times_dt(7)
            skip_add(7, 1)
            dve.wait_ge(sq_ok, GROUPS + 1)
            nc.vector.tensor_reduce(sq_tok[:], sq_sum[:].rearrange("p c t -> p t c"), AX_X,
                                    ALU.add).then_inc(var_s, 1)
            dve.wait_ge(var_s, 2)
            nc.vector.tensor_scalar(rstd[:, 0:1], ps[:, 7, 0:1], 1.0 / INTER, EPS, ALU.mult,
                                    ALU.add).then_inc(var_s, 1)
            add_out(7, step_chunk(3, 1, 1))
            dve.wait_ge(var_s, 4)
            nc.vector.reciprocal(rstd[:, 2:3], rstd[:, 1:2]).then_inc(var_s, 1)
            dve.wait_ge(var_s, 5)
            dve.wait_ge(oacc_ok, GROUPS + 1)
            nc.vector.scalar_tensor_tensor(res[:], o_acc[:], rstd[:, 2:3], res[:], ALU.mult,
                                           ALU.add).then_inc(res_ok, 1)
            dve.wait_ge(res_ok, 1)

            norm(2)
            inter = ps[:, 0:4, :].rearrange("p a n -> p (a n)")[:, 0:FF]
            blocks = inter.rearrange("p (n j) -> p n j", j=BLK)
            dve.wait_ge(f_pe, 2)
            nc.vector.tensor_reduce(bmax[:], blocks, AX_X, ALU.max).then_inc(f_mask, 1)
            dve.wait_ge(f_mask, 1)
            nc.vector.tensor_tensor(key, blocks, bmax[:].unsqueeze(2).to_broadcast([P, NBLK, BLK]),
                                    ALU.is_equal).then_inc(f_mask, 1)
            dve.wait_ge(f_mask, 2)
            nc.vector.tensor_tensor(key, key, rank[:].unsqueeze(1).to_broadcast([P, NBLK, BLK]),
                                    ALU.mult).then_inc(f_mask, 1)
            dve.wait_ge(f_mask, 3)
            nc.vector.tensor_reduce(kmax[:], key, AX_X, ALU.max).then_inc(f_mask, 1)
            dve.wait_ge(f_mask, 4)
            nc.vector.tensor_tensor(key, key, kmax[:].unsqueeze(2).to_broadcast([P, NBLK, BLK]),
                                    ALU.is_equal).then_inc(f_mask, 1)
            dve.wait_ge(f_mask, 5)
            dve.wait_ge(freed[stream(FFN0 + 3)[0]], stream(FFN0 + 3)[1] + 1)
            key_flat = decay[0][:, 0:FF // T, :].rearrange("p a b -> p (a b)")
            for i in range(4):
                lo, hi = i * BANK, min(i * BANK + BANK, FF)
                nc.vector.scalar_tensor_tensor(hsel[:, lo:hi], ps[:, 4 + i, 0:hi - lo], 0.0, key_flat[:, lo:hi],
                                               ALU.max, ALU.mult).then_inc(f_dve, 1)
            dve.wait_ge(f_pe, 7)
            nc.vector.tensor_tensor(final[:], res[:], ps[:, 4, :], ALU.add).then_inc(f_dve, 2)

        @block.tensor
        def _(pe):
            mm = nc.tensor.matmul

            def norm_transpose(k, bank):
                pe.wait_ge(ln, 8 * k + 6)
                for c in range(NC):
                    ins = nc.tensor.transpose(ps[:, bank, c * P:c * P + P], normed[:, c * P:c * P + P], ident[:])
                ins.then_inc(ln, 1)

            def split_product(dst, a_hi_, a_lo_, b_hi_, b_lo_, first, last):
                mm(dst, a_hi_, b_hi_, start=first, stop=False)
                mm(dst, a_lo_, b_hi_, start=False, stop=False)
                return mm(dst, a_hi_, b_lo_, start=False, stop=last)

            def project(j):
                ch, cl = ctx_hi[j % 2], ctx_lo[j % 2]
                if j == 0:
                    for c in range(NC):
                        pe.wait_ge(first_lo, 2 * c + 2)
                        for kv in range(KVH):
                            ins = split_product(ps[:, kv, :], wkv_hi[:, 0, c, kv * P:kv * P + P],
                                                wkv_lo[:, 0, c, kv * P:kv * P + P], ch[:, c, :], cl[:, c, :],
                                                c == 0, c == NC - 1)
                            if c == NC - 1:
                                ins.then_inc(kv_ps, 1)
                else:
                    pe.wait_ge(c_lo, j + (j == 3))
                    for kv in range(KVH):
                        pe.wait_ge(k_ev, 4 * (j - 1) + kv + 1)
                        if j == 2 and kv == 2:
                            pe.wait_ge(ln, 8)
                        for c in range(NC):
                            ins = split_product(ps[:, kv, :], wkv_hi[:, 0, c, kv * P:kv * P + P],
                                                wkv_lo[:, 0, c, kv * P:kv * P + P], ch[:, c, :], cl[:, c, :],
                                                c == 0, c == NC - 1)
                        ins.then_inc(kv_ps, 1)
                pe.wait_ge(w_lo, 1)
                for t in range(4):
                    if j:
                        pe.wait_ge(v_ev, 4 * (j - 1) + t + 1)
                    for c in range(NC):
                        ins = split_product(ps[:, 4 + t, :], ch[:, c, t * P:t * P + P], cl[:, c, t * P:t * P + P],
                                            wkv_hi[:, 1, c, :], wkv_lo[:, 1, c, :], c == 0, c == NC - 1)
                    ins.then_inc(kv_ps, 1)

            project(0)
            project(1)
            pe.wait_ge(ident_ok, 2)
            pe.wait_ge(k_ev, 7)
            norm_transpose(0, 2)
            project(2)
            project(3)
            pe.wait_ge(c_lo, 3)
            pe.wait_ge(k_ev, 13)
            for kv in range(KVH):
                for c in range(NC):
                    ins = split_product(ps[:, 0, kv * P:kv * P + P], wkv_hi[:, 0, c, kv * P:kv * P + P],
                                        wkv_lo[:, 0, c, kv * P:kv * P + P], lat_hi[:, c, :], lat_lo[:, c, :],
                                        c == 0, c == NC - 1)
            ins.then_inc(kv_ps, 1)
            pe.wait_ge(k_ev, 14)
            for c in range(NC):
                ins = split_product(ps[:, 1, :], lat_hi[:, c, :], lat_lo[:, c, :], wkv_hi[:, 1, c, :],
                                    wkv_lo[:, 1, c, :], c == 0, c == NC - 1)
            ins.then_inc(kv_ps, 1)

            def queries(m, kv, p, bank):
                s = 2 + p // 2
                if p % 2 == 0:
                    pe.wait_ge(landed[s], kv * 16 + 32)
                w = ring[s][:].rearrange("p (c n) -> p c n", c=NC)
                for h in range(2):
                    col = ((p % 2) * 2 + h) * P
                    for c in range(NC):
                        ins = mm(ps[:, bank, h * P:h * P + P], w[:, c, col:col + P], norm_t[:, c, :],
                                 start=(c == 0), stop=(c == NC - 1))
                ins.then_inc(q_ps, 1)

            def queries_done(m, p):
                pe.wait_ge(q_ps, m + 1)
                pe.sem_inc(freed[2 + p // 2], 1)

            def scores(m, qslot, c):
                h, i = c // NCHUNK, c % NCHUNK
                lo, hi = chunk_cols(i)
                early = isinstance(m, int) and m < 2
                if c >= 4:
                    pe.wait_ge(s_ev, 10 * m + c - 3)
                elif c < 2 and not (early and m == 0):
                    pe.wait_ge(s_ev, 10 * m - 1 + c)
                elif c >= 2 and not early:
                    pe.wait_ge(wo_ev, 2 * m - 5 + c)
                split_product(ps[:, c % 4, 0:hi - lo], q_hi[qslot][:, h * P:h * P + P],
                              q_lo[qslot][:, h * P:h * P + P], k_hi[:, lo:hi], k_lo[:, lo:hi],
                              True, True).then_inc(s_ps, 1)

            def output(m, h):
                if h == 0:
                    pe.wait_ge(ol_ok, m + 1)
                    pe.wait_ge(wol_ok, m + 1)
                if not (isinstance(m, int) and m >= KVH * PAIRS - 2):
                    pe.wait_ge(s_ev, 10 * (m + 2) + 7 + h)
                else:
                    pe.wait_ge(wo_ev, 2 * m + h + 1)
                split_product(ps[:, 2 + h, :], o_hi[:, h * P:h * P + P], o_lo[:, h * P:h * P + P],
                              wo_hi[:, h, :], wo_lo[:, h, :], True, True).then_inc(wo_ps, 1)

            def transposes(pair, unit, b, u, bank):
                if u in (2, 4, 6):
                    pe.wait_ge(exp_ok, 2 * NPC * pair + NPC + u // 2 + 1)
                for w in range(2 if u < 8 else 1):
                    for h in range(2):
                        kt = 2 * u + w
                        at = w * 256 + h * P
                        ins = nc.tensor.transpose(ps[:, bank, at:at + P], prob[b][:, h, kt * P:kt * P + P], ident[:])
                ins.then_inc(t_ps, 1)

            def values(unit, b, u, fresh):
                pe.wait_ge(ptl_ok, unit + 1)
                if fresh is not None and u % 3 == 0:
                    pe.wait_ge(vl_ok, 3 * fresh + u // 3 + 1)
                for w in range(2 if u < 8 else 1):
                    kt = 2 * u + w
                    ins = split_product(ps[:, 6 + b, 0:256], v_hi[:, kt, :], v_lo[:, kt, :],
                                        pt_hi[u % 3][:, w, :], pt_lo[u % 3][:, w, :], kt == 0, kt == NKT - 1)
                ins.then_inc(pv_ps, 1)

            def attn_step(kv, p, first, last):
                n = kv * PAIRS + p
                b = p % 2
                turn = p == PAIRS - 1
                for u in range(UNITS):
                    tgt = u + 2
                    if tgt < UNITS:
                        pe.wait_ge(ptl_ok, 9 * n + u + 1)
                        transposes(n, 9 * n + tgt, b, tgt, 4 + (9 * p + tgt) % 2)
                    elif not (last and turn):
                        pe.wait_ge(ptl_ok, 9 * n + u + 1)
                        if u == 7:
                            pe.wait_ge(exp_ok, 2 * NPC * (n + 1) + NPC + 1)
                        transposes(n + 1, 9 * (n + 1) + tgt - UNITS, 1 - b, tgt - UNITS, 4 + (9 * p + tgt) % 2)
                    if u == 0:
                        if last and turn:
                            pe.wait_ge(ol_ok, n - 1)
                        else:
                            pe.wait_ge(ql_ok, n + 2)
                    values(9 * n + u, b, u, kv if p == 0 else None)
                    if u < 5 and not (last and turn):
                        for c in (2 * u, 2 * u + 1):
                            if turn and c < NCHUNK:
                                pe.wait_ge(kl_ok, NCHUNK * (kv + 1) + c + 1)
                            scores(n + 1, 1 - b, c)
                    if not (last and p >= 2):
                        if u == Q_UNIT:
                            if not first:
                                pe.wait_ge(ol_ok, n)
                            queries(n + 2, kv + (p >= 2), (p + 2) % 4, 6 + (1 - b))
                        if u == Q_UNIT + 2 and p % 2 == 1:
                            queries_done(n + 2, (p + 2) % 4)
                    if u in OUT_UNITS and not first:
                        output(n - 1, u - OUT_UNITS[0])

            pe.wait_ge(v_ev, 16)
            pe.wait_ge(ln, 8)
            pe.sem_inc(pv_ps, 1)
            queries(0, 0, 0, 7)
            queries(1, 0, 1, 6)
            queries_done(1, 1)
            pe.wait_ge(k_ev, 17)
            pe.wait_ge(v_ev, 17)
            pe.wait_ge(ql_ok, 1)
            for c in range(10):
                if c < NCHUNK:
                    pe.wait_ge(kl_ok, c + 1)
                scores(0, 0, c)
            pe.wait_ge(exp_ok, NPC + 1)
            transposes(0, 0, 0, 0, 4)
            transposes(0, 1, 0, 1, 5)
            attn_step(0, 0, True, False)
            with pe.Fori(0, KVH - 1) as kv:
                for p in range(1, PAIRS):
                    attn_step(kv, p, False, False)
                attn_step(kv + 1, 0, False, False)
            for p in range(1, PAIRS):
                attn_step(KVH - 1, p, False, True)
            output(KVH * PAIRS - 1, 0)
            output(KVH * PAIRS - 1, 1)

            norm_transpose(1, 7)

            pe.wait_ge(ln, 16)
            pe.wait_ge(const_in, 160)
            for c in range(NC):
                ins = mm(ps[:, 6, 0:NH], norm_t[:, c, :], w_dt_sb[:, c, :], start=(c == 0), stop=(c == NC - 1))
            ins.then_inc(dt_ps, 1)

            def in_proj(slot, loads, q, bank):
                pe.wait_ge(landed[slot], loads * 16)
                if not (isinstance(q, int) and q < 2):
                    pe.wait_ge(proj_ev, q - 1)
                w = ring[slot][:].rearrange("p (t c n) -> p t c n", t=4, c=NC)
                for t in range(4):
                    for c in range(NC):
                        ins = mm(ps[:, bank, t * T:t * T + T], w[:, t, c, :], norm_t[:, c, :],
                                 start=(c == 0), stop=(c == NC - 1))
                ins.then_inc(freed[slot], 1)

            def segments(g, b, half):
                if not (isinstance(g, int) and g == 0 and half == 0):
                    pe.wait_ge(dec_ok, 2 * g + half)
                pe.wait_ge(at_ok, g + 1)
                for i in range(2):
                    h = 8 * half + 4 * i
                    mm(ps[:, 2 + i, :], upper_r[:], at_hi[:, h:h + 4, :].rearrange("p h t -> p (h t)"), start=True, stop=False)
                    ins = mm(ps[:, 2 + i, :], upper_r[:], at_lo[:, h:h + 4, :].rearrange("p h t -> p (h t)"), start=False, stop=True)
                ins.then_inc(seg_ps, 1)

            def x_transposes(g, b):
                pe.wait_ge(silu_ok, 2 * g + 6)
                if not (isinstance(g, int) and g == 0):
                    pe.wait_ge(y_ok, g)
                for t in range(TPG):
                    ins = nc.tensor.transpose(ps[:, 4 + t // 4, (t % 4) * T:(t % 4 + 1) * T], xc[b][:, t, :], ident[:])
                ins.then_inc(xt_ps, 1)

            def y_product(g, b):
                pe.wait_ge(xdt_ok, g + 1)
                pe.wait_ge(m_ok, 2 * g + 2)
                for h in range(HPG):
                    t = h // 2
                    ins = mm(ps[(h % 2) * 64:(h % 2) * 64 + 64, 4 + t // 4, (t % 4) * T:(t % 4 + 1) * T],
                             xdt[:, h, :], decay[b][:, h, :], start=True, stop=True)
                ins.then_inc(y_ps, 1)

            def out_proj(g, chunks):
                pe.wait_ge(ug_ok, g + 1)
                if not (isinstance(g, int) and g == 0):
                    pe.wait_ge(oacc_ok, g + 1)
                for i, (slot, loads) in enumerate(chunks):
                    pe.wait_ge(landed[slot], loads * 16)
                    w = ring[slot][:].rearrange("p (t n) -> p t n", t=4)
                    for t in range(4):
                        ins = mm(ps[:, 6, :], ug[:, 4 * i + t, :], w[:, t, :], start=(i == 0 and t == 0),
                                 stop=(i == 1 and t == 3))
                    ins.then_inc(freed[slot], 1)

            for m in range(6):
                in_proj(stream(m)[0], stream(m)[1] + 1, m, m % 2)
            pe.wait_ge(silu_ok, 4)
            for g in range(GROUPS):
                ins = mm(ps[:, 4 + g // 4, (g % 4) * T:(g % 4 + 1) * T], bc[:, g, :], bc[:, 8 + g, :],
                         start=True, stop=True)
            ins.then_inc(gm_ps, 1)
            pe.wait_ge(pool_const, 7)
            segments(0, 0, 0)
            for m in range(6, 8):
                in_proj(stream(m)[0], stream(m)[1] + 1, m, m % 2)
            segments(0, 0, 1)
            pe.wait_ge(gm_ok, 1)

            def mamba_step(g, b, turn, last):
                q = 4 * g + 8
                chunks = [(slot, before + 1) for slot, before in (step_chunk(turn, b, j) for j in range(6))]
                x_transposes(g, b)
                if last:
                    y_product(g, b)
                    out_proj(g, chunks[0:2])
                    return
                segments(g + 1, 1 - b, 0)
                in_proj(*chunks[0], q, 0)
                segments(g + 1, 1 - b, 1)
                y_product(g, b)
                in_proj(*chunks[1], q + 1, 1)
                in_proj(*chunks[2], q + 2, 0)
                in_proj(*chunks[3], q + 3, 1)
                out_proj(g, chunks[4:6])

            with pe.Fori(0, 3) as turn:
                for b in range(2):
                    mamba_step(turn * 2 + b, b, turn, False)
            mamba_step(6, 0, 3, False)
            mamba_step(7, 1, 3, True)
            pe.wait_ge(var_s, 1)
            pe.wait_ge(pool_const, 6)
            mm(ps[:, 7, 0:1], sq_tok[:], ones_m[:], start=True, stop=True).then_inc(var_s, 1)

            norm_transpose(2, 7)
            pe.wait_ge(ln, 24)
            for c in range(NC):
                ins = mm(ps[0:16, 6, 0:T], c1_sb[:, c, :], norm_t[:, c, :], start=(c == 0), stop=(c == NC - 1))
            ins.then_inc(f_pe, 1)
            pe.wait_ge(f_act, 1)
            for i in range(4):
                lo, hi = i * BANK, min(i * BANK + BANK, FF)
                ins = mm(ps[:, i, 0:hi - lo], r1_sb[:], c2_sb[:, lo:hi], start=True, stop=True)
            ins.then_inc(f_pe, 1)
            for c in range(NC):
                s, before = stream(FFN0 + c)
                pe.wait_ge(landed[s], 16 * (before + 1))
                for i in range(4):
                    lo, hi = i * BANK, min(i * BANK + BANK, FF)
                    ins = mm(ps[:, 4 + i, 0:hi - lo], norm_t[:, c, :], ring[s][:, lo:hi], start=(c == 0),
                             stop=(c == NC - 1))
                ins.then_inc(freed[s], 1)
            for i in range(4):
                pe.wait_ge(f_dve, i + 1)
                for t in range(4 * i, min(4 * i + 4, NFT)):
                    ins = nc.tensor.transpose(ps[:, i, (t % 4) * T:(t % 4 + 1) * T], hsel[:, t * T:t * T + T], ident[:])
                ins.then_inc(f_pe, 1)
            for i in range(4):
                s, before = stream(FFN0 + 4 + i)
                pe.wait_ge(landed[s], 16 * (before + 1))
                pe.wait_ge(f_act, 2 + i)
                for t in range(4 * i, min(4 * i + 4, NFT)):
                    ins = mm(ps[:, 4, :], hsel_t[:, t, :], ring[s][:, (t % 4) * DM:(t % 4 + 1) * DM],
                             start=(t == 0), stop=(t == NFT - 1))
            ins.then_inc(f_pe, 1)


_NAMES = ["x", "ctx_t", "wq", "wk", "wv", "wo", "w_in", "w_dt", "w_out", "conv_w", "conv_b", "dt_bias",
          "a_log", "d_skip", "norm_w", "c1", "c2", "w1", "w2", "w2_tail"]


def kernel(**inputs):
    import numpy as np
    import concourse.bacc as bacc
    from concourse.bass_utils import run_bass_kernel_spmd

    a = {k: np.asarray(v) for k, v in inputs.items()}

    def tiles(w, n):
        k, cols = w.shape
        return w.reshape(k // 128, 128, cols // n, n).transpose(2, 1, 0, 3).reshape(cols // n, 128, -1)

    def rows(w, r):
        k, cols = w.shape
        return w.reshape(k // (128 * r), r, 128, cols).transpose(0, 2, 1, 3).reshape(-1, 128, r * cols)

    w_in = a["L0_attn_in_proj_w"]
    w_main = w_in[:18432].reshape(36, 4, 128, 4, 128).transpose(0, 4, 1, 3, 2).reshape(36, 128, 2048)
    w2 = a["L0_ffn_w2t"]
    laid = {
        "x": a["x"][0],
        "ctx_t": tiles(a["ctx_4096"][0].T, 512),
        "wq": tiles(a["L0_xattn_Wq"], 512),
        "wk": tiles(a["L0_xattn_Wk"], 512)[0],
        "wv": tiles(a["L0_xattn_Wv"], 512)[0],
        "wo": rows(a["L0_xattn_Wo"], 4),
        "w_in": w_main,
        "w_dt": tiles(w_in[18432:].T, 128).reshape(128, 4, 128),
        "w_out": rows(a["L0_attn_out_proj_w"].T, 4),
        "conv_w": a["L0_attn_conv_w"].reshape(80, 128, 4).transpose(1, 0, 2),
        "conv_b": a["L0_attn_conv_b"].reshape(80, 128).T,
        "dt_bias": a["L0_attn_dt_bias"],
        "a_log": a["L0_attn_A_log"],
        "d_skip": a["L0_attn_D"].reshape(64, 2).T,
        "norm_w": a["L0_attn_norm_w"].reshape(64, 128).T,
        "c1": tiles(a["L0_ffn_c1_w"].T, 16).reshape(128, 4, 16),
        "c2": a["L0_ffn_c2_w"].T,
        "w1": a["L0_ffn_w1"].T.reshape(4, 128, 1792),
        "w2": rows(w2[:1536], 4),
        "w2_tail": rows(w2[1536:], 2),
    }
    nc = bacc.Bacc("TRN2", target_bir_lowering=False, num_devices=1)
    arrays, args = {}, []
    for name in _NAMES:
        v = np.ascontiguousarray(laid[name])
        arrays[f"{name}_dram"] = v
        args.append(nc.dram_tensor(f"{name}_dram", v.shape, mybir.dt.from_np(v.dtype), kind="ExternalInput").ap())
    out = nc.dram_tensor("out_dram", (T, DM), F32, kind="ExternalOutput").ap()
    build(nc, *args, out)
    r = run_bass_kernel_spmd(nc, [arrays], core_ids=[0])
    return r.results[0]["out_dram"].reshape(1, T, DM)
```

```python
from contextlib import ExitStack

import concourse.bass as bass
from concourse import mybir

F32 = mybir.dt.float32
F32R = mybir.dt.float32r
I32 = mybir.dt.int32
ALU = mybir.AluOpType
ACT = mybir.ActivationFunctionType
AX_X = mybir.AxisListType.X

P = 128
T = 128
DM = 512
NC = DM // P
BANK = 512
EPS = 1e-5

S_CTX = 2048
KV_LEN = S_CTX + T
NKT = KV_LEN // P
KVH = 4
HPK = 8
PAIRS = HPK // 2
NCHUNK = 5
UNITS = 9
PIECES = ((0, 512), (512, 1024), (1024, 1536), (1536, 2176))
NPC = len(PIECES)
EXP_AT = ((), (), ((0, 0),), ((0, 1), (0, 2)), ((0, 3),), ((1, 0), (1, 1)), ((1, 2),), ((1, 3),), ())
K_AT = {2: {5: (0,), 6: (1,), 7: (2,), 8: (3,)}, 3: {0: (4,)}}
V_AT = {4: 0, 7: 1}
W_UNIT = 2
OUT_UNITS = (6, 7)
LAST_OUT = (3, 4)
Q_UNIT = 5
V_PARTS = ((0, 6), (6, 12), (12, 17))
SCALE = 128.0 ** -0.5

GROUPS = 8
HPG = 16
TPG = 8
NH = GROUPS * HPG
INTER = NH * 64
FF = 1792
BLK = 32
NBLK = FF // BLK
NFT = FF // P

LN_STEPS = 8

RING = 6
SLOT = 2048
FFN0 = 52


def chunk_cols(c):
    return c * BANK, min((c + 1) * BANK, KV_LEN)


def build(nc, x, ctx_t, wq, wk, wv, wo, w_in, w_dt, w_out, conv_w, conv_b, dt_bias, a_log, d_skip,
          norm_w, c1, c2, w1, w2, w2_tail, out):
    with ExitStack() as ctx:
        def sem(name):
            return ctx.enter_context(nc.semaphore(name))

        def sbuf(stack, name, shape, dt=F32):
            return stack.enter_context(nc.sbuf_tensor(name, shape, dt))

        ring, ring_lo = [], []

        def add_slot(stack, s):
            with ExitStack() as same_place:
                ring_lo.append(sbuf(same_place, f"ring_lo{s}", [P, SLOT], F32R))
            ring.append(sbuf(stack, f"ring{s}", [P, SLOT]))

        for s in range(4):
            add_slot(ctx, s)
        res = sbuf(ctx, "res", [P, DM])
        normed = sbuf(ctx, "normed", [P, DM])
        norm_t = sbuf(ctx, "norm_t", [P, NC, T])
        ident = sbuf(ctx, "ident", [P, P])
        stats = sbuf(ctx, "stats", [P, 6])
        mean_var = sbuf(ctx, "mean_var", [P, 2])
        rstd = sbuf(ctx, "rstd", [P, 3])
        row_inv = sbuf(ctx, "row_inv", [P, 2, 2])
        o_hi = sbuf(ctx, "o_hi", [P, 2 * P], F32R)
        o_lo = sbuf(ctx, "o_lo", [P, 2 * P], F32R)
        wo_hi = sbuf(ctx, "wo_hi", [P, 2, DM], F32R)
        wo_lo = sbuf(ctx, "wo_lo", [P, 2, DM], F32R)

        with ExitStack() as st:
            k_all = sbuf(st, "k_all", [P, KVH, KV_LEN])
            v_all = sbuf(st, "v_all", [P, NKT, KVH * P])
            k_hi = sbuf(st, "k_hi", [P, KV_LEN], F32R)
            k_lo = sbuf(st, "k_lo", [P, KV_LEN], F32R)
            with ExitStack() as st1:
                wkv_hi = sbuf(st1, "wkv_hi", [P, 2, NC, DM], F32R)
                wkv_lo = sbuf(st1, "wkv_lo", [P, 2, NC, DM], F32R)
                ctx_hi = [sbuf(st1, f"ctx_hi{b}", [P, NC, BANK], F32R) for b in range(2)]
                ctx_lo = [sbuf(st1, f"ctx_lo{b}", [P, NC, BANK], F32R) for b in range(2)]
                lat_hi = sbuf(st1, "lat_hi", [P, NC, T], F32R)
                lat_lo = sbuf(st1, "lat_lo", [P, NC, T], F32R)
            with ExitStack() as st2:
                v_hi = sbuf(st2, "v_hi", [P, NKT, P], F32R)
                v_lo = sbuf(st2, "v_lo", [P, NKT, P], F32R)
                prob = [sbuf(st2, f"prob{b}", [P, 2, KV_LEN]) for b in range(2)]
                pt_hi = [sbuf(st2, f"pt_hi{b}", [P, 2, 2 * P], F32R) for b in range(3)]
                pt_lo = [sbuf(st2, f"pt_lo{b}", [P, 2, 2 * P], F32R) for b in range(3)]
                q_hi = [sbuf(st2, f"q_hi{b}", [P, 2 * P], F32R) for b in range(2)]
                q_lo = [sbuf(st2, f"q_lo{b}", [P, 2 * P], F32R) for b in range(2)]
                chunk_max = sbuf(st2, "chunk_max", [P, 2, 2, NCHUNK])
                neg_max = sbuf(st2, "neg_max", [P, 2, 2])
                part_sum = sbuf(st2, "part_sum", [P, 2, 2, NPC])
                row_sum = sbuf(st2, "row_sum", [P, 2, 2])
        with ExitStack() as st3:
            w_dt_sb = sbuf(st3, "w_dt_sb", [P, NC, NH])
            cw = sbuf(st3, "cw", [P, 80, 4])
            cb = sbuf(st3, "cb", [P, 80])
            dskip = sbuf(st3, "dskip", [P, 64])
            nw = sbuf(st3, "nw", [P, 64])
            dtb = sbuf(st3, "dtb", [P, NH])
            alog = sbuf(st3, "alog", [P, NH])
            upper = sbuf(st3, "upper", [P, P])
            causal = sbuf(st3, "causal", [P, P])
            ones_m = sbuf(st3, "ones_m", [P, 1])
            c1_sb = sbuf(st3, "c1_sb", [P, NC, 16])
            c2_sb = sbuf(st3, "c2_sb", [16, FF])
            rank_i = sbuf(st3, "rank_i", [P, BLK], I32)
            sq_sum = sbuf(st3, "sq_sum", [P, TPG, T])
            softplus = [sbuf(st3, f"softplus{i}", [P, NH]) for i in range(6)]
            dt = sbuf(st3, "dt", [P, NH])
            a_f = sbuf(st3, "a_f", [P, NH])
            a_hi = sbuf(st3, "a_hi", [P, NH], F32R)
            a_lo = sbuf(st3, "a_lo", [P, NH], F32R)
            upper_r = sbuf(st3, "upper_r", [P, P], F32R)
            o_acc = sbuf(st3, "o_acc", [P, DM])
            for s in range(4, RING):
                add_slot(st3, s)
            wout_hi = [sbuf(st3, f"wout_hi{b}", [P, SLOT], F32R) for b in range(2)]
            final = sbuf(st3, "final", [P, DM])
            with ExitStack() as st4:
                at_hi = sbuf(st4, "at_hi", [P, HPG, T], F32R)
                at_lo = sbuf(st4, "at_lo", [P, HPG, T], F32R)
                bc = sbuf(st4, "bc", [P, 16, T])
                gm = sbuf(st4, "gm", [P, GROUPS, T])
                raw = [sbuf(st4, f"raw{b}", [P, 4, T]) for b in range(2)]
                acc = [sbuf(st4, f"acc{b}", [P, 4, T]) for b in range(2)]
                xc = [sbuf(st4, "xc0", [P, TPG, T])]
                sg = [sbuf(st4, "sg0", [P, TPG, T])]
                decay = [sbuf(st4, "decay0", [P, HPG, T])]
                xc.append(sbuf(st4, "xc1", [P, TPG, T]))
                sg.append(sbuf(st4, "sg1", [P, TPG, T]))
                decay.append(sbuf(st4, "decay1", [P, HPG, T]))
                xdt = sbuf(st4, "xdt", [P, HPG, 64])
                yv = sbuf(st4, "yv", [P, TPG, T])
                ysq = sbuf(st4, "ysq", [P, TPG, T])
                sq_tok = sbuf(st4, "sq_tok", [P, 2, T])
                ug = sbuf(st4, "ug", [P, TPG, T])
                ug_hi = sbuf(st4, "ug_hi", [P, TPG, T], F32R)
                ug_lo = sbuf(st4, "ug_lo", [P, TPG, T], F32R)
            with ExitStack() as st5:
                w1_hi = sbuf(st5, "w1_hi", [P, NC, FF], F32R)
                w2_hi = sbuf(st5, "w2_hi", [P, NFT, DM], F32R)
                nt_hi = sbuf(st5, "nt_hi", [P, NC, T], F32R)
                nt_lo = sbuf(st5, "nt_lo", [P, NC, T], F32R)
                key_flat = sbuf(st5, "key", [P, FF])
                hsel = sbuf(st5, "hsel", [P, FF])
                hsel_hi = sbuf(st5, "hsel_hi", [P, NFT, T], F32R)
                hsel_lo = sbuf(st5, "hsel_lo", [P, NFT, T], F32R)
                r1_sb = sbuf(st5, "r1_sb", [16, T])
                rank = sbuf(st5, "rank", [P, BLK])
                bmax = sbuf(st5, "bmax", [P, NBLK])
                kmax = sbuf(st5, "kmax", [P, NBLK])
            key = key_flat[:].rearrange("p (n j) -> p n j", j=BLK)

        k_flat = k_all[:, :, :].rearrange("p k n -> p (k n)")
        ps = ctx.enter_context(nc.psum_tensor("ps", [P, 8, BANK], F32))

        landed = [sem(f"landed{s}") for s in range(RING)]
        freed = [sem(f"freed{s}") for s in range(RING)]
        x_in = sem("x_in")
        const_in = sem("const_in")
        ident_ok = sem("ident_ok")
        pool_const = sem("pool_const")
        ln = sem("ln")
        first_in = [sem(f"first_in{c}") for c in range(NC - 1)]
        first_hi, first_lo = sem("first_hi"), sem("first_lo")
        w_hi, w_lo, c_hi, c_lo = sem("w_hi"), sem("w_lo"), sem("c_hi"), sem("c_lo")
        kv_ps, k_ev, v_ev = sem("kv_ps"), sem("k_ev"), sem("v_ev")
        kh_ok, kl_ok, vh_ok, vl_ok = sem("kh_ok"), sem("kl_ok"), sem("vh_ok"), sem("vl_ok")
        q_ps, qh_ok, ql_ok = sem("q_ps"), sem("qh_ok"), sem("ql_ok")
        s_ps, s_ev, nm_ok, exp_ok = sem("s_ps"), sem("s_ev"), sem("nm_ok"), sem("exp_ok")
        t_ps, pth_ok, ptl_ok, pv_ps = sem("t_ps"), sem("pth_ok"), sem("ptl_ok"), sem("pv_ps")
        sum_ok, inv_ok, oh_ok, ol_ok = sem("sum_ok"), sem("inv_ok"), sem("oh_ok"), sem("ol_ok")
        woh_ok, wol_ok, wo_ps, wo_ev = sem("woh_ok"), sem("wol_ok"), sem("wo_ps"), sem("wo_ev")
        res_ok = sem("res_ok")
        dt_ps, dts, a_ok = sem("dt_ps"), sem("dts"), sem("a_ok")
        proj_ev, taps, conv_ok, silu_ok = sem("proj_ev"), sem("taps"), sem("conv_ok"), sem("silu_ok")
        gm_ps, gm_ok, at_ok, seg_ps, dec_ok, m_ok = (sem("gm_ps"), sem("gm_ok"), sem("at_ok"),
                                                     sem("seg_ps"), sem("dec_ok"), sem("m_ok"))
        xt_ps, xdt_ok, y_ps, y_ok, ysq_ok, sq_ok = (sem("xt_ps"), sem("xdt_ok"), sem("y_ps"),
                                                    sem("y_ok"), sem("ysq_ok"), sem("sq_ok"))
        outh_ok, outl_ok, ugh_ok, ugl_ok = sem("outh_ok"), sem("outl_ok"), sem("ugh_ok"), sem("ugl_ok")
        w1h_ok, w1l_ok, w2h_ok, w2l_ok = sem("w1h_ok"), sem("w1l_ok"), sem("w2h_ok"), sem("w2l_ok")
        hsh_ok, hsl_ok = sem("hsh_ok"), sem("hsl_ok")
        nth_ok, ntl_ok = sem("nth_ok"), sem("ntl_ok")
        ug_ok, oacc_ok, var_s = sem("ug_ok"), sem("oacc_ok"), sem("var_s")
        f_pe, f_dve, f_act, f_mask = sem("f_pe"), sem("f_dve"), sem("f_act"), sem("f_mask")
        stored = sem("stored")

        BEFORE = (6, 6, 5, 5, 0, 0)

        def stream(m):
            slot = (m + 2) % RING
            return slot, BEFORE[slot] + m // RING

        def step_chunk(g, j):
            slot, before = stream(8 + j)
            return slot, before + g

        block = ctx.enter_context(nc.Block())

        @block.sync
        def _(sp):
            def load(slot, src, prior):
                if not (isinstance(prior, int) and prior == 0):
                    sp.wait_ge(freed[slot], prior)
                cols = src.shape[-1]
                sp.dma_start(ring[slot][:, 0:cols], src).then_inc(landed[slot], 16)

            for c in range(NC):
                for slot, src in ((0, wk), (2, ctx_t[0])):
                    piece = slice(c * DM, (c + 1) * DM)
                    done = first_in[c] if c < NC - 1 else landed[slot]
                    sp.dma_start(ring[slot][:, piece], src[:, piece]).then_inc(done, 16)
            load(1, wv, 0)
            sp.dma_start(res[:], x).then_inc(x_in, 16)
            load(3, ctx_t[1], 0)
            load(0, ctx_t[2], 1)
            load(1, ctx_t[3], 1)
            load(2, wq[0], 1)
            load(3, wq[1], 1)
            load(0, wo[0], 2)
            load(1, wo[1], 2)
            for kv in range(1, KVH):
                load(2, wq[2 * kv], 1 + kv)
                load(3, wq[2 * kv + 1], 1 + kv)
                load(0, wo[2 * kv], 2 + kv)
                load(1, wo[2 * kv + 1], 2 + kv)
            sp.wait_ge(kl_ok, KVH * NCHUNK)
            sp.dma_start(w_dt_sb[:], w_dt).then_inc(const_in, 16)
            sp.dma_start(dtb[:], dt_bias.unsqueeze(0).to_broadcast([P, NH])).then_inc(const_in, 16)
            sp.dma_start(alog[:], a_log.unsqueeze(0).to_broadcast([P, NH])).then_inc(const_in, 16)
            sp.dma_start(cw[:], conv_w).then_inc(const_in, 16)
            sp.dma_start(cb[:], conv_b).then_inc(const_in, 16)
            sp.dma_start(nw[:], norm_w).then_inc(const_in, 16)
            for half in range(2):
                sp.dma_start(dskip[64 * half:64 * half + 64, :],
                             d_skip[half:half + 1, :].to_broadcast([64, 64])).then_inc(const_in, 16)
            sp.dma_start(c1_sb[:], c1).then_inc(const_in, 16)
            sp.dma_start(c2_sb[:], c2).then_inc(const_in, 16)
            sp.wait_ge(vl_ok, 3 * KVH)
            for m in range(4):
                load(stream(m)[0], w_in[32 + m], stream(m)[1])
            for j in range(2):
                load(stream(4 + j)[0], w_in[16 + j], stream(4 + j)[1])
            for j in range(2):
                load(stream(6 + j)[0], w_in[j], stream(6 + j)[1])

            w_in_rows = w_in.rearrange("n p f -> (n p) f")
            w_out_rows = w_out.rearrange("n p f -> (n p) f")

            def step_loads(g, last):
                ins = [(w_in_rows, 16 + 2 * (g + 1) + i) for i in range(2)] + \
                      [(w_in_rows, 2 * (g + 1) + i) for i in range(2)]
                outs = [(w_out_rows, 2 * g + i) for i in range(2)]
                sources = outs if last else ins + outs
                for j in (0, 1) if last else (0, 1, 2, 4, 5, 3):
                    slot, before = step_chunk(g, j)
                    rows, at = sources[j]
                    load(slot, rows[bass.ds(at * P, P), :], before)

            with sp.Fori(0, 3) as turn:
                for b in range(2):
                    step_loads(turn * 2 + b, False)
            step_loads(6, False)
            step_loads(7, True)
            for c in range(4):
                s, before = stream(FFN0 + c)
                load(s, w1[c], before)
            for c in range(4):
                s, before = stream(FFN0 + 4 + c)
                load(s, w2[c] if c < 3 else w2_tail[0], before)
            sp.wait_ge(f_dve, 6)
            sp.dma_start(out, final[:]).then_inc(stored, 16)
            sp.wait_ge(stored, 16)

        @block.gpsimd
        def _(pool):
            pool.memset(ident[:], 0.0).then_inc(ident_ok, 1)
            pool.wait_ge(ident_ok, 1)
            pool.affine_select(out=ident[:], in_=ident[:], compare_op=ALU.not_equal, fill=1.0, base=0,
                               pattern=[[-1, P]], channel_multiplier=1).then_inc(ident_ok, 1)
            pool.wait_ge(ident_ok, 2)
            sub = lambda dst, a, hi: pool.tensor_tensor(dst, a, hi, ALU.subtract)

            def k_split(kv, i):
                a, b = chunk_cols(i)
                pool.wait_ge(kh_ok, NCHUNK * kv + i + 1)
                sub(k_lo[:, a:b], k_all[:, kv, a:b], k_hi[:, a:b].bitcast(F32)).then_inc(kl_ok, 1)

            def v_split(kv, part):
                a, b = V_PARTS[part]
                pool.wait_ge(vh_ok, 3 * kv + part + 1)
                sub(v_lo[:, a:b, :], v_all[:, a:b, kv * P:kv * P + P],
                    v_hi[:, a:b, :].bitcast(F32)).then_inc(vl_ok, 1)

            def wo_split(m):
                slot, half = m % PAIRS // 2, m % 2
                pool.wait_ge(woh_ok, m + 1)
                sub(wo_lo[:], ring[slot][:, half * 2 * DM:(half + 1) * 2 * DM]
                    .rearrange("p (h n) -> p h n", h=2), wo_hi[:].bitcast(F32)).then_inc(wol_ok, 1)
                if half == 1:
                    pool.wait_ge(wol_ok, m + 1)
                    pool.sem_inc(freed[slot], 1)

            for part in range(3):
                v_split(0, part)
            for n in range(KVH * PAIRS):
                kv, p = n // PAIRS, n % PAIRS
                more = kv < KVH - 1
                if more and p == 3:
                    k_split(kv + 1, 4)
                if n:
                    wo_split(n - 1)
                if more and p == 2:
                    for i in range(4):
                        k_split(kv + 1, i)
                if more and p == 3:
                    for part in range(3):
                        v_split(kv + 1, part)

            pool.wait_ge(kl_ok, KVH * NCHUNK)
            pool.memset(upper[:], 1.0).then_inc(pool_const, 1)
            pool.memset(causal[:], 1.0).then_inc(pool_const, 1)
            pool.memset(ones_m[:], 1.0).then_inc(pool_const, 1)
            pool.iota(rank_i[:], pattern=[[-1, BLK]], base=BLK, channel_multiplier=0).then_inc(pool_const, 1)
            pool.memset(sq_sum[:], 0.0).then_inc(sq_ok, 1)
            pool.wait_ge(pool_const, 4)
            pool.affine_select(out=upper[:], in_=upper[:], compare_op=ALU.is_gt, fill=0.0, base=0,
                               pattern=[[-1, P]], channel_multiplier=1).then_inc(pool_const, 1)
            pool.affine_select(out=causal[:], in_=causal[:], compare_op=ALU.is_ge, fill=0.0, base=0,
                               pattern=[[1, P]], channel_multiplier=-1).then_inc(pool_const, 1)

            def steps_a(g):
                for dst, src in ((at_hi, a_hi), (at_lo, a_lo)):
                    i = pool.affine_select(
                        out=dst[:], in_=src[:, g * HPG:g * HPG + HPG].bitcast(F32).unsqueeze(2).to_broadcast([P, HPG, T]),
                        compare_op=ALU.is_ge, fill=0.0, base=0, pattern=[[0, HPG], [1, T]],
                        channel_multiplier=-1)
                i.then_inc(at_ok, 1)

            def add_squares(g):
                pool.wait_ge(ysq_ok, g + 1)
                pool.wait_ge(sq_ok, g + 1)
                pool.tensor_tensor(sq_sum[:], sq_sum[:], ysq[:], ALU.add).then_inc(sq_ok, 1)

            wo_split(KVH * PAIRS - 1)
            def out_split(g, i):
                slot = step_chunk(g, 4 + i)[0]
                pool.wait_ge(outh_ok, 2 * g + i + 1)
                sub(ring_lo[slot][:], ring[slot][:], wout_hi[i][:].bitcast(F32)).then_inc(outl_ok, 1)

            def ffn_split(m, cols, hi, h_ok, l_ok, count):
                slot = stream(FFN0 + m)[0]
                pool.wait_ge(h_ok, count)
                sub(ring_lo[slot][:, 0:cols], ring[slot][:, 0:cols], hi.bitcast(F32)).then_inc(l_ok, 1)

            pool.wait_ge(a_ok, 2)
            steps_a(0)
            pool.wait_ge(seg_ps, 2)
            steps_a(1)
            for g in range(GROUPS - 1):
                out_split(g, 0)
                out_split(g, 1)
                if g < GROUPS - 2:
                    pool.wait_ge(seg_ps, 2 * g + 4)
                    steps_a(g + 2)
                add_squares(g)
            for c in range(NC):
                ffn_split(c, FF, w1_hi[:, c, :], w1h_ok, w1l_ok, c + 1)
            for i in range(4):
                w = min(4, NFT - 4 * i)
                ffn_split(NC + i, w * DM, w2_hi[:, 4 * i:4 * i + w, :].rearrange("p t n -> p (t n)"),
                          w2h_ok, w2l_ok, i + 1)

        @block.scalar
        def _(act):
            copy = lambda dst, src: nc.scalar.activation(dst, src, ACT.Copy)

            def norm_sqrt(k):
                act.wait_ge(ln, LN_STEPS * k + 3)
                nc.scalar.activation(rstd[:, 1:2], rstd[:, 0:1], ACT.Sqrt).then_inc(ln, 1)

            def norm_evac(k, bank):
                act.wait_ge(ln, LN_STEPS * k + 7)
                copy(norm_t[:], ps[:, bank, :].rearrange("p (c t) -> p c t", c=NC)).then_inc(ln, 1)

            def split_first(c):
                if c < NC - 1:
                    act.wait_ge(first_in[c], 32)
                else:
                    act.wait_ge(landed[0], 16)
                copy(wkv_hi[:, 0, c, :], ring[0][:, c * DM:(c + 1) * DM]).then_inc(first_hi, 1)
                if c == NC - 1:
                    act.wait_ge(landed[2], 16)
                copy(ctx_hi[0][:, c, :], ring[2][:, c * DM:(c + 1) * DM]).then_inc(first_hi, 1)

            def split_wv():
                act.wait_ge(landed[1], 16)
                copy(wkv_hi[:, 1], ring[1][:].rearrange("p (c n) -> p c n", c=NC)).then_inc(w_hi, 1)

            def split_ctx(j):
                s, k = (2, 3, 0, 1)[j], (1, 1, 2, 2)[j]
                act.wait_ge(landed[s], 16 * k)
                if j >= 2:
                    act.wait_ge(kv_ps, 8 * (j - 1))
                copy(ctx_hi[j % 2][:], ring[s][:].rearrange("p (c n) -> p c n", c=NC)).then_inc(c_hi, 1)

            def v_out(j):
                for t in range(4):
                    act.wait_ge(kv_ps, 8 * j + 5 + t)
                    copy(v_all[:, 4 * j + t, :], ps[:, 4 + t, :]).then_inc(v_ev, 1)

            def k_split(kv, i):
                a, b = chunk_cols(i)
                copy(k_hi[:, a:b], k_flat[:, bass.ds(kv * KV_LEN + a, b - a)]).then_inc(kh_ok, 1)

            for c in range(NC):
                split_first(c)
            split_wv()
            split_ctx(1)
            norm_sqrt(0)
            v_out(0)
            split_ctx(2)
            act.wait_ge(k_ev, 5)
            k_split(0, 0)
            k_split(0, 1)
            norm_evac(0, 2)
            act.wait_ge(ln, LN_STEPS)
            copy(lat_hi[:], norm_t[:]).then_inc(c_hi, 1)
            v_out(1)
            split_ctx(3)
            v_out(2)
            act.wait_ge(k_ev, 13)
            k_split(0, 2)
            k_split(0, 3)
            v_out(3)
            act.wait_ge(kv_ps, 34)
            copy(v_all[:, 16, :], ps[:, 1, :]).then_inc(v_ev, 1)

            def v_split(kv, part):
                a, b = V_PARTS[part]
                copy(v_hi[:, a:b, :], v_all[:, a:b, bass.ds(kv * P, P)]).then_inc(vh_ok, 1)

            def q_split(m, slot, bank):
                act.wait_ge(q_ps, m + 1)
                copy(q_hi[slot][:], ps[:, bank, 0:2 * P]).then_inc(qh_ok, 1)

            def soft_exp(m, b, h, i):
                if i == 0:
                    act.wait_ge(nm_ok, 2 * m + h + 1)
                lo, hi = PIECES[i]
                nc.scalar.activation(prob[b][:, h, lo:hi], prob[b][:, h, lo:hi], ACT.Exp,
                                     bias=neg_max[:, b, h:h + 1],
                                     accum_out=part_sum[:, b, h, i:i + 1]).then_inc(exp_ok, 1)

            def pt_split(unit, u, bank):
                w = 2 if u < 8 else 1
                act.wait_ge(t_ps, unit + 1)
                copy(pt_hi[u % 3][:, 0:w, :],
                     ps[:, bank, 0:w * 256].rearrange("p (w n) -> p w n", w=w)).then_inc(pth_ok, 1)

            def o_split(b):
                copy(o_hi[:], ps[:, 6 + b, 0:2 * P]).then_inc(oh_ok, 1)

            def wo_split(kv, p):
                act.wait_ge(landed[p // 2], 16 * kv + 48)
                copy(wo_hi[:], ring[p // 2][:, (p % 2) * 2 * DM:(p % 2 + 1) * 2 * DM]
                     .rearrange("p (h n) -> p h n", h=2)).then_inc(woh_ok, 1)

            def attn_step(kv, p, first, last):
                n = kv * PAIRS + p
                b = p % 2
                turn = p == PAIRS - 1
                for u in range(UNITS):
                    tgt = u + 2
                    if tgt < UNITS or not (last and turn):
                        act.wait_ge(pv_ps, 9 * n + u + 1)
                        pt_split(9 * n + tgt, tgt % UNITS, 4 + (9 * p + tgt) % 2)
                    if u == 0 and not first:
                        o_split(1 - b)
                    if u == (0 if last and turn else W_UNIT) and not first:
                        wo_split(kv - (p == 0), (p - 1) % PAIRS)
                    if last and turn and u == LAST_OUT[1] + 2:
                        act.wait_ge(wo_ps, 2 * n)
                        wo_split(kv, p)
                    if not (last and turn):
                        for h, i in EXP_AT[u]:
                            soft_exp(n + 1, 1 - b, h, i)
                    if u == Q_UNIT + 1 and not first and not (last and p >= 2):
                        q_split(n + 2, b, 6 + (1 - b))
                    if not last:
                        for i in K_AT.get(p, {}).get(u, ()):
                            k_split(kv + 1, i)
                        if turn and u in V_AT:
                            v_split(kv + 1, V_AT[u])
                if turn and not last:
                    act.wait_ge(pv_ps, 9 * n + 10)
                    v_split(kv + 1, 2)

            act.wait_ge(k_ev, 17)
            act.wait_ge(kv_ps, 34)
            q_split(0, 0, 7)
            k_split(0, NCHUNK - 1)
            act.wait_ge(v_ev, 17)
            v_split(0, 0)
            for i in range(NPC):
                soft_exp(0, 0, 0, i)
            soft_exp(0, 0, 1, 0)
            q_split(1, 1, 6)
            for i in range(1, NPC):
                soft_exp(0, 0, 1, i)
            pt_split(0, 0, 4)
            pt_split(1, 1, 5)
            q_split(2, 0, 7)
            v_split(0, 1)
            v_split(0, 2)
            attn_step(0, 0, True, False)
            with act.Fori(0, KVH - 1) as kv:
                for p in range(1, PAIRS):
                    attn_step(kv, p, False, False)
                attn_step(kv + 1, 0, False, False)
            for p in range(1, PAIRS):
                attn_step(KVH - 1, p, False, True)
            act.wait_ge(pv_ps, 9 * KVH * PAIRS + 1)
            o_split(1)

            norm_sqrt(1)
            norm_evac(1, 7)
            act.wait_ge(dts, 2)
            nc.scalar.activation(softplus[2][:], softplus[1][:], ACT.Exp, scale=-1.0).then_inc(dts, 1)
            act.wait_ge(const_in, 160)
            nc.scalar.activation(softplus[5][:], alog[:], ACT.Exp).then_inc(a_ok, 1)

            def raw_out(chunk, k, bank, tile):
                act.wait_ge(freed[chunk[0]], chunk[1] + 1)
                if not (isinstance(k, int) and k < 2):
                    act.wait_ge(taps, k - 1)
                    act.wait_ge(silu_ok, k - 1)
                copy(raw[bank][:], ps[:, bank, :].rearrange("p (c t) -> p c t", c=4))
                for i in range(4):
                    ins = nc.scalar.activation(acc[bank][:, i, :], ps[:, bank, i * T:i * T + T], ACT.Identity,
                                               bias=cb[:, bass.ds(tile + i, 1)],
                                               scale=cw[:, bass.ds(tile + i, 1), 3:4].rearrange("p a b -> p (a b)"))
                ins.then_inc(proj_ev, 1)

            def conv_silu(k, slot, dst):
                act.wait_ge(taps, k + 1)
                nc.scalar.activation(dst, acc[slot][:], ACT.Silu).then_inc(silu_ok, 1)

            def gate_out(chunk, bank, dst):
                act.wait_ge(freed[chunk[0]], chunk[1] + 1)
                nc.scalar.activation(dst, ps[:, bank, :].rearrange("p (c t) -> p c t", c=4),
                                     ACT.Silu).then_inc(proj_ev, 1)

            def decay_exp(g, b, half):
                act.wait_ge(seg_ps, 2 * g + half + 1)
                nc.scalar.activation(decay[b][:, 8 * half:8 * half + 8, :],
                                     ps[:, 2:4, :].rearrange("p a (h t) -> p (a h) t", t=T),
                                     ACT.Exp).then_inc(dec_ok, 1)

            def squares(g):
                act.wait_ge(y_ok, g + 1 + (isinstance(g, int) and g == GROUPS - 1))
                act.wait_ge(sq_ok, g + 1)
                nc.scalar.activation(ysq[:], yv[:], ACT.Square).then_inc(ysq_ok, 1)

            for k in range(4):
                raw_out(stream(k), k, k % 2, 64 + 4 * k)
                if k:
                    conv_silu(k - 1, (k - 1) % 2, bc[:, 4 * (k - 1):4 * k, :])
            decay_exp(0, 0, 0)
            raw_out(stream(4), 4, 0, 0)
            conv_silu(3, 1, bc[:, 12:16, :])
            decay_exp(0, 0, 1)
            raw_out(stream(5), 5, 1, 4)
            conv_silu(4, 0, xc[0][:, 0:4, :])
            conv_silu(5, 1, xc[0][:, 4:8, :])
            gate_out(stream(6), 0, sg[0][:, 0:4, :])
            gate_out(stream(7), 1, sg[0][:, 4:8, :])

            def out_split(g, i):
                slot, before = step_chunk(g, 4 + i)
                act.wait_ge(landed[slot], 16 * (before + 1))
                copy(wout_hi[i][:], ring[slot][:]).then_inc(outh_ok, 1)

            def mamba_step(g, b):
                k, o = 2 * g + 6, 1 - b
                decay_exp(g + 1, o, 0)
                out_split(g, 0)
                raw_out(step_chunk(g, 0), k, 0, 8 * g + 8)
                decay_exp(g + 1, o, 1)
                out_split(g, 1)
                act.wait_ge(ug_ok, g + 1)
                copy(ug_hi[:], ug[:]).then_inc(ugh_ok, 1)
                raw_out(step_chunk(g, 1), k + 1, 1, 8 * g + 12)
                squares(g)
                gate_out(step_chunk(g, 2), 0, sg[o][:, 0:4, :])
                conv_silu(k, 0, xc[o][:, 0:4, :])
                conv_silu(k + 1, 1, xc[o][:, 4:8, :])
                gate_out(step_chunk(g, 3), 1, sg[o][:, 4:8, :])

            with act.Fori(0, 3) as turn:
                for b in range(2):
                    mamba_step(turn * 2 + b, b)
            mamba_step(6, 0)

            def ffn_split(m, hi, ok):
                slot, before = stream(FFN0 + m)
                act.wait_ge(landed[slot], 16 * (before + 1))
                copy(hi, ring[slot][:, 0:hi.shape[-1]]).then_inc(ok, 1)

            act.wait_ge(xdt_ok, GROUPS)
            squares(GROUPS - 1)
            ffn_split(0, w1_hi[:, 0, :], w1h_ok)
            act.wait_ge(var_s, 4)
            nc.scalar.activation(rstd[:, 1:2], rstd[:, 0:1], ACT.Sqrt).then_inc(var_s, 1)
            ffn_split(1, w1_hi[:, 1, :], w1h_ok)

            norm_sqrt(2)
            norm_evac(2, 7)
            act.wait_ge(ln, 3 * LN_STEPS)
            copy(nt_hi[:], norm_t[:]).then_inc(nth_ok, 1)
            act.wait_ge(f_pe, 1)
            copy(r1_sb[:], ps[0:16, 6, 0:T]).then_inc(f_act, 1)
            for c in range(2, NC):
                ffn_split(c, w1_hi[:, c, :], w1h_ok)
            for i in range(4):
                w = min(4, NFT - 4 * i)
                ffn_split(NC + i, w2_hi[:, 4 * i:4 * i + w, :].rearrange("p t n -> p (t n)"), w2h_ok)
            for i in range(4):
                w = min(4, NFT - 4 * i)
                act.wait_ge(f_pe, 3 + i)
                copy(hsel_hi[:, 4 * i:4 * i + w, :],
                     ps[:, i, 0:w * T].rearrange("p (c t) -> p c t", t=T)).then_inc(hsh_ok, 1)

        @block.vector
        def _(dve):
            sub = lambda dst, a, hi: nc.vector.tensor_tensor(dst, a, hi, ALU.subtract)

            def norm(k):
                nc.vector.bn_stats(stats[:], res[:]).then_inc(ln, 1)
                dve.wait_ge(ln, LN_STEPS * k + 1)
                nc.vector.bn_aggr(mean_var[:], stats[:]).then_inc(ln, 1)
                dve.wait_ge(ln, LN_STEPS * k + 2)
                nc.vector.tensor_scalar(rstd[:, 0:1], mean_var[:, 1:2], EPS, None, ALU.add).then_inc(ln, 1)
                dve.wait_ge(ln, LN_STEPS * k + 4)
                nc.vector.reciprocal(rstd[:, 2:3], rstd[:, 1:2]).then_inc(ln, 1)
                dve.wait_ge(ln, LN_STEPS * k + 5)
                nc.vector.tensor_scalar(normed[:], res[:], mean_var[:, 0:1], rstd[:, 2:3],
                                        ALU.subtract, ALU.mult).then_inc(ln, 1)

            def split_first(c):
                dve.wait_ge(first_hi, 2 * c + 1)
                sub(wkv_lo[:, 0, c, :], ring[0][:, c * DM:(c + 1) * DM],
                    wkv_hi[:, 0, c, :].bitcast(F32)).then_inc(first_lo, 1)
                dve.wait_ge(first_hi, 2 * c + 2)
                sub(ctx_lo[0][:, c, :], ring[2][:, c * DM:(c + 1) * DM],
                    ctx_hi[0][:, c, :].bitcast(F32)).then_inc(first_lo, 1)

            def split_wv():
                dve.wait_ge(w_hi, 1)
                sub(wkv_lo[:, 1], ring[1][:].rearrange("p (c n) -> p c n", c=NC),
                    wkv_hi[:, 1].bitcast(F32)).then_inc(w_lo, 1)
                dve.wait_ge(w_lo, 1)
                dve.sem_inc(freed[1], 1)

            def k_split(i):
                a, b = chunk_cols(i)
                dve.wait_ge(kh_ok, i + 1)
                sub(k_lo[:, a:b], k_flat[:, a:b], k_hi[:, a:b].bitcast(F32)).then_inc(kl_ok, 1)

            def split_ctx(j):
                s = (2, 3, 0, 1)[j]
                dve.wait_ge(c_hi, j + (j == 3))
                if j >= 2:
                    dve.wait_ge(kv_ps, 8 * (j - 1))
                sub(ctx_lo[j % 2][:], ring[s][:].rearrange("p (c n) -> p c n", c=NC),
                    ctx_hi[j % 2][:].bitcast(F32)).then_inc(c_lo, 1)
                dve.wait_ge(c_lo, j + (j == 3))
                dve.sem_inc(freed[s], 1)

            def k_out(j):
                for kv in range(KVH):
                    dve.wait_ge(kv_ps, 8 * j + 1 + kv)
                    nc.vector.tensor_copy(k_all[:, kv, BANK * j:BANK * j + BANK], ps[:, kv, :]).then_inc(k_ev, 1)

            dve.sem_inc(wo_ev, 2)
            for c in range(NC):
                split_first(c)
            dve.wait_ge(first_lo, 2 * NC)
            dve.sem_inc(freed[0], 1)
            dve.sem_inc(freed[2], 1)
            split_wv()
            split_ctx(1)
            dve.wait_ge(x_in, 16)
            norm(0)
            k_out(0)
            split_ctx(2)
            k_out(1)
            k_split(0)
            k_split(1)
            dve.wait_ge(c_hi, 3)
            sub(lat_lo[:], norm_t[:], lat_hi[:].bitcast(F32)).then_inc(c_lo, 1)
            split_ctx(3)
            k_out(2)
            k_out(3)
            k_split(2)
            k_split(3)
            dve.wait_ge(kv_ps, 33)
            nc.vector.tensor_copy(k_all[:, :, S_CTX:KV_LEN],
                                  ps[:, 0, :].rearrange("p (k t) -> p k t", k=KVH)).then_inc(k_ev, 1)

            def q_split(m, slot, bank):
                dve.wait_ge(qh_ok, m + 1)
                sub(q_lo[slot][:], ps[:, bank, 0:2 * P], q_hi[slot][:].bitcast(F32)).then_inc(ql_ok, 1)

            def scores_out(m, b, c):
                h, i = c // NCHUNK, c % NCHUNK
                lo, hi = chunk_cols(i)
                dve.wait_ge(s_ps, 10 * m + c + 1)
                nc.vector.tensor_scalar(prob[b][:, h, lo:hi], ps[:, c % 4, 0:hi - lo], SCALE, None,
                                        ALU.mult, ALU.max, accum_out=chunk_max[:, b, h, i:i + 1]).then_inc(s_ev, 1)
                if i == NCHUNK - 1:
                    dve.wait_ge(s_ev, 10 * m + c + 1)
                    nc.vector.tensor_reduce(neg_max[:, b, h:h + 1], chunk_max[:, b, h, :], AX_X, ALU.max,
                                            negate=True).then_inc(nm_ok, 1)

            def invert(m, b):
                dve.wait_ge(exp_ok, 2 * NPC * (m + 1))
                nc.vector.tensor_reduce(row_sum[:, b, :], part_sum[:, b, :, :], AX_X, ALU.add).then_inc(sum_ok, 1)
                dve.wait_ge(sum_ok, m + 1)
                nc.vector.reciprocal(row_inv[:, b, :], row_sum[:, b, :]).then_inc(inv_ok, 1)

            def pt_split(unit, u, bank):
                w = 2 if u < 8 else 1
                dve.wait_ge(pth_ok, unit + 1)
                sub(pt_lo[u % 3][:, 0:w, :], ps[:, bank, 0:w * 256].rearrange("p (w n) -> p w n", w=w),
                    pt_hi[u % 3][:, 0:w, :].bitcast(F32)).then_inc(ptl_ok, 1)

            def o_split(m, b):
                dve.wait_ge(oh_ok, m + 1)
                sub(o_lo[:], ps[:, 6 + b, 0:2 * P], o_hi[:].bitcast(F32)).then_inc(ol_ok, 1)

            def add_heads(m, b, h):
                dve.wait_ge(inv_ok, m + 1)
                dve.wait_ge(wo_ev, 2 * m + h + 2)
                dve.wait_ge(wo_ps, 2 * m + h + 1)
                nc.vector.scalar_tensor_tensor(res[:], ps[:, 2 + h, :], row_inv[:, b, h:h + 1], res[:],
                                               ALU.mult, ALU.add).then_inc(wo_ev, 1)

            def attn_step(kv, p, first, last):
                n = kv * PAIRS + p
                b = p % 2
                turn = p == PAIRS - 1
                for u in range(UNITS):
                    tgt = u + 2
                    if tgt < UNITS or not (last and turn):
                        pt_split(9 * n + tgt, tgt % UNITS, 4 + (9 * p + tgt) % 2)
                    if u == 0 and not first:
                        o_split(n - 1, 1 - b)
                    add_at = tuple(unit + 1 for unit in (LAST_OUT if last and turn else OUT_UNITS))
                    if u in add_at and not first:
                        add_heads(n - 1, 1 - b, u - add_at[0])
                    if u == Q_UNIT + 1 and not first and not (last and p >= 2):
                        q_split(n + 2, b, 6 + (1 - b))
                    if u < 5 and not (last and turn):
                        scores_out(n + 1, 1 - b, 2 * u)
                        scores_out(n + 1, 1 - b, 2 * u + 1)
                if not (last and turn):
                    invert(n + 1, 1 - b)

            q_split(0, 0, 7)
            scores_out(0, 0, 0)
            k_split(NCHUNK - 1)
            for c in range(1, 10):
                scores_out(0, 0, c)
            q_split(1, 1, 6)
            pt_split(0, 0, 4)
            pt_split(1, 1, 5)
            q_split(2, 0, 7)
            invert(0, 0)
            attn_step(0, 0, True, False)
            with dve.Fori(0, KVH - 1) as kv:
                for p in range(1, PAIRS):
                    attn_step(kv, p, False, False)
                attn_step(kv + 1, 0, False, False)
            for p in range(1, PAIRS):
                attn_step(KVH - 1, p, False, True)
            o_split(KVH * PAIRS - 1, 1)
            add_heads(KVH * PAIRS - 1, 1, 0)
            add_heads(KVH * PAIRS - 1, 1, 1)

            dve.wait_ge(wo_ev, 2 * KVH * PAIRS + 2)
            norm(1)
            dve.wait_ge(pool_const, 6)
            nc.vector.tensor_copy(upper_r[:], upper[:]).then_inc(pool_const, 1)
            nc.vector.memset(o_acc[:], 0.0).then_inc(oacc_ok, 1)

            dve.wait_ge(dt_ps, 1)
            dve.wait_ge(const_in, 160)
            z, zabs, exp_z, ratio, s2, exp_a = softplus
            nc.vector.tensor_tensor(z[:], ps[:, 6, 0:NH], dtb[:], ALU.add).then_inc(dts, 1)
            dve.wait_ge(dts, 1)
            nc.vector.scalar_tensor_tensor(zabs[:], z[:], -1.0, z[:], ALU.mult, ALU.max).then_inc(dts, 1)
            dve.wait_ge(dts, 3)
            nc.vector.tensor_scalar(zabs[:], exp_z[:], 2.0, None, ALU.add).then_inc(dts, 1)
            dve.wait_ge(dts, 4)
            nc.vector.reciprocal(s2[:], zabs[:]).then_inc(dts, 1)
            dve.wait_ge(dts, 5)
            nc.vector.tensor_tensor(ratio[:], exp_z[:], s2[:], ALU.mult).then_inc(dts, 1)
            dve.wait_ge(dts, 6)
            nc.vector.tensor_tensor(s2[:], ratio[:], ratio[:], ALU.mult).then_inc(dts, 1)
            dve.wait_ge(dts, 7)
            nc.vector.tensor_scalar(zabs[:], s2[:], 1.0 / 17, None, ALU.mult).then_inc(dts, 1)
            k = 8
            for odd in (15, 13, 11, 9, 7, 5, 3):
                dve.wait_ge(dts, k)
                nc.vector.scalar_tensor_tensor(zabs[:], zabs[:], 1.0 / odd, s2[:], ALU.add,
                                               ALU.mult).then_inc(dts, 1)
                k += 1
            dve.wait_ge(dts, k)
            nc.vector.scalar_tensor_tensor(zabs[:], zabs[:], 1.0, ratio[:], ALU.add, ALU.mult).then_inc(dts, 1)
            dve.wait_ge(dts, k + 1)
            nc.vector.tensor_scalar(z[:], z[:], 0.0, None, ALU.max).then_inc(dts, 1)
            dve.wait_ge(dts, k + 2)
            nc.vector.scalar_tensor_tensor(dt[:], zabs[:], 2.0, z[:], ALU.mult, ALU.add).then_inc(dts, 1)
            dve.wait_ge(dts, k + 3)
            dve.wait_ge(a_ok, 1)
            nc.vector.scalar_tensor_tensor(a_f[:], exp_a[:], -1.0, dt[:], ALU.mult, ALU.mult).then_inc(dts, 1)
            dve.wait_ge(dts, k + 4)
            nc.vector.tensor_copy(a_hi[:], a_f[:]).then_inc(dts, 1)
            dve.wait_ge(dts, k + 5)
            sub(a_lo[:], a_f[:], a_hi[:].bitcast(F32)).then_inc(a_ok, 1)

            def conv(k, slot, tile):
                r, a = raw[slot], acc[slot]
                for back in range(1, 4):
                    for i in range(4):
                        if back > 1:
                            dve.wait_ge(conv_ok, 12 * k + 4 * (back - 2) + i + 1)
                        ins = nc.vector.scalar_tensor_tensor(
                            a[:, i, back:], r[:, i, 0:T - back],
                            cw[:, bass.ds(tile + i, 1), 3 - back:4 - back].rearrange("p a b -> p (a b)"),
                            a[:, i, back:], ALU.mult, ALU.add)
                        ins.then_inc(conv_ok, 1)
                dve.wait_ge(conv_ok, 12 * k + 12)
                dve.sem_inc(taps, 1)

            def taps_of(q, k, slot, tile):
                dve.wait_ge(proj_ev, q + 1)
                conv(k, slot, tile)

            def mask_decay(g, b, half):
                dve.wait_ge(dec_ok, 2 * g + half + 1)
                d = decay[b][:, 8 * half:8 * half + 8, :]
                nc.vector.tensor_tensor(d, d, gm[:, bass.ds(g, 1), :].to_broadcast([P, 8, T]),
                                        ALU.mult).then_inc(m_ok, 1)

            def x_times_dt(g):
                dve.wait_ge(xt_ps, g + 1)
                nc.vector.tensor_tensor(xdt[:], ps[:, 4:6, :].rearrange("p a (h c) -> p (a h) c", c=64),
                                        dt[:, bass.ds(g * HPG, HPG)].unsqueeze(2).to_broadcast([P, HPG, 64]),
                                        ALU.mult).then_inc(xdt_ok, 1)

            def skip_add(g, b, halves=1):
                dve.wait_ge(y_ps, g + 1)
                for half in range(halves):
                    tiles = range(half * TPG // halves, (half + 1) * TPG // halves)
                    for t in tiles:
                        ins = nc.vector.scalar_tensor_tensor(
                            yv[:, t, :], xc[b][:, t, :], dskip[:, bass.ds(g * TPG + t, 1)],
                            ps[:, 4 + t // 4, (t % 4) * T:(t % 4 + 1) * T], ALU.mult, ALU.add)
                    ins.then_inc(y_ok, 1)
                    dve.wait_ge(proj_ev, 4 * g + 8 - (halves == 2 and half == 0))
                    dve.wait_ge(y_ok, g + 1 + half)
                    for t in tiles:
                        ins = nc.vector.scalar_tensor_tensor(
                            ug[:, t, :], yv[:, t, :], nw[:, bass.ds(g * TPG + t, 1)], sg[b][:, t, :],
                            ALU.mult, ALU.mult)
                    ins.then_inc(ug_ok, 1)

            def add_out(g, chunk):
                dve.wait_ge(freed[chunk[0]], chunk[1] + 1)
                dve.wait_ge(oacc_ok, g + 1)
                nc.vector.tensor_tensor(o_acc[:], o_acc[:], ps[:, 6, :], ALU.add).then_inc(oacc_ok, 1)

            for k in range(4):
                taps_of(k, k, k % 2, 64 + 4 * k)
            taps_of(4, 4, 0, 0)
            taps_of(5, 5, 1, 4)
            dve.wait_ge(gm_ps, 1)
            nc.vector.tensor_tensor(gm[:], ps[:, 4:6, :].rearrange("p a (g t) -> p (a g) t", t=T),
                                    causal[:].unsqueeze(1).to_broadcast([P, GROUPS, T]),
                                    ALU.mult).then_inc(gm_ok, 1)
            dve.wait_ge(gm_ok, 1)
            mask_decay(0, 0, 0)
            mask_decay(0, 0, 1)

            def mamba_step(g, b):
                q, k, o = 4 * g + 8, 2 * g + 6, 1 - b
                x_times_dt(g)
                mask_decay(g + 1, o, 0)
                skip_add(g, b)
                mask_decay(g + 1, o, 1)
                dve.wait_ge(ugh_ok, g + 1)
                sub(ug_lo[:], ug[:], ug_hi[:].bitcast(F32)).then_inc(ugl_ok, 1)
                taps_of(q, k, 0, 8 * g + 8)
                taps_of(q + 1, k + 1, 1, 8 * g + 12)
                add_out(g, step_chunk(g, 5))

            with dve.Fori(0, 3) as turn:
                for b in range(2):
                    mamba_step(turn * 2 + b, b)
            mamba_step(6, 0)
            x_times_dt(7)
            dve.wait_ge(sq_ok, GROUPS)
            nc.vector.tensor_reduce(sq_tok[:, 0, :], sq_sum[:].rearrange("p c t -> p t c"), AX_X,
                                    ALU.add).then_inc(var_s, 1)
            skip_add(7, 1, halves=2)
            dve.wait_ge(ysq_ok, GROUPS)
            nc.vector.tensor_reduce(sq_tok[:, 1, :], ysq[:].rearrange("p c t -> p t c"), AX_X,
                                    ALU.add).then_inc(var_s, 1)
            dve.wait_ge(var_s, 3)
            nc.vector.tensor_scalar(rstd[:, 0:1], ps[:, 7, 0:1], 1.0 / INTER, EPS, ALU.mult,
                                    ALU.add).then_inc(var_s, 1)
            dve.wait_ge(var_s, 5)
            nc.vector.reciprocal(rstd[:, 2:3], rstd[:, 1:2]).then_inc(var_s, 1)
            dve.wait_ge(var_s, 6)
            dve.wait_ge(oacc_ok, GROUPS)
            nc.vector.scalar_tensor_tensor(res[:], o_acc[:], rstd[:, 2:3], res[:], ALU.mult,
                                           ALU.add).then_inc(res_ok, 1)
            dve.wait_ge(res_ok, 1)
            slot, before = step_chunk(GROUPS - 1, 1)
            dve.wait_ge(freed[slot], before + 1)
            nc.vector.scalar_tensor_tensor(res[:], ps[:, 6, :], rstd[:, 2:3], res[:], ALU.mult,
                                           ALU.add).then_inc(res_ok, 1)
            dve.wait_ge(res_ok, 2)

            norm(2)
            nc.vector.tensor_copy(rank[:], rank_i[:]).then_inc(pool_const, 1)
            dve.wait_ge(nth_ok, 1)
            sub(nt_lo[:], norm_t[:], nt_hi[:].bitcast(F32)).then_inc(ntl_ok, 1)
            inter = ps[:, 0:4, :].rearrange("p a n -> p (a n)")[:, 0:FF]
            blocks = inter.rearrange("p (n j) -> p n j", j=BLK)
            dve.wait_ge(f_pe, 2)
            nc.vector.tensor_reduce(bmax[:], blocks, AX_X, ALU.max).then_inc(f_mask, 1)
            dve.wait_ge(f_mask, 1)
            nc.vector.tensor_tensor(key, blocks, bmax[:].unsqueeze(2).to_broadcast([P, NBLK, BLK]),
                                    ALU.is_equal).then_inc(f_mask, 1)
            dve.wait_ge(f_mask, 2)
            dve.wait_ge(pool_const, 8)
            nc.vector.tensor_tensor(key, key, rank[:].unsqueeze(1).to_broadcast([P, NBLK, BLK]),
                                    ALU.mult).then_inc(f_mask, 1)
            dve.wait_ge(f_mask, 3)
            nc.vector.tensor_reduce(kmax[:], key, AX_X, ALU.max).then_inc(f_mask, 1)
            dve.wait_ge(f_mask, 4)
            nc.vector.tensor_tensor(key, key, kmax[:].unsqueeze(2).to_broadcast([P, NBLK, BLK]),
                                    ALU.is_equal).then_inc(f_mask, 1)
            dve.wait_ge(f_mask, 5)
            dve.wait_ge(freed[stream(FFN0 + 3)[0]], stream(FFN0 + 3)[1] + 1)
            for i in range(4):
                lo, hi = i * BANK, min(i * BANK + BANK, FF)
                nc.vector.scalar_tensor_tensor(hsel[:, lo:hi], ps[:, 4 + i, 0:hi - lo], 0.0, key_flat[:, lo:hi],
                                               ALU.max, ALU.mult).then_inc(f_dve, 1)
            for i in range(4):
                w = min(4, NFT - 4 * i)
                dve.wait_ge(hsh_ok, i + 1)
                sub(hsel_lo[:, 4 * i:4 * i + w, :], ps[:, i, 0:w * T].rearrange("p (c t) -> p c t", t=T),
                    hsel_hi[:, 4 * i:4 * i + w, :].bitcast(F32)).then_inc(hsl_ok, 1)
            dve.wait_ge(f_pe, 7)
            nc.vector.tensor_tensor(final[:], res[:], ps[:, 4, :], ALU.add).then_inc(f_dve, 2)

        @block.tensor
        def _(pe):
            mm = nc.tensor.matmul

            def norm_transpose(k, bank):
                pe.wait_ge(ln, LN_STEPS * k + 6)
                for c in range(NC):
                    ins = nc.tensor.transpose(ps[:, bank, c * P:c * P + P], normed[:, c * P:c * P + P], ident[:])
                ins.then_inc(ln, 1)

            def split_product(dst, a_hi_, a_lo_, b_hi_, b_lo_, first, last):
                mm(dst, a_hi_, b_hi_, start=first, stop=False)
                mm(dst, a_lo_, b_hi_, start=False, stop=False)
                return mm(dst, a_hi_, b_lo_, start=False, stop=last)

            def project(j):
                ch, cl = ctx_hi[j % 2], ctx_lo[j % 2]
                if j == 0:
                    for c in range(NC):
                        pe.wait_ge(first_lo, 2 * c + 2)
                        for kv in range(KVH):
                            ins = split_product(ps[:, kv, :], wkv_hi[:, 0, c, kv * P:kv * P + P],
                                                wkv_lo[:, 0, c, kv * P:kv * P + P], ch[:, c, :], cl[:, c, :],
                                                c == 0, c == NC - 1)
                            if c == NC - 1:
                                ins.then_inc(kv_ps, 1)
                else:
                    pe.wait_ge(c_lo, j + (j == 3))
                    for kv in range(KVH):
                        pe.wait_ge(k_ev, 4 * (j - 1) + kv + 1)
                        if j == 2 and kv == 2:
                            pe.wait_ge(ln, LN_STEPS)
                        for c in range(NC):
                            ins = split_product(ps[:, kv, :], wkv_hi[:, 0, c, kv * P:kv * P + P],
                                                wkv_lo[:, 0, c, kv * P:kv * P + P], ch[:, c, :], cl[:, c, :],
                                                c == 0, c == NC - 1)
                        ins.then_inc(kv_ps, 1)
                pe.wait_ge(w_lo, 1)
                for t in range(4):
                    if j:
                        pe.wait_ge(v_ev, 4 * (j - 1) + t + 1)
                    for c in range(NC):
                        ins = split_product(ps[:, 4 + t, :], ch[:, c, t * P:t * P + P], cl[:, c, t * P:t * P + P],
                                            wkv_hi[:, 1, c, :], wkv_lo[:, 1, c, :], c == 0, c == NC - 1)
                    ins.then_inc(kv_ps, 1)

            project(0)
            project(1)
            pe.wait_ge(ident_ok, 2)
            pe.wait_ge(k_ev, 7)
            norm_transpose(0, 2)
            project(2)
            project(3)
            pe.wait_ge(c_lo, 3)
            pe.wait_ge(k_ev, 13)
            for kv in range(KVH):
                for c in range(NC):
                    ins = split_product(ps[:, 0, kv * P:kv * P + P], wkv_hi[:, 0, c, kv * P:kv * P + P],
                                        wkv_lo[:, 0, c, kv * P:kv * P + P], lat_hi[:, c, :], lat_lo[:, c, :],
                                        c == 0, c == NC - 1)
            ins.then_inc(kv_ps, 1)
            pe.wait_ge(k_ev, 14)
            for c in range(NC):
                ins = split_product(ps[:, 1, :], lat_hi[:, c, :], lat_lo[:, c, :], wkv_hi[:, 1, c, :],
                                    wkv_lo[:, 1, c, :], c == 0, c == NC - 1)
            ins.then_inc(kv_ps, 1)

            def queries(m, kv, p, bank):
                s = 2 + p // 2
                if p % 2 == 0:
                    pe.wait_ge(landed[s], kv * 16 + 32)
                w = ring[s][:].rearrange("p (c n) -> p c n", c=NC)
                for h in range(2):
                    col = ((p % 2) * 2 + h) * P
                    for c in range(NC):
                        ins = mm(ps[:, bank, h * P:h * P + P], w[:, c, col:col + P], norm_t[:, c, :],
                                 start=(c == 0), stop=(c == NC - 1))
                ins.then_inc(q_ps, 1)

            def queries_done(m, p):
                pe.wait_ge(q_ps, m + 1)
                pe.sem_inc(freed[2 + p // 2], 1)

            def scores(m, qslot, c):
                h, i = c // NCHUNK, c % NCHUNK
                lo, hi = chunk_cols(i)
                early = isinstance(m, int) and m < 2
                if c >= 4:
                    pe.wait_ge(s_ev, 10 * m + c - 3)
                elif c < 2 and not (early and m == 0):
                    pe.wait_ge(s_ev, 10 * m - 1 + c)
                elif c >= 2 and not early:
                    pe.wait_ge(wo_ev, 2 * m - 5 + c)
                split_product(ps[:, c % 4, 0:hi - lo], q_hi[qslot][:, h * P:h * P + P],
                              q_lo[qslot][:, h * P:h * P + P], k_hi[:, lo:hi], k_lo[:, lo:hi],
                              True, True).then_inc(s_ps, 1)

            def output(m, h):
                if h == 0:
                    pe.wait_ge(ol_ok, m + 1)
                    pe.wait_ge(wol_ok, m + 1)
                if not (isinstance(m, int) and m >= KVH * PAIRS - 2):
                    pe.wait_ge(s_ev, 10 * (m + 2) + 7 + h)
                else:
                    pe.wait_ge(wo_ev, 2 * m + h + 1)
                split_product(ps[:, 2 + h, :], o_hi[:, h * P:h * P + P], o_lo[:, h * P:h * P + P],
                              wo_hi[:, h, :], wo_lo[:, h, :], True, True).then_inc(wo_ps, 1)

            def transposes(pair, unit, b, u, bank):
                if u in (2, 4, 6):
                    pe.wait_ge(exp_ok, 2 * NPC * pair + NPC + u // 2 + 1)
                for w in range(2 if u < 8 else 1):
                    for h in range(2):
                        kt = 2 * u + w
                        at = w * 256 + h * P
                        ins = nc.tensor.transpose(ps[:, bank, at:at + P], prob[b][:, h, kt * P:kt * P + P], ident[:])
                ins.then_inc(t_ps, 1)

            def values(unit, b, u, fresh):
                pe.wait_ge(ptl_ok, unit + 1)
                if fresh is not None and u % 3 == 0:
                    pe.wait_ge(vl_ok, 3 * fresh + u // 3 + 1)
                for w in range(2 if u < 8 else 1):
                    kt = 2 * u + w
                    ins = split_product(ps[:, 6 + b, 0:256], v_hi[:, kt, :], v_lo[:, kt, :],
                                        pt_hi[u % 3][:, w, :], pt_lo[u % 3][:, w, :], kt == 0, kt == NKT - 1)
                ins.then_inc(pv_ps, 1)

            def attn_step(kv, p, first, last):
                n = kv * PAIRS + p
                b = p % 2
                turn = p == PAIRS - 1
                for u in range(UNITS):
                    tgt = u + 2
                    if tgt < UNITS:
                        pe.wait_ge(ptl_ok, 9 * n + u + 1)
                        transposes(n, 9 * n + tgt, b, tgt, 4 + (9 * p + tgt) % 2)
                    elif not (last and turn):
                        pe.wait_ge(ptl_ok, 9 * n + u + 1)
                        if u == 7:
                            pe.wait_ge(exp_ok, 2 * NPC * (n + 1) + NPC + 1)
                        transposes(n + 1, 9 * (n + 1) + tgt - UNITS, 1 - b, tgt - UNITS, 4 + (9 * p + tgt) % 2)
                    if u == 0:
                        if last and turn:
                            pe.wait_ge(ol_ok, n - 1)
                        else:
                            pe.wait_ge(ql_ok, n + 2)
                    values(9 * n + u, b, u, kv if p == 0 else None)
                    if u < 5 and not (last and turn):
                        for c in (2 * u, 2 * u + 1):
                            if turn and c < NCHUNK:
                                pe.wait_ge(kl_ok, NCHUNK * (kv + 1) + c + 1)
                            scores(n + 1, 1 - b, c)
                    if not (last and p >= 2):
                        if u == Q_UNIT and not first:
                            pe.wait_ge(ol_ok, n)
                            queries(n + 2, kv + (p >= 2), (p + 2) % 4, 6 + (1 - b))
                        if u == Q_UNIT + 2 and p % 2 == 1:
                            queries_done(n + 2, (p + 2) % 4)
                    out_at = LAST_OUT if last and turn else OUT_UNITS
                    if u in out_at and not first:
                        output(n - 1, u - out_at[0])

            pe.wait_ge(v_ev, 16)
            pe.wait_ge(ln, LN_STEPS)
            pe.sem_inc(pv_ps, 1)
            queries(0, 0, 0, 7)
            pe.wait_ge(k_ev, 17)
            pe.wait_ge(v_ev, 17)
            pe.wait_ge(ql_ok, 1)
            for c in range(10):
                if c < NCHUNK:
                    pe.wait_ge(kl_ok, c + 1)
                scores(0, 0, c)
            queries(1, 0, 1, 6)
            pe.wait_ge(ql_ok, 1)
            queries(2, 0, 2, 7)
            queries_done(1, 1)
            pe.wait_ge(exp_ok, NPC + 1)
            transposes(0, 0, 0, 0, 4)
            transposes(0, 1, 0, 1, 5)
            attn_step(0, 0, True, False)
            with pe.Fori(0, KVH - 1) as kv:
                for p in range(1, PAIRS):
                    attn_step(kv, p, False, False)
                attn_step(kv + 1, 0, False, False)
            for p in range(1, PAIRS):
                attn_step(KVH - 1, p, False, True)
            output(KVH * PAIRS - 1, 0)
            output(KVH * PAIRS - 1, 1)

            norm_transpose(1, 7)

            pe.wait_ge(ln, 2 * LN_STEPS)
            pe.wait_ge(const_in, 160)
            for c in range(NC):
                ins = mm(ps[:, 6, 0:NH], norm_t[:, c, :], w_dt_sb[:, c, :], start=(c == 0), stop=(c == NC - 1))
            ins.then_inc(dt_ps, 1)

            def in_proj(slot, loads, q, bank):
                pe.wait_ge(landed[slot], loads * 16)
                if not (isinstance(q, int) and q < 2):
                    pe.wait_ge(proj_ev, q - 1)
                w = ring[slot][:].rearrange("p (t c n) -> p t c n", t=4, c=NC)
                for t in range(4):
                    for c in range(NC):
                        ins = mm(ps[:, bank, t * T:t * T + T], w[:, t, c, :], norm_t[:, c, :],
                                 start=(c == 0), stop=(c == NC - 1))
                ins.then_inc(freed[slot], 1)

            def segments(g, b, half):
                if not (isinstance(g, int) and g == 0 and half == 0):
                    pe.wait_ge(dec_ok, 2 * g + half)
                pe.wait_ge(at_ok, g + 1)
                for i in range(2):
                    h = 8 * half + 4 * i
                    mm(ps[:, 2 + i, :], upper_r[:], at_hi[:, h:h + 4, :].rearrange("p h t -> p (h t)"), start=True, stop=False)
                    ins = mm(ps[:, 2 + i, :], upper_r[:], at_lo[:, h:h + 4, :].rearrange("p h t -> p (h t)"), start=False, stop=True)
                ins.then_inc(seg_ps, 1)

            def x_transposes(g, b):
                pe.wait_ge(silu_ok, 2 * g + 6)
                if not (isinstance(g, int) and g == 0):
                    pe.wait_ge(y_ok, g)
                for t in range(TPG):
                    ins = nc.tensor.transpose(ps[:, 4 + t // 4, (t % 4) * T:(t % 4 + 1) * T], xc[b][:, t, :], ident[:])
                ins.then_inc(xt_ps, 1)

            def y_product(g, b):
                pe.wait_ge(xdt_ok, g + 1)
                pe.wait_ge(m_ok, 2 * g + 2)
                for h in range(HPG):
                    t = h // 2
                    ins = mm(ps[(h % 2) * 64:(h % 2) * 64 + 64, 4 + t // 4, (t % 4) * T:(t % 4 + 1) * T],
                             xdt[:, h, :], decay[b][:, h, :], start=True, stop=True)
                ins.then_inc(y_ps, 1)

            def out_proj(g, chunks):
                pe.wait_ge(oacc_ok, g + 1)
                for i, (slot, loads) in enumerate(chunks):
                    pe.wait_ge(ug_ok, g + 1 + i)
                    pe.wait_ge(landed[slot], loads * 16)
                    w = ring[slot][:].rearrange("p (t n) -> p t n", t=4)
                    for t in range(4):
                        ins = mm(ps[:, 6, :], ug[:, 4 * i + t, :], w[:, t, :], start=(i == 0 and t == 0),
                                 stop=(i == 1 and t == 3))
                    ins.then_inc(freed[slot], 1)
                    if i == 0:
                        pe.wait_ge(pool_const, 6)
                        pe.wait_ge(var_s, 2)
                        mm(ps[:, 7, 0:1], sq_tok[:, 0, :], ones_m[:], start=True, stop=False)
                        mm(ps[:, 7, 0:1], sq_tok[:, 1, :], ones_m[:], start=False, stop=True).then_inc(var_s, 1)

            for m in range(8):
                in_proj(stream(m)[0], stream(m)[1] + 1, m, m % 2)
                if m == 3:
                    pe.wait_ge(pool_const, 7)
                    segments(0, 0, 0)
                if m == 4:
                    segments(0, 0, 1)
                if m == 6:
                    pe.wait_ge(silu_ok, 4)
                    for g in range(GROUPS):
                        ins = mm(ps[:, 4 + g // 4, (g % 4) * T:(g % 4 + 1) * T], bc[:, g, :], bc[:, 8 + g, :],
                                 start=True, stop=True)
                    ins.then_inc(gm_ps, 1)
            pe.wait_ge(gm_ok, 1)

            def out_proj_split(g):
                pe.wait_ge(ugl_ok, g + 1)
                if not (isinstance(g, int) and g == 0):
                    pe.wait_ge(oacc_ok, g + 1)
                for i in range(2):
                    slot, _ = step_chunk(g, 4 + i)
                    pe.wait_ge(outl_ok, 2 * g + i + 1)
                    hi, lo = (w[:].rearrange("p (t n) -> p t n", t=4) for w in (wout_hi[i], ring_lo[slot]))
                    for t in range(4):
                        ins = split_product(ps[:, 6, :], ug_hi[:, 4 * i + t, :], ug_lo[:, 4 * i + t, :],
                                            hi[:, t, :], lo[:, t, :], i == 0 and t == 0, i == 1 and t == 3)
                    ins.then_inc(freed[slot], 1)

            def mamba_step(g, b, last):
                q = 4 * g + 8

                def project(j):
                    slot, before = step_chunk(g, j)
                    in_proj(slot, before + 1, q + j, j % 2)

                x_transposes(g, b)
                if last:
                    y_product(g, b)
                    out_proj(g, [(slot, before + 1) for slot, before in (step_chunk(g, 0), step_chunk(g, 1))])
                    return
                segments(g + 1, 1 - b, 0)
                project(0)
                segments(g + 1, 1 - b, 1)
                y_product(g, b)
                project(1)
                project(2)
                out_proj_split(g)
                project(3)

            with pe.Fori(0, 3) as turn:
                for b in range(2):
                    mamba_step(turn * 2 + b, b, False)
            mamba_step(6, 0, False)
            mamba_step(7, 1, True)

            norm_transpose(2, 7)
            pe.wait_ge(ln, 3 * LN_STEPS)
            for c in range(NC):
                ins = mm(ps[0:16, 6, 0:T], c1_sb[:, c, :], norm_t[:, c, :], start=(c == 0), stop=(c == NC - 1))
            ins.then_inc(f_pe, 1)
            pe.wait_ge(f_act, 1)
            for i in range(4):
                lo, hi = i * BANK, min(i * BANK + BANK, FF)
                ins = mm(ps[:, i, 0:hi - lo], r1_sb[:], c2_sb[:, lo:hi], start=True, stop=True)
            ins.then_inc(f_pe, 1)
            for c in range(NC):
                s, _ = stream(FFN0 + c)
                pe.wait_ge(w1l_ok, c + 1)
                if c == 0:
                    pe.wait_ge(ntl_ok, 1)
                for i in range(4):
                    lo, hi = i * BANK, min(i * BANK + BANK, FF)
                    ins = split_product(ps[:, 4 + i, 0:hi - lo], nt_hi[:, c, :], nt_lo[:, c, :],
                                        w1_hi[:, c, lo:hi], ring_lo[s][:, lo:hi], c == 0, c == NC - 1)
                ins.then_inc(freed[s], 1)
            for i in range(4):
                pe.wait_ge(f_dve, i + 1)
                for t in range(4 * i, min(4 * i + 4, NFT)):
                    ins = nc.tensor.transpose(ps[:, i, (t % 4) * T:(t % 4 + 1) * T], hsel[:, t * T:t * T + T], ident[:])
                ins.then_inc(f_pe, 1)
            for i in range(4):
                s, _ = stream(FFN0 + 4 + i)
                pe.wait_ge(w2l_ok, i + 1)
                pe.wait_ge(hsl_ok, i + 1)
                for t in range(4 * i, min(4 * i + 4, NFT)):
                    ins = split_product(ps[:, 4, :], hsel_hi[:, t, :], hsel_lo[:, t, :], w2_hi[:, t, :],
                                        ring_lo[s][:, (t % 4) * DM:(t % 4 + 1) * DM], t == 0, t == NFT - 1)
            ins.then_inc(f_pe, 1)


_NAMES = ["x", "ctx_t", "wq", "wk", "wv", "wo", "w_in", "w_dt", "w_out", "conv_w", "conv_b", "dt_bias",
          "a_log", "d_skip", "norm_w", "c1", "c2", "w1", "w2", "w2_tail"]


def kernel(**inputs):
    import numpy as np
    import concourse.bacc as bacc
    from concourse.bass_utils import run_bass_kernel_spmd

    a = {k: np.asarray(v) for k, v in inputs.items()}

    def tiles(w, n):
        k, cols = w.shape
        return w.reshape(k // 128, 128, cols // n, n).transpose(2, 1, 0, 3).reshape(cols // n, 128, -1)

    def rows(w, r):
        k, cols = w.shape
        return w.reshape(k // (128 * r), r, 128, cols).transpose(0, 2, 1, 3).reshape(-1, 128, r * cols)

    w_in = a["L0_attn_in_proj_w"]
    w_main = w_in[:18432].reshape(36, 4, 128, 4, 128).transpose(0, 4, 1, 3, 2).reshape(36, 128, 2048)
    w2 = a["L0_ffn_w2t"]
    laid = {
        "x": a["x"][0],
        "ctx_t": tiles(a["ctx_4096"][0].T, 512),
        "wq": tiles(a["L0_xattn_Wq"], 512),
        "wk": tiles(a["L0_xattn_Wk"], 512)[0],
        "wv": tiles(a["L0_xattn_Wv"], 512)[0],
        "wo": rows(a["L0_xattn_Wo"], 4),
        "w_in": w_main,
        "w_dt": tiles(w_in[18432:].T, 128).reshape(128, 4, 128),
        "w_out": rows(a["L0_attn_out_proj_w"].T, 4),
        "conv_w": a["L0_attn_conv_w"].reshape(80, 128, 4).transpose(1, 0, 2),
        "conv_b": a["L0_attn_conv_b"].reshape(80, 128).T,
        "dt_bias": a["L0_attn_dt_bias"],
        "a_log": a["L0_attn_A_log"],
        "d_skip": a["L0_attn_D"].reshape(64, 2).T,
        "norm_w": a["L0_attn_norm_w"].reshape(64, 128).T,
        "c1": tiles(a["L0_ffn_c1_w"].T, 16).reshape(128, 4, 16),
        "c2": a["L0_ffn_c2_w"].T,
        "w1": a["L0_ffn_w1"].T.reshape(4, 128, 1792),
        "w2": rows(w2[:1536], 4),
        "w2_tail": rows(w2[1536:], 2),
    }
    nc = bacc.Bacc("TRN2", target_bir_lowering=False, num_devices=1)
    arrays, args = {}, []
    for name in _NAMES:
        v = np.ascontiguousarray(laid[name])
        arrays[f"{name}_dram"] = v
        args.append(nc.dram_tensor(f"{name}_dram", v.shape, mybir.dt.from_np(v.dtype), kind="ExternalInput").ap())
    out = nc.dram_tensor("out_dram", (T, DM), F32, kind="ExternalOutput").ap()
    build(nc, *args, out)
    r = run_bass_kernel_spmd(nc, [arrays], core_ids=[0])
    return r.results[0]["out_dram"].reshape(1, T, DM)
```
